# Optimizing a Trainium2 kernel written in Bass

```python
import numpy as np
import jax
import jax.numpy as jnp

def _softmax(x, axis=-1):
    return jax.nn.softmax(x, axis=axis)

def _gelu(x):
    return jax.nn.gelu(x, approximate=True)

def _silu(x):
    return jax.nn.silu(x)

def _sigmoid(x):
    return jax.nn.sigmoid(x)

def _layernorm(x, axis=-1, eps=1e-05):
    m = jnp.mean(x, axis=axis, keepdims=True)
    v = jnp.var(x, axis=axis, keepdims=True)
    return (x - m) / jnp.sqrt(v + eps)

def _scatter_add(tgt, idx, src, axis=0):
    return tgt.at[idx].add(src)

def _segment_sum(src, seg, n):
    return jax.ops.segment_sum(src, seg, n)
kernel_name = 'mk_adaln_attn_ffn_d1_seqx_r8_677b2c'

def setup_inputs(seed: int=0):
    np.random.seed(seed)
    _w = jnp.asarray

    def _rec_inputs():
        import jax
        import jax.numpy as jnp
        _rk = jax.random.key(seed)
        x = 0.0001734 + 0.8201 * jax.random.normal(jax.random.fold_in(_rk, 1), (32, 32, 512), jnp.float32)
        _lenS = 32 - jax.random.randint(jax.random.fold_in(_rk, 7), (32,), 0, max(1, 32 // 4) + 1, jnp.int32)
        _lenS2 = 32 - jax.random.randint(jax.random.fold_in(_rk, 8), (32,), 0, max(1, 32 // 4) + 1, jnp.int32)
        itok_B_0_7 = jax.random.randint(jax.random.fold_in(_rk, 11), (32,), 0, 8, jnp.int32)
        itok_B_2182_4065 = jax.random.randint(jax.random.fold_in(_rk, 13), (32,), 2182, 4066, jnp.int32)
        itok_Bx16_0_63 = jax.random.randint(jax.random.fold_in(_rk, 14), (32, 16), 0, 64, jnp.int32)
        itok_B_207_1644 = jax.random.randint(jax.random.fold_in(_rk, 15), (32,), 207, 1645, jnp.int32)
        return (x, itok_B_0_7, itok_B_2182_4065, itok_Bx16_0_63, itok_B_207_1644, _lenS)
    x, itok_B_0_7, itok_B_2182_4065, itok_Bx16_0_63, itok_B_207_1644, _lenS = _rec_inputs()

    def _L0_cond_setup():
        import jax, jax.numpy as jnp
        import numpy as np
        SESSION_CHANNELS = [128, 160, 192, 224, 240, 248, 252, 32]
        N_SESS = len(SESSION_CHANNELS)
        B, MAX_C, MAX_T = (16, 32, 512)
        HID, N_SRC = (64, 32)
        key = jax.random.key(seed)
        ks = jax.random.split(key, 7)
        session_ids = jax.random.randint(ks[0], (B,), 0, N_SESS)
        chan_table = jnp.asarray(SESSION_CHANNELS)
        channel_counts = chan_table[session_ids]
        seq_lens = jax.random.randint(ks[1], (B,), MAX_T // 2, MAX_T + 1)
        x = jax.random.normal(ks[2], (B, MAX_C, MAX_T), jnp.float32)
        cmask = (jnp.arange(MAX_C)[None, :] < channel_counts[:, None]).astype(x.dtype)
        tmask = (jnp.arange(MAX_T)[None, :] < seq_lens[:, None]).astype(x.dtype)
        x = x * cmask[:, :, None] * tmask[:, None, :]
        lim1 = 1.0 / np.sqrt(MAX_C)
        W_sess = jax.random.uniform(ks[3], (N_SESS, MAX_C, HID), jnp.float32, -lim1, lim1)
        b_sess = jax.random.uniform(ks[4], (N_SESS, HID), jnp.float32, -lim1, lim1)
        lim2 = 1.0 / np.sqrt(HID)
        W2 = jax.random.uniform(ks[5], (HID, N_SRC), jnp.float32, -lim2, lim2)
        b2 = jax.random.uniform(ks[6], (N_SRC,), jnp.float32, -lim2, lim2)
        return dict(x=x, session_ids=session_ids, channel_counts=channel_counts, seq_lens=seq_lens, W_sess=W_sess, b_sess=b_sess, W2=W2, b2=b2)
    _L0_cond_all = _L0_cond_setup()
    _L0_cond_in = {k: v for k, v in _L0_cond_all.items() if k in ('W_sess', 'b_sess', 'W2', 'b2')}
    del _L0_cond_all

    def _L0_attn_setup():
        import jax, jax.numpy as jnp
        import numpy as np
        HID = 512
        DM = 128
        DIN = 2 * DM
        DST = 16
        HD = 64
        NH = DIN // HD
        DCONV = 7
        CONV_DIM = DIN + 2 * DST
        DIN_PROJ = 2 * DIN + 2 * DST + 2 * NH
        SEQ, BATCH = (256, 4)

        def _causal_conv(x, w, b):
            y = jax.lax.conv_general_dilated(jnp.transpose(x, (0, 2, 1)), w, (1,), [(DCONV - 1, 0)], feature_group_count=CONV_DIM, dimension_numbers=('NCH', 'OIH', 'NCH'))
            return jnp.transpose(y, (0, 2, 1)) + b

        def _ssm_scan(x, dt, A, B, C):
            dA = jnp.exp(dt * A)
            dBx = dt[..., None] * x

            def step(h, t):
                dA_t, dBx_t, B_t, C_t = t
                h = dA_t[:, :, None, None] * h + dBx_t[..., None] * B_t[:, None, None, :]
                y = jnp.einsum('bhpn,bn->bhp', h, C_t)
                return (h, y)
            h0 = jnp.zeros((x.shape[0], NH, HD, DST), x.dtype)
            _, ys = jax.lax.scan(step, h0, (jnp.moveaxis(dA, 1, 0), jnp.moveaxis(dBx, 1, 0), jnp.moveaxis(B, 1, 0), jnp.moveaxis(C, 1, 0)))
            return jnp.moveaxis(ys, 0, 1)

        def _hydra(u, in_w, conv_w, conv_b, dt_bias, A_log, D, fcD_w, norm_w, out_w):
            b, l, _ = u.shape
            zxbcdt = u @ in_w.T
            z = zxbcdt[..., :DIN]
            xBC = zxbcdt[..., DIN:DIN + CONV_DIM]
            dt2 = zxbcdt[..., DIN + CONV_DIM:]
            dt_fw = jax.nn.softplus(dt2[..., :NH] + dt_bias)
            dt_bw = jax.nn.softplus(jnp.flip(dt2[..., NH:], 1) + dt_bias)
            xBC = jax.nn.silu(_causal_conv(xBC, conv_w, conv_b))
            xs = xBC[..., :DIN]
            Bm = xBC[..., DIN:DIN + DST]
            Cm = xBC[..., DIN + DST:]
            A = -jnp.exp(A_log)
            x4 = xs.reshape(b, l, NH, HD)
            y_fw = _ssm_scan(x4, dt_fw, A, Bm, Cm).reshape(b, l, DIN)
            y_bw = jnp.flip(_ssm_scan(jnp.flip(x4, 1), dt_bw, A, jnp.flip(Bm, 1), jnp.flip(Cm, 1)).reshape(b, l, DIN), 1)
            zero = jnp.zeros((b, 1, DIN), u.dtype)
            y = jnp.concatenate([zero, y_fw[:, :-1]], 1) + jnp.concatenate([y_bw[:, 1:], zero], 1)
            y = y + xs * jnp.repeat(xs @ fcD_w.T + D, HD, axis=-1)
            yz = y * jax.nn.silu(z)
            y = yz * jax.lax.rsqrt(jnp.mean(jnp.square(yz), -1, keepdims=True) + 1e-05) * norm_w
            return y @ out_w.T
        key = jax.random.key(seed)
        ks = jax.random.split(key, 12)
        rn = lambda k, shape, s=0.02: jax.random.normal(k, shape, jnp.float32) * s
        dt = jnp.exp(jax.random.uniform(ks[5], (NH,), jnp.float32, np.log(0.001), np.log(0.1)))
        return dict(x=jax.random.normal(ks[0], (SEQ, BATCH, HID), jnp.float32), w_down=rn(ks[1], (DM, HID)), b_down=jnp.zeros((DM,), jnp.float32), w_up=rn(ks[2], (HID, DM)), b_up=jnp.zeros((HID,), jnp.float32), gate1=jnp.asarray(0.6, jnp.float32), hy_in_w=rn(ks[3], (DIN_PROJ, DM)), hy_conv_w=rn(ks[4], (CONV_DIM, 1, DCONV), 0.2), hy_conv_b=jnp.zeros((CONV_DIM,), jnp.float32), hy_dt_bias=jnp.log(jnp.expm1(dt)), hy_A_log=jnp.log(jax.random.uniform(ks[6], (NH,), jnp.float32, 1.0, 16.0)), hy_D=jnp.ones((NH,), jnp.float32), hy_fcD_w=rn(ks[7], (NH, DIN)), hy_norm_w=jnp.ones((DIN,), jnp.float32), hy_out_w=rn(ks[8], (DM, DIN)))
    _L0_attn_all = _L0_attn_setup()
    _L0_attn_in = {k: v for k, v in _L0_attn_all.items() if k in ('w_down', 'b_down', 'w_up', 'b_up', 'gate1', 'hy_in_w', 'hy_conv_w', 'hy_conv_b', 'hy_dt_bias', 'hy_A_log', 'hy_D', 'hy_fcD_w', 'hy_norm_w', 'hy_out_w')}
    del _L0_attn_all

    def _L0_cond2_setup():
        import jax, jax.numpy as jnp
        import numpy as np
        B, S, HID = (4, 128, 512)
        D, HQ, HK = (128, 32, 8)
        PAGES, PSIZE, NPP = (64, 32, 16)
        THETA = 10000.0
        EPS = 1e-06
        SCALE = 1.0 / float(np.sqrt(D))

        def _rmsnorm(t, w):
            var = jnp.mean(t * t, axis=-1, keepdims=True)
            return t * jax.lax.rsqrt(var + EPS) * w

        def _rope(t, pos):
            inv_freq = 1.0 / THETA ** (jnp.arange(0, D, 2, dtype=jnp.float32) / D)
            freqs = pos[..., None].astype(jnp.float32) * inv_freq
            cos = jnp.cos(freqs)[:, :, None, :]
            sin = jnp.sin(freqs)[:, :, None, :]
            t1, t2 = (t[..., :D // 2], t[..., D // 2:])
            return jnp.concatenate([t1 * cos - t2 * sin, t2 * cos + t1 * sin], axis=-1)
        key = jax.random.key(seed)
        ks = jax.random.split(key, 10)
        x = jax.random.normal(ks[0], (B, S, HID), jnp.float32)
        Wq = jax.random.normal(ks[1], (HQ * D, HID), jnp.float32) * 0.02
        Wk = jax.random.normal(ks[2], (HK * D, HID), jnp.float32) * 0.02
        Wv = jax.random.normal(ks[3], (HK * D, HID), jnp.float32) * 0.02
        Wo = jax.random.normal(ks[4], (HID, HQ * D), jnp.float32) * 0.02
        q_norm_w = jax.random.uniform(ks[5], (D,), jnp.float32)
        k_norm_w = jax.random.uniform(ks[6], (D,), jnp.float32)
        k_cache = jax.random.normal(ks[7], (PAGES, PSIZE, HK, D), jnp.float32)
        v_cache = jax.random.normal(ks[8], (PAGES, PSIZE, HK, D), jnp.float32)
        block_table = jnp.arange(B * NPP, dtype=jnp.int32).reshape(B, NPP)
        cache_seqlens = jax.random.randint(ks[9], (B,), 0, 475).astype(jnp.int32)
        return dict(x=x, Wq=Wq, Wk=Wk, Wv=Wv, Wo=Wo, q_norm_w=q_norm_w, k_norm_w=k_norm_w, k_cache=k_cache, v_cache=v_cache, block_table=block_table, cache_seqlens=cache_seqlens)
    _L0_cond2_all = _L0_cond2_setup()
    _L0_cond2_in = {k: v for k, v in _L0_cond2_all.items() if k in ('Wq', 'Wk', 'Wv', 'Wo', 'q_norm_w', 'k_norm_w', 'k_cache', 'v_cache')}
    del _L0_cond2_all

    def _L0_ffn_setup():
        import jax, jax.numpy as jnp
        import numpy as np
        HID, BOT, RDIM, NSLOT, K, VB = (512, 64, 48, 128, 8, 32)
        TAU_LOW, TAU_HIGH, EARLY_EXIT = (0.5, 2.0, 0.05)

        def _uncertainty(h, Wu1, bu1, Wu2, bu2):
            var = jnp.var(h, axis=-1)
            log_var = jnp.log1p(var)
            norm_var = log_var / (jnp.mean(log_var) + 1e-06)
            learned = (jax.nn.gelu(h @ Wu1.T + bu1) @ Wu2.T + bu2)[..., 0]
            return jnp.clip(norm_var * 0.5 + jax.nn.sigmoid(learned) * 2.5, 0.0, 5.0)
        key = jax.random.key(seed)
        ks = jax.random.split(key, 12)
        B, S = (2, 256)
        return {'hidden_states': jax.random.normal(ks[0], (B, S, HID), dtype=jnp.float32), 'Wq': jax.random.normal(ks[1], (BOT, HID), dtype=jnp.float32) / np.sqrt(HID), 'Wr': jax.random.normal(ks[2], (RDIM, BOT), dtype=jnp.float32) / np.sqrt(BOT), 'aux_keys': jax.random.normal(ks[3], (NSLOT, BOT), dtype=jnp.float32) * 0.01, 'aux_values': jax.random.normal(ks[4], (NSLOT, HID), dtype=jnp.float32) * 0.02, 'Wvd': jax.random.normal(ks[5], (VB, HID), dtype=jnp.float32) * 0.1 / np.sqrt(HID), 'Wvu': jax.random.normal(ks[6], (HID, VB), dtype=jnp.float32) * 0.1 / np.sqrt(VB), 'Wu1': jax.random.normal(ks[7], (HID // 4, HID), dtype=jnp.float32) / np.sqrt(HID), 'bu1': jnp.zeros((HID // 4,), dtype=jnp.float32), 'Wu2': jax.random.normal(ks[8], (1, HID // 4), dtype=jnp.float32) * 0.01, 'bu2': jnp.zeros((1,), dtype=jnp.float32), 'gate_w1': jnp.float32(0.5), 'gate_bias': jnp.float32(-1.0), 'log_rel': jnp.zeros((NSLOT,), dtype=jnp.float32)}
    _L0_ffn_all = _L0_ffn_setup()
    _L0_ffn_in = {k: v for k, v in _L0_ffn_all.items() if k in ('Wq', 'Wr', 'aux_keys', 'aux_values', 'Wvd', 'Wvu', 'Wu1', 'bu1', 'Wu2', 'bu2', 'gate_w1', 'gate_bias', 'log_rel')}
    del _L0_ffn_all
    return {'x': x, 'itok_B_0_7': itok_B_0_7, 'itok_B_2182_4065': itok_B_2182_4065, 'itok_Bx16_0_63': itok_Bx16_0_63, 'itok_B_207_1644': itok_B_207_1644, '_lenS': _lenS, 'L0_cond_W_sess': _L0_cond_in['W_sess'], 'L0_cond_b_sess': _L0_cond_in['b_sess'], 'L0_cond_W2': _L0_cond_in['W2'], 'L0_cond_b2': _L0_cond_in['b2'], 'L0_attn_w_down': _L0_attn_in['w_down'], 'L0_attn_b_down': _L0_attn_in['b_down'], 'L0_attn_w_up': _L0_attn_in['w_up'], 'L0_attn_b_up': _L0_attn_in['b_up'], 'L0_attn_gate1': _L0_attn_in['gate1'], 'L0_attn_hy_in_w': _L0_attn_in['hy_in_w'], 'L0_attn_hy_conv_w': _L0_attn_in['hy_conv_w'], 'L0_attn_hy_conv_b': _L0_attn_in['hy_conv_b'], 'L0_attn_hy_dt_bias': _L0_attn_in['hy_dt_bias'], 'L0_attn_hy_A_log': _L0_attn_in['hy_A_log'], 'L0_attn_hy_D': _L0_attn_in['hy_D'], 'L0_attn_hy_fcD_w': _L0_attn_in['hy_fcD_w'], 'L0_attn_hy_norm_w': _L0_attn_in['hy_norm_w'], 'L0_attn_hy_out_w': _L0_attn_in['hy_out_w'], 'L0_cond2_Wq': _L0_cond2_in['Wq'], 'L0_cond2_Wk': _L0_cond2_in['Wk'], 'L0_cond2_Wv': _L0_cond2_in['Wv'], 'L0_cond2_Wo': _L0_cond2_in['Wo'], 'L0_cond2_q_norm_w': _L0_cond2_in['q_norm_w'], 'L0_cond2_k_norm_w': _L0_cond2_in['k_norm_w'], 'L0_cond2_k_cache': _L0_cond2_in['k_cache'], 'L0_cond2_v_cache': _L0_cond2_in['v_cache'], 'L0_ffn_Wq': _L0_ffn_in['Wq'], 'L0_ffn_Wr': _L0_ffn_in['Wr'], 'L0_ffn_aux_keys': _L0_ffn_in['aux_keys'], 'L0_ffn_aux_values': _L0_ffn_in['aux_values'], 'L0_ffn_Wvd': _L0_ffn_in['Wvd'], 'L0_ffn_Wvu': _L0_ffn_in['Wvu'], 'L0_ffn_Wu1': _L0_ffn_in['Wu1'], 'L0_ffn_bu1': _L0_ffn_in['bu1'], 'L0_ffn_Wu2': _L0_ffn_in['Wu2'], 'L0_ffn_bu2': _L0_ffn_in['bu2'], 'L0_ffn_gate_w1': _L0_ffn_in['gate_w1'], 'L0_ffn_gate_bias': _L0_ffn_in['gate_bias'], 'L0_ffn_log_rel': _L0_ffn_in['log_rel']}

def reference(x, itok_B_0_7, itok_B_2182_4065, itok_Bx16_0_63, itok_B_207_1644, _lenS, L0_cond_W_sess, L0_cond_b_sess, L0_cond_W2, L0_cond_b2, L0_attn_w_down, L0_attn_b_down, L0_attn_w_up, L0_attn_b_up, L0_attn_gate1, L0_attn_hy_in_w, L0_attn_hy_conv_w, L0_attn_hy_conv_b, L0_attn_hy_dt_bias, L0_attn_hy_A_log, L0_attn_hy_D, L0_attn_hy_fcD_w, L0_attn_hy_norm_w, L0_attn_hy_out_w, L0_cond2_Wq, L0_cond2_Wk, L0_cond2_Wv, L0_cond2_Wo, L0_cond2_q_norm_w, L0_cond2_k_norm_w, L0_cond2_k_cache, L0_cond2_v_cache, L0_ffn_Wq, L0_ffn_Wr, L0_ffn_aux_keys, L0_ffn_aux_values, L0_ffn_Wvd, L0_ffn_Wvu, L0_ffn_Wu1, L0_ffn_bu1, L0_ffn_Wu2, L0_ffn_bu2, L0_ffn_gate_w1, L0_ffn_gate_bias, L0_ffn_log_rel):
    import jax
    import jax.numpy as jnp

    def _L0_cond_ref(x, session_ids, channel_counts, seq_lens, W_sess, b_sess, W2, b2):
        import jax, jax.numpy as jnp
        import numpy as np
        SESSION_CHANNELS = [128, 160, 192, 224, 240, 248, 252, 32]
        N_SESS = len(SESSION_CHANNELS)
        B, MAX_C, MAX_T = (16, 32, 512)
        HID, N_SRC = (64, 32)
        cmask = (jnp.arange(x.shape[1])[None, :] < channel_counts[:, None]).astype(x.dtype)
        xm = x * cmask[:, :, None]
        W = W_sess[session_ids]
        b = b_sess[session_ids]
        h = jnp.einsum('bct,bch->bht', xm, W) + b[:, :, None]
        h = jax.nn.gelu(h, approximate=False)
        out = jnp.einsum('bht,hs->bst', h, W2) + b2[None, :, None]
        tmask = (jnp.arange(x.shape[2])[None, :] < seq_lens[:, None]).astype(x.dtype)
        return out * tmask[:, None, :]

    def _L0_attn_ref(x, w_down, b_down, w_up, b_up, gate1, hy_in_w, hy_conv_w, hy_conv_b, hy_dt_bias, hy_A_log, hy_D, hy_fcD_w, hy_norm_w, hy_out_w):
        import jax, jax.numpy as jnp
        import numpy as np
        HID = 512
        DM = 128
        DIN = 2 * DM
        DST = 16
        HD = 64
        NH = DIN // HD
        DCONV = 7
        CONV_DIM = DIN + 2 * DST
        DIN_PROJ = 2 * DIN + 2 * DST + 2 * NH
        SEQ, BATCH = (256, 4)

        def _causal_conv(x, w, b):
            y = jax.lax.conv_general_dilated(jnp.transpose(x, (0, 2, 1)), w, (1,), [(DCONV - 1, 0)], feature_group_count=CONV_DIM, dimension_numbers=('NCH', 'OIH', 'NCH'))
            return jnp.transpose(y, (0, 2, 1)) + b

        def _ssm_scan(x, dt, A, B, C):
            dA = jnp.exp(dt * A)
            dBx = dt[..., None] * x

            def step(h, t):
                dA_t, dBx_t, B_t, C_t = t
                h = dA_t[:, :, None, None] * h + dBx_t[..., None] * B_t[:, None, None, :]
                y = jnp.einsum('bhpn,bn->bhp', h, C_t)
                return (h, y)
            h0 = jnp.zeros((x.shape[0], NH, HD, DST), x.dtype)
            _, ys = jax.lax.scan(step, h0, (jnp.moveaxis(dA, 1, 0), jnp.moveaxis(dBx, 1, 0), jnp.moveaxis(B, 1, 0), jnp.moveaxis(C, 1, 0)))
            return jnp.moveaxis(ys, 0, 1)

        def _hydra(u, in_w, conv_w, conv_b, dt_bias, A_log, D, fcD_w, norm_w, out_w):
            b, l, _ = u.shape
            zxbcdt = u @ in_w.T
            z = zxbcdt[..., :DIN]
            xBC = zxbcdt[..., DIN:DIN + CONV_DIM]
            dt2 = zxbcdt[..., DIN + CONV_DIM:]
            dt_fw = jax.nn.softplus(dt2[..., :NH] + dt_bias)
            dt_bw = jax.nn.softplus(jnp.flip(dt2[..., NH:], 1) + dt_bias)
            xBC = jax.nn.silu(_causal_conv(xBC, conv_w, conv_b))
            xs = xBC[..., :DIN]
            Bm = xBC[..., DIN:DIN + DST]
            Cm = xBC[..., DIN + DST:]
            A = -jnp.exp(A_log)
            x4 = xs.reshape(b, l, NH, HD)
            y_fw = _ssm_scan(x4, dt_fw, A, Bm, Cm).reshape(b, l, DIN)
            y_bw = jnp.flip(_ssm_scan(jnp.flip(x4, 1), dt_bw, A, jnp.flip(Bm, 1), jnp.flip(Cm, 1)).reshape(b, l, DIN), 1)
            zero = jnp.zeros((b, 1, DIN), u.dtype)
            y = jnp.concatenate([zero, y_fw[:, :-1]], 1) + jnp.concatenate([y_bw[:, 1:], zero], 1)
            y = y + xs * jnp.repeat(xs @ fcD_w.T + D, HD, axis=-1)
            yz = y * jax.nn.silu(z)
            y = yz * jax.lax.rsqrt(jnp.mean(jnp.square(yz), -1, keepdims=True) + 1e-05) * norm_w
            return y @ out_w.T
        x_init = x
        h = x @ w_down.T + b_down
        h = jnp.transpose(h, (1, 0, 2))
        h = jax.nn.gelu(h, approximate=False)
        xmid = h
        hp = (hy_in_w, hy_conv_w, hy_conv_b, hy_dt_bias, hy_A_log, hy_D, hy_fcD_w, hy_norm_w, hy_out_w)
        h = _hydra(h, *hp)
        h = _hydra(h, *hp)
        alpha = jax.nn.sigmoid(gate1)
        h = alpha * xmid + (1.0 - alpha) * h
        h = xmid + h
        h = h @ w_up.T + b_up
        return x_init + jnp.transpose(h, (1, 0, 2))

    def _L0_cond2_ref(x, Wq, Wk, Wv, Wo, q_norm_w, k_norm_w, k_cache, v_cache, block_table, cache_seqlens):
        import jax, jax.numpy as jnp
        import numpy as np
        B, S, HID = (4, 128, 512)
        D, HQ, HK = (128, 32, 8)
        PAGES, PSIZE, NPP = (64, 32, 16)
        THETA = 10000.0
        EPS = 1e-06
        SCALE = 1.0 / float(np.sqrt(D))

        def _rmsnorm(t, w):
            var = jnp.mean(t * t, axis=-1, keepdims=True)
            return t * jax.lax.rsqrt(var + EPS) * w

        def _rope(t, pos):
            inv_freq = 1.0 / THETA ** (jnp.arange(0, D, 2, dtype=jnp.float32) / D)
            freqs = pos[..., None].astype(jnp.float32) * inv_freq
            cos = jnp.cos(freqs)[:, :, None, :]
            sin = jnp.sin(freqs)[:, :, None, :]
            t1, t2 = (t[..., :D // 2], t[..., D // 2:])
            return jnp.concatenate([t1 * cos - t2 * sin, t2 * cos + t1 * sin], axis=-1)
        bsz, seqlen, _ = x.shape
        q = jnp.einsum('bsd,ed->bse', x, Wq).reshape(bsz, seqlen, HQ, D)
        k = jnp.einsum('bsd,ed->bse', x, Wk).reshape(bsz, seqlen, HK, D)
        v = jnp.einsum('bsd,ed->bse', x, Wv).reshape(bsz, seqlen, HK, D)
        q = _rmsnorm(q, q_norm_w)
        k = _rmsnorm(k, k_norm_w)
        pos = cache_seqlens[:, None] + jnp.arange(seqlen)[None, :]
        q = _rope(q, pos)
        k = _rope(k, pos)
        L = NPP * PSIZE
        kc = k_cache[block_table].reshape(bsz, L, HK, D)
        vc = v_cache[block_table].reshape(bsz, L, HK, D)
        k_all = jnp.concatenate([kc, k], axis=1)
        v_all = jnp.concatenate([vc, v], axis=1)
        valid_c = jnp.arange(L)[None, :] < cache_seqlens[:, None]
        valid = jnp.concatenate([valid_c, jnp.ones((bsz, seqlen), dtype=bool)], axis=1)
        rep = HQ // HK
        k_all = jnp.repeat(k_all, rep, axis=2)
        v_all = jnp.repeat(v_all, rep, axis=2)
        scores = jnp.einsum('bqhd,bkhd->bhqk', q, k_all) * SCALE
        scores = jnp.where(valid[:, None, None, :], scores, -1e+30)
        probs = jax.nn.softmax(scores, axis=-1)
        o = jnp.einsum('bhqk,bkhd->bqhd', probs, v_all)
        o = o.reshape(bsz, seqlen, HQ * D)
        return jnp.einsum('bse,de->bsd', o, Wo)

    def _L0_ffn_ref(hidden_states, Wq, Wr, aux_keys, aux_values, Wvd, Wvu, Wu1, bu1, Wu2, bu2, gate_w1, gate_bias, log_rel):
        import jax, jax.numpy as jnp
        import numpy as np
        HID, BOT, RDIM, NSLOT, K, VB = (512, 64, 48, 128, 8, 32)
        TAU_LOW, TAU_HIGH, EARLY_EXIT = (0.5, 2.0, 0.05)

        def _uncertainty(h, Wu1, bu1, Wu2, bu2):
            var = jnp.var(h, axis=-1)
            log_var = jnp.log1p(var)
            norm_var = log_var / (jnp.mean(log_var) + 1e-06)
            learned = (jax.nn.gelu(h @ Wu1.T + bu1) @ Wu2.T + bu2)[..., 0]
            return jnp.clip(norm_var * 0.5 + jax.nn.sigmoid(learned) * 2.5, 0.0, 5.0)
        query = hidden_states @ Wq.T
        rq = query @ Wr.T
        rk = aux_keys @ Wr.T
        router_scores = jnp.einsum('bsr,nr->bsn', rq, rk) / np.sqrt(RDIM) + log_rel
        top_scores, top_idx = jax.lax.top_k(router_scores, K)
        sel_keys = aux_keys[top_idx]
        attn = jnp.einsum('bsd,bskd->bsk', query, sel_keys) / np.sqrt(BOT) + log_rel[top_idx]
        w = jax.nn.softmax(attn, axis=-1)
        sel_vals = aux_values[top_idx]
        aux_out = jnp.einsum('bsk,bskh->bsh', w, sel_vals)
        aux_out = aux_out @ Wvd.T @ Wvu.T
        u = _uncertainty(hidden_states, Wu1, bu1, Wu2, bu2)
        u_norm = jnp.clip((u - TAU_LOW) / (TAU_HIGH - TAU_LOW), 0.0, 1.0)
        gate = jax.nn.sigmoid(gate_w1 * u_norm + gate_bias)
        gate = jnp.where(gate < EARLY_EXIT, 0.0, gate)
        return hidden_states + gate[..., None] * aux_out
    x = x + _L0_attn_ref(_L0_cond_ref(x, itok_B_0_7, _lenS, itok_B_2182_4065, L0_cond_W_sess, L0_cond_b_sess, L0_cond_W2, L0_cond_b2), L0_attn_w_down, L0_attn_b_down, L0_attn_w_up, L0_attn_b_up, L0_attn_gate1, L0_attn_hy_in_w, L0_attn_hy_conv_w, L0_attn_hy_conv_b, L0_attn_hy_dt_bias, L0_attn_hy_A_log, L0_attn_hy_D, L0_attn_hy_fcD_w, L0_attn_hy_norm_w, L0_attn_hy_out_w)
    x = x + _L0_ffn_ref(_L0_cond2_ref(x, L0_cond2_Wq, L0_cond2_Wk, L0_cond2_Wv, L0_cond2_Wo, L0_cond2_q_norm_w, L0_cond2_k_norm_w, L0_cond2_k_cache, L0_cond2_v_cache, itok_Bx16_0_63, itok_B_207_1644), L0_ffn_Wq, L0_ffn_Wr, L0_ffn_aux_keys, L0_ffn_aux_values, L0_ffn_Wvd, L0_ffn_Wvu, L0_ffn_Wu1, L0_ffn_bu1, L0_ffn_Wu2, L0_ffn_bu2, L0_ffn_gate_w1, L0_ffn_gate_bias, L0_ffn_log_rel)
    return x

_drawn_inputs = setup_inputs


def setup_inputs(seed=0):
    import zlib

    import numpy as np

    out = dict(_drawn_inputs(seed))
    spreads = {'L0_attn_b_down': (0.0, 0.338),
     'L0_attn_b_up': (0.0, 0.1),
     'L0_attn_hy_conv_b': (0.0, 0.8),
     'L0_attn_hy_D': (1.0, 0.6),
     'L0_attn_hy_norm_w': (1.0, 0.6),
     'L0_ffn_bu1': (0.0, 2.0),
     'L0_ffn_log_rel': (0.0, 2.0)}
    factors = {'L0_attn_w_down': 2.929,
     'L0_attn_hy_in_w': 8.0,
     'L0_attn_hy_conv_w': 8.0,
     'L0_attn_hy_dt_bias': 8.0,
     'L0_attn_hy_A_log': 8.0,
     'L0_attn_hy_fcD_w': 8.0,
     'L0_attn_hy_out_w': 8.0,
     'L0_cond2_Wk': 8.0,
     'L0_cond2_Wv': 7.619,
     'L0_cond2_k_norm_w': 8.0,
     'L0_ffn_Wq': 46.051,
     'L0_ffn_Wr': 58.835,
     'L0_ffn_aux_keys': 46.311,
     'L0_ffn_aux_values': 44.356,
     'L0_ffn_Wvd': 45.648,
     'L0_ffn_Wvu': 44.598,
     'L0_ffn_Wu1': 64.0,
     'L0_ffn_Wu2': 64.0,
     'L0_cond2_k_cache': 3.904}
    for name, (base, spread) in spreads.items():
        noise = np.random.default_rng([zlib.crc32(name.encode()), seed]).standard_normal(out[name].shape)
        drawn = base * np.exp(spread * noise) if base else spread * noise
        out[name] = jnp.asarray(drawn.astype(out[name].dtype))
    for name, factor in factors.items():
        out[name] = (out[name] * factor).astype(out[name].dtype)
    return out
```

```python
from contextlib import ExitStack

import numpy as np
import concourse.bass as bass
from concourse import mybir

F32 = mybir.dt.float32
I32 = mybir.dt.int32
ACT = mybir.ActivationFunctionType
ALU = mybir.AluOpType
AXX = mybir.AxisListType.X
ds = bass.ds

P = 128
B, S, HID = 32, 32, 512
TOK = B * S
HALF = TOK // 2
KC = HID // P
SESS, CHID = 8, 64
DM, DIN, DST, NH, DCONV = 128, 256, 16, 4, 7
PADL = S + DCONV - 1
D, HQ, HK = 128, 32, 8
REP = HQ // HK
PAGES, NPP = 64, 16
LC = NPP * S
LK = LC + S
BOT, RDIM, NSLOT, TOPK, VB = 64, 48, 128, 8, 32
SCALE = 1.0 / float(np.sqrt(D))
THETA = 10000.0
TILES = TOK // P
BPT = P // S

PACK_A = [
    ("sessidx", 1), ("chan", 1), ("tcol", KC), ("bsess", P), ("w2", 2 * S), ("b2", S),
    ("wdown", KC * DM), ("bdown", 1), ("srow", S), ("invf", 1), ("sign", 1), ("qnw", 1), ("knw", 1),
    ("dtw", 2 * NH), ("bcw", 3 * DST), ("xw", DIN), ("zw", DIN), ("convx", 2 * DCONV),
    ("convbc", DCONV), ("convbx", 2), ("convbbc", 1), ("dtb", 2 * NH), ("alog", NH), ("dskip", 2),
    ("fcd", 2 * DIN), ("normw", 2), ("outw", 2 * DM), ("wup", HID), ("bup", KC), ("gate1", 1),
    ("ufw", P), ("ubw", P), ("before", S), ("after", S),
]
PACK_B = [
    ("ident", P), ("iota", LC),
    ("fwq", KC * BOT), ("fwr", RDIM), ("fkeys", NSLOT), ("flog", NSLOT), ("fval", KC * NSLOT),
    ("fwvd", KC * VB), ("fwvu", HID), ("fwu1", KC * P), ("fbu1", 1), ("fwu2", 1), ("fbu2", 1),
    ("fgw", 1), ("fgb", 1),
]


def columns(pack):
    at, out = 0, {}
    for name, n in pack:
        out[name] = (at, n)
        at += n
    return out, at


COL_A, COLS_A = columns(PACK_A)
COL_B, COLS_B = columns(PACK_B)

PI2_A, PI2_B = 6.28125, 0.0019350051879882812
PI2_C = float(2 * np.pi - PI2_A - PI2_B)
ROUND = 12582912.0
PI = 3.1415925
NEG = -1e30
EPS_HYDRA, EPS_QK = 1e-5, 1e-6
INTS = 4 * B
NPAIR = B // 2
NCHAIN = 44
KTILES, VTILES, QTILES = 16, 16, 32
UNITS = B * HK


def adaln_attention_ffn(nc, t):
    with ExitStack() as ctx:
        def sem(name):
            return ctx.enter_context(nc.semaphore(name))

        def sb(stack, name, shape, dt=F32):
            return stack.enter_context(nc.sbuf_tensor(name, shape, dt))

        psum = ctx.enter_context(nc.psum_tensor("psum", [P, 8, 512], F32))

        def bank(n):
            return psum[:, n, :]

        pkb = sb(ctx, "pkb", [P, COLS_B])
        x2T = sb(ctx, "x2T", [P, KC, TOK])
        ints = sb(ctx, "ints", [P, INTS], I32)
        intf = sb(ctx, "intf", [P, INTS])
        table = sb(ctx, "table", [1, B * NPP], I32)
        ones = sb(ctx, "ones", [P, P])
        rq = sb(ctx, "rq", [P, B * HK])
        nrq = sb(ctx, "nrq", [P, B * HK])
        with ExitStack() as c1:
            wring = sb(c1, "wring", [P, 2, KC, 1024])
            tabs = sb(c1, "tabs", [P, 4, TOK])
            with ExitStack() as s1:
                pka = sb(s1, "pka", [P, COLS_A])
                xmid = sb(s1, "xmid", [P, TOK])
                u = sb(s1, "u", [P, TOK])
                with ExitStack() as st:
                    xc = sb(st, "xc", [2 * S, NPAIR, HID])
                    wgat = sb(st, "wgat", [2 * S, NPAIR, P])
                    wst = sb(st, "wst", [2 * S, 2, P])
                    cmask = sb(st, "cmask", [2 * S, NPAIR])
                    tmask = sb(st, "tmask", [P, KC, B])
                    onehot = sb(st, "onehot", [SESS, B])
                    bias1 = sb(st, "bias1", [P, NPAIR])
                    hbuf = sb(st, "hbuf", [P, 2, HID])
                    condT = sb(st, "condT", [P, KC, TOK])
                    ang = sb(st, "ang", [P, TOK])
                    turns = sb(st, "turns", [P, 2, TOK])
                with ExitStack() as st:
                    xpad = sb(st, "xpad", [P, 2, S, PADL])
                    bcpad = sb(st, "bcpad", [3 * DST, S, PADL])
                    cacc = sb(st, "cacc", [P, 3, TOK])
                    xs = sb(st, "xs", [P, 2, TOK])
                    Bt = sb(st, "Bt", [DST, TOK])
                    Ct = sb(st, "Ct", [DST, TOK + 2])
                    zs = sb(st, "zs", [P, 2, TOK])
                    xtok = sb(st, "xtok", [P, TILES, DIN])
                    dtv = sb(st, "dtv", [P, 5, TILES * 2 * NH])
                    dtd = sb(st, "dtd", [P, 4, TILES * NH])
                    negA = sb(st, "negA", [P, NH])
                    Rm = sb(st, "Rm", [P, 2, TILES * NH, S])
                    E = sb(st, "E", [P, TILES * NH, S])
                    W12 = sb(st, "W12", [P, 2, TILES, S])
                    M = sb(st, "M", [P, TILES * NH, P])
                    yb = sb(st, "yb", [P, 2, TOK])
                    rb = sb(st, "rb", [P, 2, HALF])
                    outw = sb(st, "outw", [P, 2, DM])
                    alpha = sb(st, "alpha", [P, 3])
            T12 = Rm
            with ExitStack() as st:
                KT = sb(st, "KT", [P, PAGES * HK * S])
                stage = sb(st, "stage", [P, 4, REP * HALF])
                ab = sb(st, "ab", [P, 2, 2, HALF])
                vo = sb(st, "vo", [P, 2, HK * D])
        with ExitStack() as st:
            kring = sb(st, "kring", [P, 2, NPP + 1, HK * S])
            qring = sb(st, "qring", [P, 2, HQ * S])
            mask = sb(st, "mask", [P, LK])
            sb(st, "gap", [P, 2 * KC * 1024 + 4 * TOK - 2 * (NPP + 1) * HK * S - 2 * HQ * S - LK])
            sb(st, "KT_place", [P, PAGES * HK * S])
            vring = sb(st, "vring", [P, 2, BPT + 1, HK * D])
            oring = sb(st, "oring", [P, 2, HQ * S])
            prob = sb(st, "prob", [P, 4, LK])
            pT = sb(st, "pT", [P, 2, LC])
            pT4 = sb(st, "pT4", [S, 2, P])
            mx = sb(st, "mx", [P, 4])
            nb = sb(st, "nb", [P, 4])
            rs = sb(st, "rs", [P, 4])
            ri = sb(st, "ri", [P, 4])
        wo = KT[:, :].rearrange("p (h n) -> p h n", h=HQ)
        with ExitStack() as st:
            oin = sb(st, "oin", [P, BPT, HQ * S])
            htok = sb(st, "htok", [P, TILES, HID])
            hT = sb(st, "hT", [P, KC, TOK])
            sb(st, "KT_place2", [P, PAGES * HK * S])
            bn = sb(st, "bn", [P, TILES, 6])
            mv = sb(st, "mv", [P, TILES, 2])
            with ExitStack() as so:
                oin2 = sb(so, "oin2", [P, BPT, HQ * S])
                operm = sb(so, "operm", [P, 2, HQ, BPT, S])
            queryT = sb(st, "queryT", [BOT, TOK])
            rqT = sb(st, "rqT", [RDIM, TOK])
            rkT = sb(st, "rkT", [RDIM, NSLOT])
            AV = sb(st, "AV", [NSLOT, VB])
            uT = sb(st, "uT", [P, TOK])
            rsc = sb(st, "rsc", [P, TILES, NSLOT])
            rep8 = sb(st, "rep8", [P, TILES, NSLOT])
            asc = sb(st, "asc", [P, TILES, NSLOT])
            top8 = sb(st, "top8", [P, TILES, TOPK])
            amx = sb(st, "amx", [P, TILES])
            wsum = sb(st, "wsum", [P, TILES])
            sm = sb(st, "sm", [P, 10, TILES])
            lsum = sb(st, "lsum", [P, 2])
            wTs = sb(st, "wTs", [NSLOT, TOK])
            auxT = sb(st, "auxT", [VB, TOK])
        oins = [oin, oin2]

        def A(name, rows=P, lo=0):
            a, n = COL_A[name]
            return pka[lo:lo + rows, a:a + n]

        def G(name, rows=P, lo=0):
            a, n = COL_B[name]
            return pkb[lo:lo + rows, a:a + n]

        s_pka, s_pkb, s_x, s_ids, s_xT = sem("s_pka"), sem("s_pkb"), sem("s_x"), sem("s_ids"), sem("s_xT")
        s_wz, s_gather = sem("s_wz"), sem("s_gather")
        s_prep, s_bias = sem("s_prep"), sem("s_bias")
        s_masks = sem("s_masks")
        s_wst = sem("s_wst")
        s_h1, s_g1 = sem("s_h1"), sem("s_g1")
        s_co, s_ca, s_cT = sem("s_co"), sem("s_ca"), sem("s_cT")
        s_dn, s_xm = sem("s_dn"), sem("s_xm")
        s_xc = sem("s_xc")
        s_ang, s_sin, s_tab = sem("s_ang"), sem("s_sin"), sem("s_tab")
        s_hz, s_hzs = sem("s_hz"), sem("s_hzs")
        s_u = sem("s_u")
        s_hd = sem("s_hd")
        s_pr, s_xp = sem("s_pr"), sem("s_xp")
        s_dtp, s_nv, s_ey = sem("s_dtp"), sem("s_nv"), sem("s_ey")
        s_zp, s_zs, s_cv, s_xs = sem("s_zp"), sem("s_zs"), sem("s_cv"), sem("s_xs")
        s_R, s_seg, s_E, s_GG, s_W = sem("s_R"), sem("s_seg"), sem("s_E"), sem("s_GG"), sem("s_W")
        s_xt, s_xe, s_T, s_Ts, s_M = sem("s_xt"), sem("s_xe"), sem("s_T"), sem("s_Ts"), sem("s_M")
        s_r, s_t, s_y, s_yz, s_ysq = sem("s_r"), sem("s_t"), sem("s_y"), sem("s_yz"), sem("s_ysq")
        s_ss0, s_rr, s_rb, s_hy = sem("s_ss0"), sem("s_rr"), sem("s_rb"), sem("s_hy")
        s_al, s_hf, s_up, s_x2 = sem("s_al"), sem("s_hf"), sem("s_up"), sem("s_x2")
        s_w = [sem("s_w0"), sem("s_w1")]
        s_pj, s_sq, s_ab, s_po, s_ss = sem("s_pj"), sem("s_sq"), sem("s_ab"), sem("s_po"), sem("s_ss")
        s_add, s_kr1, s_kr2 = sem("s_add"), sem("s_kr1"), sem("s_kr2")
        s_kst, s_qst = sem("s_kst"), [sem("s_qst0"), sem("s_qst1")]
        s_ve, s_vst = sem("s_ve"), [sem("s_vst0"), sem("s_vst1")]
        s_rqa, s_rqb, s_rq = sem("s_rqa"), sem("s_rqb"), sem("s_rq")
        s_KT, s_in, s_v = sem("s_KT"), [sem("s_in0"), sem("s_in1")], [sem("s_v0"), sem("s_v1")]
        s_kc, s_msk = sem("s_kc"), sem("s_msk")
        s_sc, s_mx, s_nb, s_ex = sem("s_sc"), sem("s_mx"), sem("s_nb"), sem("s_ex")
        s_rc, s_pn, s_tp, s_pt, s_p4 = sem("s_rc"), sem("s_pn"), sem("s_tp"), sem("s_pt"), sem("s_p4")
        s_pv, s_ov = sem("s_pv"), sem("s_ov")
        s_ost = [sem("s_ost0"), sem("s_ost1")]
        s_wo, s_oin = sem("s_wo"), [sem("s_oin0"), sem("s_oin1")]
        s_hp, s_ht, s_htt, s_hT, s_bn = sem("s_hp"), sem("s_ht"), sem("s_htt"), sem("s_hT"), sem("s_bn")
        s_fp, s_fe, s_fd, s_fa = sem("s_fp"), sem("s_fe"), sem("s_fd"), sem("s_fa")
        s_rsp, s_rse, s_asp, s_ase = sem("s_rsp"), sem("s_rse"), sem("s_asp"), sem("s_ase")
        s_ler, s_am, s_exw, s_w8, s_wt, s_wte = sem("s_ler"), sem("s_am"), sem("s_exw"), sem("s_w8"), sem("s_wt"), sem("s_wte")
        s_lv, s_ls, s_sg, s_ga, s_gb, s_gate = sem("s_lv"), sem("s_ls"), sem("s_sg"), sem("s_ga"), sem("s_gb"), sem("s_gate")
        s_ax, s_axe, s_fo, s_fin, s_out = sem("s_ax"), sem("s_axe"), sem("s_fo"), sem("s_fin"), sem("s_out")
        s_mean, s_ab0, s_op = sem("s_mean"), sem("s_ab0"), sem("s_op")
        s_seen = sem("s_seen")

        block = ctx.enter_context(nc.Block())

        def after(eng, sem, value):
            if not isinstance(value, int) or value > 0:
                eng.wait_ge(sem, value)

        def page_number(eng, b, n):
            return eng.value_load(table[0:1, ds(NPP * b + n, 1)], min_val=0, max_val=PAGES - 1)

        def bc(ap, axis, shape):
            return ap.unsqueeze(axis).to_broadcast(shape)

        def score(j):
            return psum[:, 2 * (j % 2):2 * (j % 2) + 2, :].rearrange("p a n -> p (a n)")[:, 0:LK]

        def by_batch(ap):
            return ap.rearrange("p (b s) -> p b s", s=S)

        ko = [stage[:, 2 * h:2 * h + 2, :].rearrange("p a n -> p (a n)").rearrange("p (b g s) -> p b g s", g=HK, s=S)
              for h in range(2)]
        sqr = [stage[:, n, :].rearrange("p (b r s) -> p b r s", r=REP, s=S) for n in range(2)]
        qor = [stage[:, 2 + n, :].rearrange("p (b r s) -> p b r s", r=REP, s=S) for n in range(2)]
        ksq = [vo[:, n, 0:HALF] for n in range(2)]
        rk = [vo[:, n, HALF:TOK] for n in range(2)]

        @block.sync
        def _(sp):
            sp.dma_start(ints[:, :], t["ints"]).then_inc(s_ids, 16)
            sp.dma_start(pka[:, :], t["packa"]).then_inc(s_pka, 16)
            xv = t["x"].rearrange("(p j) c w -> (j c) p w", j=2)
            for j in range(2):
                sp.dma_start(xc[S * j:S * j + S, :, :],
                             t["x"].rearrange("(p j) c w -> j c p w", j=2)[j]).then_inc(s_x, 16)
            sp.wait_ge(s_ids, 16)
            sp.wait_ge(s_wz, 1)
            with sp.Fori(0, NPAIR) as p:
                for j in range(2):
                    sid = sp.value_load(ints[0:1, ds(2 * p + j, 1)], min_val=0, max_val=SESS - 1)
                    sp.dma_start(wgat[S * j:S * j + S, ds(p, 1), CHID * j:CHID * j + CHID],
                                 t["wsess"][ds(sid, 1), :, :].rearrange("a c h -> c a h")).then_inc(s_gather, 16)
            sp.dma_start(x2T[:, :, :], t["xT"].rearrange("(k p) n -> p k n", p=P)).then_inc(s_xT, 16)
            sp.dma_start(pkb[:, :], t["packb"]).then_inc(s_pkb, 16)
            sp.dma_start(table[:, :], t["table"]).then_inc(s_ids, 16)
            sp.dma_start(wring[:, 0], t["wkT"].rearrange("(k p) n -> p k n", p=P)).then_inc(s_w[0], 16)
            sp.dma_start(wring[:, 1], t["wvT"].rearrange("(k p) n -> p k n", p=P)).then_inc(s_w[1], 16)

            sp.wait_ge(s_x2, 2 * KC)
            sp.dma_start(KT[:, :], t["kcT"].rearrange("d a g s -> d (a g s)")).then_inc(s_KT, 16)
            wq_v = t["wqT"].rearrange("(k p) n -> p k n", p=P)
            sp.wait_ge(s_pj, KTILES)
            sp.dma_start(wring[:, 0], wq_v[:, :, 0:1024]).then_inc(s_w[0], 16)
            kv = t["k_s"].rearrange("b p n -> p b n")
            for h in range(2):
                sp.wait_ge(s_po, HK * (h + 1))
                for q in range(2):
                    done = s_kst if h == 0 else s_qst[q]
                    sp.dma_start(kv[:, 16 * h + 8 * q:16 * h + 8 * q + 8, :],
                                 ko[h][:, 8 * q:8 * q + 8].rearrange("p b g s -> p b (g s)")).then_inc(done, 16)
            for n in range(TILES):
                sp.wait_ge(s_ve, 2 * n + 2)
                sp.dma_start(t["v_s"][P * n:P * n + P, :], vo[:, n % 2, :]).then_inc(s_vst[n % 2], 16)
            sp.dma_start(wring[:, 1], wq_v[:, :, 1024:2048]).then_inc(s_w[1], 16)
            qv = t["q_s"].rearrange("b p n -> p b n")
            for sl in range(4):
                for m in range(4):
                    g, h = 2 * sl + m // 2, m % 2
                    sp.wait_ge(s_po, KTILES + 16 * sl + 4 * m + 4)
                    sp.dma_start(qv[:, 16 * h:16 * h + 16, P * g:P * g + P],
                                 qor[h].rearrange("p b r s -> p b (r s)")).then_inc(s_qst[h], 16)
                if sl < 2:
                    sp.dma_start(wring[:, sl], wq_v[:, :, 1024 * (sl + 2):1024 * (sl + 3)]).then_inc(s_w[sl], 16)

            pages = t["vc"].rearrange("a s g d -> a s (g d)")

            def load(b, i, par):
                after(sp, s_sc, 8 * b - 8)
                sp.dma_start(qring[:, par, :], t["q_s"][ds(b, 1)].rearrange("a p n -> p (a n)")).then_inc(s_in[par], 16)
                sp.dma_start(kring[:, par, NPP, :], t["k_s"][ds(b, 1)].rearrange("a p n -> p (a n)")).then_inc(s_in[par], 16)
                after(sp, s_pv, 8 * b - 8)
                sp.dma_start(vring[0:S, par, BPT, :], t["v_s"][ds(S * b, S), :]).then_inc(s_v[par], 16)
                for n in range(NPP):
                    page = page_number(sp, b, n)
                    sp.dma_start(vring[S * (n % BPT):S * (n % BPT) + S, par, n // BPT, :],
                                 pages[ds(page, 1)].rearrange("a s n -> s (a n)")).then_inc(s_v[par], 16)

            def store(b, par):
                sp.wait_ge(s_ov, 8 * b + 8)
                sp.dma_start(t["o_s"][ds(b, 1)].rearrange("a p n -> p (a n)"), oring[:, par, :]).then_inc(s_ost[par], 16)

            sp.wait_ge(s_rq, 1)
            sp.wait_ge(s_qst[0], 16 * (HK + 1))
            sp.wait_ge(s_qst[1], 16 * (HK + 1))
            sp.wait_ge(s_kst, 32)
            sp.wait_ge(s_vst[0], 16 * TILES // 2)
            sp.wait_ge(s_vst[1], 16 * TILES // 2)
            load(0, 0, 0)
            load(1, 0, 1)
            with sp.Fori(0, B // 2 - 1) as i:
                for par in range(2):
                    store(2 * i + par, par)
                    load(2 * i + 2 + par, i + 1, par)
            sp.wait_ge(s_kc, NPP * B)
            sp.dma_start(wo, t["woT"].rearrange("(h p) n -> p h n", p=P)).then_inc(s_wo, 16)
            store(B - 2, 0)
            store(B - 1, 1)
            for par in range(2):
                sp.wait_ge(s_ost[par], 16 * (B // 2))
            for n in range(TILES):
                if n >= 2:
                    sp.wait_ge(s_op, n - 1)
                sp.dma_start(oins[n % 2][:, :, :],
                             t["o_s"][BPT * n:BPT * n + BPT].rearrange("b p n -> p b n")).then_inc(s_oin[n % 2], 16)
            for n in range(2 * KC):
                m, h = n // 2, n % 2
                sp.wait_ge(s_fin, n + 1)
                sp.dma_start(t["out"][P * m:P * m + P, HALF * h:HALF * h + HALF],
                             hT[:, m, HALF * h:HALF * h + HALF]).then_inc(s_out, 16)
            sp.wait_ge(s_out, 16 * 2 * KC)

        @block.gpsimd
        def _(pool):
            pool.memset(wgat[:, :, :], 0.0).then_inc(s_wz, 1)
            pool.memset(ones[:, :], 1.0).then_inc(s_wz, 1)
            pool.wait_ge(s_xT, 16)
            with pool.Fori(0, 2) as h:
                for k in range(KC):
                    pool.wait_ge(s_cT, KC * h + k + 1)
                    pool.tensor_tensor(x2T[:, k, ds(HALF * h, HALF)], x2T[:, k, ds(HALF * h, HALF)],
                                       condT[:, k, ds(HALF * h, HALF)], ALU.add).then_inc(s_xc, 1)
            pool.wait_ge(s_xc, 2 * KC)
            pool.wait_ge(s_xm, 2)
            pool.wait_ge(s_tab, 4)
            pool.memset(xpad[:, :, :, 0:DCONV - 1], 0.0).then_inc(s_hz, 1)
            pool.memset(bcpad[:, :, 0:DCONV - 1], 0.0).then_inc(s_hz, 1)
            pool.memset(Ct[:, 0:1], 0.0).then_inc(s_hz, 1)
            pool.memset(Ct[:, TOK + 1:TOK + 2], 0.0).then_inc(s_hz, 1)
            pool.memset(M[:, :, :], 0.0).then_inc(s_hz, 1)
            with pool.Fori(0, 2) as i:
                pool.wait_ge(s_W, 16 * i + 16)
                pool.wait_ge(s_seg, 2 * i + 2)
                w4 = bc(W12[:, 1], 2, [P, TILES, NH, S])
                d4 = bc(dtd[:, 1].rearrange("p (a h) -> p a h", h=NH), 3, [P, TILES, NH, S])
                pool.tensor_tensor(T12[:, 1].rearrange("p (a h) s -> p a h s", h=NH), w4, d4, ALU.mult).then_inc(s_T, 1)
                pool.wait_ge(s_T, 3 * i + 2)
                pool.tensor_tensor(T12[:, 0], T12[:, 0], T12[:, 1], ALU.add).then_inc(s_T, 1)

            def key_scale(n):
                h, g = n // HK, n % HK
                pool.wait_ge(s_add, n + 1)
                pool.wait_ge(s_kr2, n + 1)
                pool.tensor_tensor(ko[h][:, :, g, :], by_batch(ab[:, n % 2, 0, :]), by_batch(rk[n % 2]),
                                   ALU.mult).then_inc(s_po, 1)

            for n in range(KTILES):
                pool.wait_ge(s_ab, n + 1)
                pool.tensor_tensor(ab[:, n % 2, 0, :], ab[:, n % 2, 0, :], ab[:, n % 2, 1, :], ALU.add).then_inc(s_add, 1)
                if n >= 1:
                    key_scale(n - 1)
            key_scale(KTILES - 1)
            with pool.Fori(0, 2) as i:
                for n in range(QTILES):
                    m, r = n // 4, n % 4
                    if r == 0:
                        pool.wait_ge(s_qst[m % 2], 16 * (4 * i + m // 2 + 1))
                    pool.wait_ge(s_ab, KTILES + QTILES * i + n + 1)
                    pool.tensor_tensor(qor[m % 2][:, :, r, :], by_batch(ab[:, n % 2, 0, :]),
                                       by_batch(ab[:, n % 2, 1, :]), ALU.add).then_inc(s_po, 1)

            def normalise(n, slot):
                pool.wait_ge(s_rc, n + 1)
                pool.sem_inc(s_seen, 1)
                pool.tensor_scalar(prob[:, slot, :], prob[:, slot, :], ri[:, slot:slot + 1], 1.0,
                                   ALU.mult, ALU.mult).then_inc(s_pn, 1)

            normalise(0, 0)
            normalise(1, 1)

            def pool_turn(i):
                for j in range(16):
                    n = 16 * i + j
                    if not (isinstance(i, int) and n + 2 >= UNITS):
                        normalise(n + 2, (j + 2) % 4)

            pool_turn(0)
            with pool.Fori(1, 15) as i:
                pool_turn(i)
            pool_turn(15)
            pool.wait_ge(s_hT, TILES)
            pool.tensor_tensor(x2T[:, :, :], x2T[:, :, :], hT[:, :, :], ALU.add).then_inc(s_fa, 1)

        @block.scalar
        def _(act):
            with act.Fori(0, 2) as h:
                for p in range(8):
                    n = 8 * h + p
                    if p == 0:
                        act.wait_ge(s_prep, 9)
                    act.wait_ge(s_h1, n + 1)
                    if p >= 2:
                        act.wait_ge(s_co, KC * (n - 1))
                    act.activation(hbuf[:, p % 2, :], bank(p % 2), ACT.Gelu,
                                   bias=bias1[:, ds(n, 1)]).then_inc(s_g1, 1)
                act.wait_ge(s_dn, h + 1)
                act.activation(xmid[:, :].rearrange("p (s b) -> p b s", b=B)[:, ds(16 * h, 16), :],
                               by_batch(bank(6)), ACT.Gelu, bias=A("bdown")).then_inc(s_xm, 1)
            act.wait_ge(s_ang, 2)
            for n in range(2):
                act.activation(turns[:, n, :], turns[:, n, :], ACT.Sin).then_inc(s_sin, 1)
            act.wait_ge(s_hz, 5)
            act.activation(alpha[:, 0:1], A("gate1"), ACT.Sigmoid).then_inc(s_al, 1)
            act.activation(negA[:, :], A("alog"), ACT.Exp).then_inc(s_al, 1)

            with act.Fori(0, 2) as i:
                for n, (dst, c) in enumerate([(bcpad, None), (xpad, 0), (xpad, 1)]):
                    for h in range(2):
                        act.wait_ge(s_pr, 6 * i + 2 * n + h + 1)
                        src = bank(2 * n + h)[0:3 * DST] if c is None else bank(2 * n + h)
                        out = bcpad[:, 16 * h:16 * h + 16, DCONV - 1:] if c is None else \
                            xpad[:, c, 16 * h:16 * h + 16, DCONV - 1:]
                        act.activation(out, by_batch(src), ACT.Copy).then_inc(s_xp, 1)
                act.wait_ge(s_nv, i + 1)
                act.activation(dtv[:, 2, :], dtv[:, 1, :], ACT.Exp).then_inc(s_ey, 1)
                for n in range(4):
                    act.wait_ge(s_zp, 4 * i + n + 1)
                    act.activation(zs[:, n // 2, HALF * (n % 2):HALF * (n % 2) + HALF], bank(2 + n),
                                   ACT.Silu).then_inc(s_zs, 1)
                act.wait_ge(s_cv, 3 * i + 1)
                act.activation(Bt[:, :], cacc[0:DST, 2, :], ACT.Silu, bias=A("convbbc", DST)).then_inc(s_xs, 1)
                act.activation(Ct[:, 1:TOK + 1], cacc[2 * DST:3 * DST, 2, :], ACT.Silu,
                               bias=A("convbbc", DST, 2 * DST)).then_inc(s_xs, 1)
                for h in range(2):
                    act.wait_ge(s_seg, 2 * i + h + 1)
                    act.activation(E[:, 16 * h:16 * h + 16, :], by_batch(bank(h)), ACT.Exp).then_inc(s_E, 1)
                for c in range(2):
                    act.wait_ge(s_cv, 3 * i + c + 2)
                    act.activation(xs[:, c, :], cacc[:, c, :], ACT.Silu, bias=A("convbx")[:, c:c + 1]).then_inc(s_xs, 1)
                for n in range(4):
                    act.wait_ge(s_xt, 4 * i + n + 1)
                    act.activation(xtok[:, 4 * (n % 2):4 * (n % 2) + 4, P * (n // 2):P * (n // 2) + P],
                                   bank(2 + n % 2).rearrange("p (a c) -> p a c", a=4), ACT.Copy).then_inc(s_xe, 1)
                act.wait_ge(s_yz, 4 * i + 4)
                for c in range(2):
                    act.activation(cacc[:, c, :], yb[:, c, :], ACT.Square).then_inc(s_ysq, 1)
                for h in range(2):
                    act.wait_ge(s_rr, 2 * i + h + 1)
                    act.activation(rb[:, h, :], rb[:, h, :], ACT.Sqrt).then_inc(s_rb, 1)

            def key_root(n):
                act.wait_ge(s_kr1, n + 1)
                act.activation(rk[n % 2], rk[n % 2], ACT.Sqrt).then_inc(s_kr2, 1)

            for n in range(KTILES):
                act.wait_ge(s_pj, n + 1)
                if n >= 2:
                    act.wait_ge(s_ss, n - 1)
                act.activation(ksq[n % 2], bank(n % 4), ACT.Square).then_inc(s_sq, 1)
                if n >= 1:
                    key_root(n - 1)
            key_root(KTILES - 1)
            act.wait_ge(s_po, KTILES)
            for n in range(VTILES):
                act.wait_ge(s_pj, KTILES + n + 1)
                if n >= 4 and n % 2 == 0:
                    act.wait_ge(s_vst[n // 2 % 2], 16 * (n // 4))
                act.activation(vo[:, n // 2 % 2, HALF * (n % 2):HALF * (n % 2) + HALF], bank(n % 4),
                               ACT.Copy).then_inc(s_ve, 1)
            act.wait_ge(s_kst, 32)
            with act.Fori(0, 2) as i:
                for n in range(QTILES):
                    m, r = n // 4, n % 4
                    act.wait_ge(s_pj, KTILES + VTILES + QTILES * i + n + 1)
                    if r == 0:
                        act.wait_ge(s_ss, KTILES + 8 * i + m - 1)
                    act.activation(sqr[m % 2][:, :, r, :], by_batch(bank(n % 4)), ACT.Square).then_inc(s_sq, 1)
            act.wait_ge(s_rqa, 1)
            act.activation(rq[:, :], rq[:, :], ACT.Sqrt).then_inc(s_rqb, 1)

            def exponentials(n, col, slot):
                act.wait_ge(s_nb, n + 1)
                act.activation(prob[:, slot, :], prob[:, slot, :], ACT.Exp, bias=nb[:, slot:slot + 1],
                               scale=rq[:, col], accum_out=rs[:, slot:slot + 1]).then_inc(s_ex, 1)


            for n in range(3):
                exponentials(n, slice(n, n + 1), n)

            def act_turn(i):
                for j in range(16):
                    n = 16 * i + j
                    act.wait_ge(s_tp, n + 1)
                    after(act, s_pv, n - 1)
                    act.activation(pT4[:, j % 2, :], bank(6 + j % 2)[0:S, P:2 * P], ACT.Copy).then_inc(s_p4, 1)
                    if not (isinstance(i, int) and n == 0):
                        jj = (j - 1) % 16
                        act.wait_ge(s_pv, n)
                        if jj % 8 == 0:
                            turn = i if j > 0 else i - 1
                            after(act, s_ost[jj // 8], 16 * turn)
                        act.activation(oring[:, jj // 8, P * (jj % 8):P * (jj % 8) + P], bank(6 + jj % 2)[:, 0:P],
                                       ACT.Copy).then_inc(s_ov, 1)
                    if not (isinstance(i, int) and n + 3 >= UNITS):
                        exponentials(n + 3, ds(n + 3, 1) if not isinstance(i, int) else slice(n + 3, n + 4), (j + 3) % 4)

            act_turn(0)
            with act.Fori(1, 15) as i:
                act_turn(i)
            act_turn(15)
            act.wait_ge(s_pv, UNITS)
            act.activation(oring[:, 1, P * 7:P * 8], bank(7)[:, 0:P], ACT.Copy).then_inc(s_ov, 1)

            act.wait_ge(s_ost[0], 16 * B // 2)
            act.wait_ge(s_ost[1], 16 * B // 2)
            for n in range(TILES):
                act.wait_ge(s_hp, n + 1)
                act.activation(htok[:, n, :], bank(n % 2), ACT.Copy).then_inc(s_ht, 1)
            act.wait_ge(s_fp, 1)
            act.activation(rkT[:, :], bank(4)[0:RDIM, 0:NSLOT], ACT.Copy).then_inc(s_fe, 1)
            act.wait_ge(s_fp, 2)
            act.activation(AV[:, :], bank(5)[:, 0:VB], ACT.Copy).then_inc(s_fe, 1)
            for h in range(2):
                act.wait_ge(s_fp, 3 + h)
                act.activation(queryT[:, HALF * h:HALF * h + HALF], bank(h)[0:BOT], ACT.Copy).then_inc(s_fe, 1)
            for h in range(2):
                act.wait_ge(s_fp, 5 + h)
                act.activation(rqT[:, HALF * h:HALF * h + HALF], bank(2 + h)[0:RDIM], ACT.Copy).then_inc(s_fe, 1)
            for h in range(2):
                act.wait_ge(s_fp, 7 + h)
                act.activation(uT[:, HALF * h:HALF * h + HALF], bank(6 + h), ACT.Gelu_apprx_tanh,
                               bias=G("fbu1")).then_inc(s_fe, 1)
            act.wait_ge(s_bn, TILES)
            act.activation(sm[:, 0, :], mv[:, :, 1], ACT.Ln, bias=1.0, accum_out=lsum[:, 0:1]).then_inc(s_lv, 1)
            act.wait_ge(s_ler, 1)
            act.activation(sm[:, 1, :], bank(6)[:, 0:TILES], ACT.Sigmoid, bias=G("fbu2")).then_inc(s_sg, 1)
            act.wait_ge(s_ga, 1)
            act.activation(sm[:, 4, :], sm[:, 3, :], ACT.Sigmoid, bias=G("fgb"), scale=G("fgw")).then_inc(s_gb, 1)
            act.wait_ge(s_am, 1)
            for n in range(TILES):
                act.activation(asc[:, n, :], asc[:, n, :], ACT.Exp, bias=amx[:, n:n + 1],
                               accum_out=wsum[:, n:n + 1]).then_inc(s_exw, 1)
            for n in range(2):
                act.wait_ge(s_wt, n + 1)
                act.activation(wTs[:, HALF * n:HALF * n + HALF], bank(2 + n), ACT.Copy).then_inc(s_wte, 1)
            for h in range(2):
                act.wait_ge(s_ax, h + 1)
                act.activation(auxT[:, HALF * h:HALF * h + HALF], bank(h)[0:VB], ACT.Copy).then_inc(s_axe, 1)

        @block.vector
        def _(dve):
            done = [0]

            def prep(ins):
                done[0] += 1
                ins.then_inc(s_prep, 1)
                dve.wait_ge(s_prep, done[0])

            dve.wait_ge(s_ids, 16)
            prep(dve.tensor_copy(intf[:, :], ints[:, :]))
            dve.wait_ge(s_pka, 16)
            dve.tensor_scalar(onehot[:, :], intf[0:SESS, 0:B], A("sessidx", SESS), None, ALU.is_equal).then_inc(s_masks, 1)
            for j in range(2):
                dve.tensor_scalar(cmask[S * j:S * j + S, :], intf[S * j:S * j + S, B + j:2 * B:2],
                                  A("chan", S, S * j), None, ALU.is_gt).then_inc(s_prep, 1)
            for k in range(KC):
                dve.tensor_scalar(tmask[:, k, :], intf[:, 2 * B:3 * B], A("tcol")[:, k:k + 1], None,
                                  ALU.is_gt).then_inc(s_prep, 1)
            done[0] += 2 + KC
            dve.wait_ge(s_prep, done[0])
            dve.wait_ge(s_bias, 1)
            for j in range(2):
                dve.tensor_copy(bias1[CHID * j:CHID * j + CHID, :], bank(7)[CHID * j:CHID * j + CHID, j:B:2]).then_inc(s_prep, 1)
            done[0] += 2
            dve.wait_ge(s_prep, done[0])
            dve.wait_ge(s_gather, 16 * B)

            with dve.Fori(0, 2) as h:
                for p in range(8):
                    n = 8 * h + p
                    if p >= 2:
                        dve.wait_ge(s_h1, n - 1)
                    dve.tensor_scalar(wst[:, p % 2, :], wgat[:, ds(n, 1), :].rearrange("p a n -> p (a n)"),
                                      cmask[:, ds(n, 1)], None, ALU.mult).then_inc(s_wst, 1)
                for k in range(KC):
                    dve.wait_ge(s_co, 8 * KC * h + 7 * KC + k + 1)
                    out = condT[:, k, ds(HALF * h, HALF)].rearrange("p (b s) -> p b s", s=S)
                    dve.tensor_tensor(out, by_batch(bank(2 + k)), bc(A("b2"), 1, [P, 16, S]), ALU.add).then_inc(s_ca, 1)
                    dve.wait_ge(s_ca, KC * h + k + 1)
                    dve.tensor_tensor(out, out, bc(tmask[:, k, ds(16 * h, 16)], 2, [P, 16, S]),
                                      ALU.mult).then_inc(s_cT, 1)

            prep(dve.tensor_tensor(by_batch(ang[:, :]), bc(intf[:, 3 * B:4 * B], 2, [P, B, S]),
                                   bc(A("srow"), 1, [P, B, S]), ALU.add))
            prep(dve.tensor_scalar(ang[:, :], ang[:, :], A("invf"), None, ALU.mult))
            for n in range(2):
                tn = turns[:, n, :]
                count = condT[:, n, :]
                if n == 0:
                    dve.wait_ge(s_xc, 2 * KC)
                    dve.wait_ge(s_dn, 2)
                prep(dve.tensor_scalar(count, ang[:, :], float(1 / (2 * np.pi)), 0.25 * n, ALU.mult, ALU.add))
                prep(dve.tensor_scalar(count, count, ROUND, ROUND, ALU.add, ALU.subtract))
                prep(dve.scalar_tensor_tensor(out=tn, in0=count, scalar=-PI2_A, in1=ang[:, :], op0=ALU.mult, op1=ALU.add))
                prep(dve.scalar_tensor_tensor(out=tn, in0=count, scalar=-PI2_B, in1=tn, op0=ALU.mult, op1=ALU.add))
                prep(dve.scalar_tensor_tensor(out=tn, in0=count, scalar=-PI2_C, in1=tn, op0=ALU.mult, op1=ALU.add))
                if n == 1:
                    prep(dve.tensor_scalar(tn, tn, float(np.pi / 2), None, ALU.add))
                dve.tensor_scalar(tn, tn, PI, -PI, ALU.min, ALU.max).then_inc(s_ang, 1)
            for n in range(4):
                sine = n % 2
                dve.wait_ge(s_sin, 2 - sine)
                dve.tensor_scalar(tabs[:, n, :], turns[:, 1 - sine, :], A("qnw") if n < 2 else A("knw"),
                                  A("sign") if sine else 1.0, ALU.mult, ALU.mult).then_inc(s_tab, 1)

            dve.wait_ge(s_xm, 2)
            dve.wait_ge(s_al, 2)
            prep(dve.tensor_scalar(negA[:, :], negA[:, :], -1.0, None, ALU.mult))
            prep(dve.tensor_scalar(alpha[:, 1:2], alpha[:, 0:1], 1.0, None, ALU.add))
            prep(dve.tensor_scalar(alpha[:, 2:3], alpha[:, 0:1], -1.0, 1.0, ALU.mult, ALU.add))
            for c in range(2):
                prep(dve.tensor_scalar(outw[:, c, :], A("outw")[:, DM * c:DM * c + DM], A("normw")[:, c:c + 1],
                                       None, ALU.mult))
            dve.wait_ge(s_hz, 5)
            dve.tensor_copy(u[:, :], xmid[:, :]).then_inc(s_u, 1)

            ta = "p (a h) -> p a h"
            with dve.Fori(0, 2) as i:
                steps = [0]

                def step(ins):
                    steps[0] += 1
                    ins.then_inc(s_hd, 1)
                    dve.wait_ge(s_hd, NCHAIN * i + steps[0])

                dve.wait_ge(s_dtp, i + 1)
                step(dve.tensor_tensor(dtv[:, 0, :].rearrange(ta, h=8), bank(6)[:, 0:8 * TILES].rearrange(ta, h=8),
                                       bc(A("dtb"), 1, [P, TILES, 8]), ALU.add))
                dve.scalar_tensor_tensor(out=dtv[:, 1, :], in0=dtv[:, 0, :], scalar=-1.0, in1=dtv[:, 0, :],
                                         op0=ALU.mult, op1=ALU.min).then_inc(s_nv, 1)

                def convolve(src, w, dst):
                    out = dst.rearrange("p (a s) -> p a s", s=S)
                    step(dve.tensor_scalar(out, src[:, :, 0:S], w[:, 0:1], None, ALU.mult))
                    for k in range(1, DCONV):
                        ins = dve.scalar_tensor_tensor(out=out, in0=src[:, :, k:k + S], scalar=w[:, k:k + 1],
                                                       in1=out, op0=ALU.mult, op1=ALU.add)
                        if k < DCONV - 1:
                            step(ins)
                    ins.then_inc(s_cv, 1)

                dve.wait_ge(s_xp, 6 * i + 2)
                convolve(bcpad, A("convbc", 3 * DST), cacc[0:3 * DST, 2, :])

                dve.wait_ge(s_ey, i + 1)
                y, z, z2, p = dtv[:, 2, :], dtv[:, 3, :], dtv[:, 4, :], dtv[:, 1, :]
                step(dve.tensor_scalar(z, y, 2.0, None, ALU.add))
                step(dve.reciprocal(z, z))
                step(dve.tensor_tensor(z, z, y, ALU.mult))
                step(dve.tensor_tensor(z2, z, z, ALU.mult))
                step(dve.tensor_scalar(p, z2, 1.0 / 15, None, ALU.mult))
                for c in (13, 11, 9, 7, 5, 3):
                    step(dve.scalar_tensor_tensor(out=p, in0=p, scalar=1.0 / c, in1=z2, op0=ALU.add, op1=ALU.mult))
                step(dve.scalar_tensor_tensor(out=p, in0=p, scalar=1.0, in1=z, op0=ALU.add, op1=ALU.mult))
                step(dve.tensor_scalar(y, dtv[:, 0, :], 0.0, None, ALU.max))
                step(dve.scalar_tensor_tensor(out=y, in0=p, scalar=2.0, in1=y, op0=ALU.mult, op1=ALU.add))
                y8 = y.rearrange(ta, h=8)
                for d in range(2):
                    step(dve.tensor_copy(dtd[:, d, :].rearrange(ta, h=NH), y8[:, :, NH * d:NH * d + NH]))
                    step(dve.tensor_tensor(dtd[:, 2 + d, :].rearrange(ta, h=NH), y8[:, :, NH * d:NH * d + NH],
                                           bc(negA[:, :], 1, [P, TILES, NH]), ALU.mult))
                for d, side in enumerate(("before", "after")):
                    dve.tensor_tensor(Rm[:, d], bc(dtd[:, 2 + d, :], 2, [P, TILES * NH, S]),
                                      bc(A(side), 1, [P, TILES * NH, S]), ALU.mult).then_inc(s_R, 1)

                dve.wait_ge(s_xp, 6 * i + 4)
                convolve(xpad[:, 0], A("convx")[:, 0:DCONV], cacc[:, 0, :])

                for d, side in enumerate(("before", "after")):
                    for m in range(2):
                        dve.wait_ge(s_GG, 4 * i + 2 * d + m + 1)
                        src = bank((6, 4)[d] + m).rearrange("p (a c) -> p a c", a=4)
                        for q in range(BPT):
                            lo = S * q
                            dve.tensor_tensor(W12[lo:lo + S, d, 4 * m:4 * m + 4, :], src[lo:lo + S, :, lo:lo + S],
                                              bc(A(side, S, lo), 1, [S, 4, S]), ALU.mult).then_inc(s_W, 1)

                dve.wait_ge(s_xp, 6 * i + 6)
                convolve(xpad[:, 1], A("convx")[:, DCONV:2 * DCONV], cacc[:, 1, :])

                dve.wait_ge(s_W, 16 * i + 16)
                dve.wait_ge(s_seg, 2 * i + 2)
                dve.tensor_tensor(T12[:, 0].rearrange("p (a h) s -> p a h s", h=NH),
                                  bc(W12[:, 0], 2, [P, TILES, NH, S]),
                                  bc(dtd[:, 0].rearrange(ta, h=NH), 3, [P, TILES, NH, S]), ALU.mult).then_inc(s_T, 1)
                dve.wait_ge(s_T, 3 * i + 3)
                dve.wait_ge(s_E, 2 * i + 2)
                for q in range(BPT):
                    lo = S * q
                    dve.tensor_tensor(M[lo:lo + S, :, lo:lo + S], T12[lo:lo + S, 0], E[lo:lo + S], ALU.mult).then_inc(s_M, 1)
                for n in range(4):
                    c, h = n // 2, n % 2
                    sl = slice(HALF * h, HALF * h + HALF)
                    dve.wait_ge(s_r, 4 * i + n + 1)
                    dve.scalar_tensor_tensor(out=yb[:, c, sl], in0=bank(4 + n), scalar=A("dskip")[:, c:c + 1],
                                             in1=xs[:, c, sl], op0=ALU.add, op1=ALU.mult).then_inc(s_t, 1)
                for n in range(4):
                    c, h = n // 2, n % 2
                    sl = slice(HALF * h, HALF * h + HALF)
                    dve.wait_ge(s_y, 4 * i + n + 1)
                    dve.wait_ge(s_t, 4 * i + n + 1)
                    step(dve.tensor_tensor(yb[:, c, sl], bank(n), yb[:, c, sl], ALU.add))
                    dve.tensor_tensor(yb[:, c, sl], yb[:, c, sl], zs[:, c, sl], ALU.mult).then_inc(s_yz, 1)
                for h in range(2):
                    dve.wait_ge(s_ss0, 2 * i + h + 1)
                    step(dve.tensor_scalar(rb[:, h, :], bank(4 + h), 1.0 / DIN, EPS_HYDRA, ALU.mult, ALU.add))
                    dve.reciprocal(rb[:, h, :], rb[:, h, :]).then_inc(s_rr, 1)
                for h in range(2):
                    sl = slice(HALF * h, HALF * h + HALF)
                    dve.wait_ge(s_hy, 2 * i + h + 1)
                    dve.wait_ge(s_rb, 2 * i + h + 1)
                    ins = dve.tensor_tensor(u[:, sl], bank(6 + h), rb[:, h, :], ALU.mult)
                    if h == 0:
                        step(ins)
                ins.then_inc(s_u, 1)
                assert steps[0] == NCHAIN, steps
            dve.wait_ge(s_u, 3)
            prep(dve.tensor_scalar(u[:, :], u[:, :], alpha[:, 2:3], None, ALU.mult))
            dve.scalar_tensor_tensor(out=u[:, :], in0=xmid[:, :], scalar=alpha[:, 1:2], in1=u[:, :],
                                     op0=ALU.mult, op1=ALU.add).then_inc(s_hf, 1)
            for n in range(2 * KC):
                k, h = n // 2, n % 2
                sl = slice(HALF * h, HALF * h + HALF)
                dve.wait_ge(s_up, n + 1)
                if n == 0:
                    dve.wait_ge(s_xc, 2 * KC)
                dve.scalar_tensor_tensor(out=x2T[:, k, sl], in0=bank(n), scalar=A("bup")[:, k:k + 1],
                                         in1=x2T[:, k, sl], op0=ALU.add, op1=ALU.add).then_inc(s_x2, 1)

            def rotate(tile, slot, h, tab):
                sl = slice(HALF * h, HALF * h + HALF)
                dve.tensor_tensor(ab[:, slot, 0, :], tile, tabs[:, tab, sl], ALU.mult).then_inc(s_ab0, 1)
                dve.tensor_tensor(ab[0:64, slot, 1, :], tile[64:P], tabs[64:P, tab + 1, sl], ALU.mult).then_inc(s_ab0, 1)
                dve.tensor_tensor(ab[64:P, slot, 1, :], tile[0:64], tabs[0:64, tab + 1, sl], ALU.mult).then_inc(s_ab, 1)

            def key_mean(n):
                dve.wait_ge(s_ss, n + 1)
                prep(dve.tensor_scalar(rk[n % 2], bank(4 + n % 2), 1.0 / D, EPS_QK, ALU.mult, ALU.add))
                dve.reciprocal(rk[n % 2], rk[n % 2]).then_inc(s_kr1, 1)

            for n in range(KTILES):
                dve.wait_ge(s_sq, n + 1)
                if n >= 2:
                    dve.wait_ge(s_po, n - 1)
                rotate(bank(n % 4), n % 2, n // HK, 2)
                if n >= 1:
                    key_mean(n - 1)
            key_mean(KTILES - 1)
            with dve.Fori(0, 2) as i:
                for n in range(QTILES):
                    dve.wait_ge(s_sq, KTILES + QTILES * i + n + 1)
                    dve.wait_ge(s_po, KTILES + QTILES * i + n - 1)
                    rotate(bank(n % 4), n % 2, n // 4 % 2, 0)
            dve.wait_ge(s_ss, KTILES + 16)
            prep(dve.tensor_scalar(rq[:, :], bank(7)[:, 0:B * HK], 1.0 / D, EPS_QK, ALU.mult, ALU.add))
            dve.reciprocal(rq[:, :], rq[:, :]).then_inc(s_rqa, 1)
            dve.wait_ge(s_rqb, 1)
            prep(dve.tensor_scalar(nrq[:, :], rq[:, :], -SCALE, None, ALU.mult))
            dve.tensor_scalar(rq[:, :], rq[:, :], SCALE, None, ALU.mult).then_inc(s_rq, 1)

            def cached_mask(b):
                dve.tensor_scalar(mask[:, 0:LC], G("iota"), b, NEG, ALU.is_ge, ALU.mult).then_inc(s_msk, 1)

            def col(tensor, n):
                return tensor[:, n:n + 1] if isinstance(n, int) else tensor[:, ds(n, 1)]

            def masked_max(n, b, j):
                slot = j % 4
                if j % 8 == 0:
                    after(dve, s_mx, n)
                    cached_mask(col(intf, 3 * B + b))
                    dve.wait_ge(s_msk, b + 2)
                dve.wait_ge(s_sc, n + 1)
                after(dve, s_tp, n - 3)
                dve.sem_inc(s_seen, 1)
                dve.tensor_tensor_reduce(out=prob[:, slot, :], in0=score(j), in1=mask[:, :], scale=1.0,
                                         scalar=-3e38, op0=ALU.add, op1=ALU.max,
                                         accum_out=mx[:, slot:slot + 1]).then_inc(s_mx, 1)

            def exponent_bias(n, j):
                slot = j % 4
                dve.wait_ge(s_mx, n + 1)
                dve.tensor_tensor(nb[:, slot:slot + 1], mx[:, slot:slot + 1], col(nrq, n), ALU.mult).then_inc(s_nb, 1)

            def copy_page(par, n, page):
                dve.tensor_copy(kring[:, par, n, :], KT[:, ds(page * (HK * S), HK * S)]).then_inc(s_kc, 1)

            def inverse(n, j):
                dve.wait_ge(s_ex, n + 1)
                dve.reciprocal(ri[:, j % 4:j % 4 + 1], rs[:, j % 4:j % 4 + 1]).then_inc(s_rc, 1)

            dve.wait_ge(s_pkb, 16)
            dve.wait_ge(s_qst[0], 16 * (HK + 1))
            dve.wait_ge(s_qst[1], 16 * (HK + 1))
            dve.wait_ge(s_vst[0], 16 * TILES // 2)
            dve.wait_ge(s_vst[1], 16 * TILES // 2)
            dve.wait_ge(s_rq, 1)
            dve.memset(mask[:, LC:LK], 0.0).then_inc(s_msk, 1)
            dve.wait_ge(s_ids, 32)
            dve.wait_ge(s_KT, 16)
            for n in range(NPP):
                copy_page(0, n, page_number(dve, 0, n))
            for n in range(3):
                masked_max(n, 0, n)
                exponent_bias(n, n)
                for m in range(2 * n, 2 * n + 2):
                    copy_page(1, m, page_number(dve, 1, m))
            inverse(0, 0)
            inverse(1, 1)

            def dve_turn(i):
                for j in range(16):
                    n = 16 * i + j
                    b, lo = (j + 3) // 8 + 1, 2 * ((j + 3) % 8)
                    copies = not (isinstance(i, int) and 2 * i + b >= B)
                    dve.wait_ge(s_tp, n + 1)
                    after(dve, s_pv, n - 1)
                    dve.tensor_copy(pT[:, j % 2, :], bank(4 + j % 2)).then_inc(s_pt, 1)
                    if copies:
                        page0 = page_number(dve, 2 * i + b, lo)
                    if not (isinstance(i, int) and n + 2 >= UNITS):
                        inverse(n + 2, j + 2)
                    if not (isinstance(i, int) and n + 3 >= UNITS):
                        masked_max(n + 3, 2 * i + (j + 3) // 8, j + 3)
                        if copies:
                            page1 = page_number(dve, 2 * i + b, lo + 1)
                        exponent_bias(n + 3, j + 3)
                    if copies:
                        copy_page(b % 2, lo, page0)
                        copy_page(b % 2, lo + 1, page1)

            dve_turn(0)
            with dve.Fori(1, 15) as i:
                dve_turn(i)
            dve_turn(15)

            dve.wait_ge(s_pv, UNITS)
            dve.wait_ge(s_ost[0], 16 * B // 2)
            dve.wait_ge(s_ost[1], 16 * B // 2)
            def reorder(n):
                dve.wait_ge(s_oin[n % 2], 16 * (n // 2) + 16)
                if n >= 2:
                    dve.wait_ge(s_hp, n - 1)
                dve.tensor_copy(operm[:, n % 2], oins[n % 2][:, :, :].rearrange("p b (h s) -> p h b s", s=S)).then_inc(s_op, 1)

            reorder(0)
            for n in range(TILES + 1):
                if n + 1 < TILES:
                    reorder(n + 1)
                if n < TILES:
                    dve.wait_ge(s_ht, n + 1)
                    prep(dve.bn_stats(bn[:, n, :], htok[:, n, :]))
                    dve.bn_aggr(mv[:, n, :], bn[:, n, :]).then_inc(s_bn, 1)
                if n >= 1:
                    m = n - 1
                    dve.wait_ge(s_htt, m + 1)
                    dve.tensor_copy(hT[:, :, P * m:P * m + P],
                                    bank(2 + m % 2).rearrange("p (k c) -> p k c", k=KC)).then_inc(s_hT, 1)
            for n in range(TILES):
                q = P * (n % 4)
                dve.wait_ge(s_rsp, n // 4 + 1)
                dve.scalar_tensor_tensor(out=rsc[:, n, :], in0=bank(4 + n // 4)[:, q:q + P], scalar=float(1 / np.sqrt(RDIM)),
                                         in1=G("flog"), op0=ALU.mult, op1=ALU.add).then_inc(s_rse, 1)
            for n in range(TILES):
                dve.wait_ge(s_rse, n + 1)
                prep(dve.max(top8[:, n, :], rsc[:, n, :]))
                dve.match_replace(out=rep8[:, n, :], in_to_replace=top8[:, n, :], in_values=rsc[:, n, :],
                                  imm_value=-3e38).then_inc(s_rse, 1)
            for n in range(TILES):
                q = P * (n % 4)
                dve.wait_ge(s_asp, n // 4 + 1)
                dve.scalar_tensor_tensor(out=asc[:, n, :], in0=bank(n // 4)[:, q:q + P], scalar=float(1 / np.sqrt(BOT)),
                                         in1=G("flog"), op0=ALU.mult, op1=ALU.add).then_inc(s_ase, 1)
            dve.wait_ge(s_rse, 2 * TILES)
            dve.wait_ge(s_ase, TILES)
            prep(dve.tensor_tensor(rep8[:, :, :], rsc[:, :, :], rep8[:, :, :], ALU.not_equal))
            prep(dve.tensor_tensor(asc[:, :, :], asc[:, :, :], rep8[:, :, :], ALU.mult))
            prep(dve.tensor_scalar(rep8[:, :, :], rep8[:, :, :], -NEG, NEG, ALU.mult, ALU.add))
            prep(dve.tensor_tensor(asc[:, :, :], asc[:, :, :], rep8[:, :, :], ALU.add))
            prep(dve.tensor_reduce(amx[:, :], asc[:, :, :], AXX, ALU.max))
            dve.tensor_scalar(amx[:, :], amx[:, :], -1.0, None, ALU.mult).then_inc(s_am, 1)
            dve.wait_ge(s_mean, 1)
            prep(dve.tensor_scalar(lsum[:, 1:2], bank(7)[:, 0:1], 1.0 / TOK, 1e-6, ALU.mult, ALU.add))
            prep(dve.reciprocal(lsum[:, 1:2], lsum[:, 1:2]))
            prep(dve.tensor_scalar(sm[:, 2, :], sm[:, 0, :], lsum[:, 1:2], 0.5, ALU.mult, ALU.mult))
            dve.wait_ge(s_sg, 1)
            prep(dve.scalar_tensor_tensor(out=sm[:, 3, :], in0=sm[:, 1, :], scalar=2.5, in1=sm[:, 2, :],
                                          op0=ALU.mult, op1=ALU.add))
            prep(dve.tensor_scalar(sm[:, 3, :], sm[:, 3, :], 0.0, 5.0, ALU.max, ALU.min))
            prep(dve.tensor_scalar(sm[:, 3, :], sm[:, 3, :], 0.5, 1.0 / 1.5, ALU.subtract, ALU.mult))
            dve.tensor_scalar(sm[:, 3, :], sm[:, 3, :], 0.0, 1.0, ALU.max, ALU.min).then_inc(s_ga, 1)
            dve.wait_ge(s_gb, 1)
            prep(dve.scalar_tensor_tensor(out=sm[:, 5, :], in0=sm[:, 4, :], scalar=0.05, in1=sm[:, 4, :],
                                          op0=ALU.is_ge, op1=ALU.mult))
            dve.wait_ge(s_exw, TILES)
            prep(dve.reciprocal(sm[:, 6, :], wsum[:, :]))
            prep(dve.tensor_tensor(sm[:, 7, :], sm[:, 6, :], sm[:, 5, :], ALU.mult))
            for n in range(TILES):
                dve.tensor_scalar(asc[:, n, :], asc[:, n, :], sm[:, 7, n:n + 1], None, ALU.mult).then_inc(s_w8, 1)
            dve.wait_ge(s_fa, 1)
            for n in range(2 * KC):
                m, h = n // 2, n % 2
                sl = slice(HALF * h, HALF * h + HALF)
                dve.wait_ge(s_fo, n + 1)
                dve.tensor_tensor(hT[:, m, sl], bank(4 + n % 4), x2T[:, m, sl], ALU.add).then_inc(s_fin, 1)

        @block.tensor
        def _(pe):
            pe.wait_ge(s_masks, 1)
            pe.matmul(bank(7)[:, 0:B], lhsT=A("bsess", SESS), rhs=onehot[:, :], start=True, stop=True).then_inc(s_bias, 1)
            for j in range(2):
                pe.wait_ge(s_x, 32)

            def encoder_out(n, p):
                pe.wait_ge(s_g1, n + 1)
                for k in range(KC):
                    pe.matmul(bank(2 + k)[:, 2 * S * p:2 * S * p + 2 * S], lhsT=hbuf[:, p % 2, P * k:P * k + P],
                              rhs=A("w2"), start=True, stop=True).then_inc(s_co, 1)

            def encoder_half(h):
                for p in range(8):
                    n = 8 * h + p
                    pe.wait_ge(s_wst, n + 1)
                    if p >= 2:
                        pe.wait_ge(s_g1, n - 1)
                    pe.matmul(bank(p % 2), lhsT=wst[:, p % 2, :], rhs=xc[:, ds(n, 1), :].rearrange("p a n -> p (a n)"),
                              start=True, stop=True).then_inc(s_h1, 1)
                    if p >= 1:
                        encoder_out(n - 1, p - 1)
                encoder_out(8 * h + 7, 7)
                pe.wait_ge(s_cT, KC * h + KC)
                for k in range(KC):
                    mm = pe.matmul(bank(6), lhsT=A("wdown")[:, DM * k:DM * k + DM], rhs=condT[:, k, ds(HALF * h, HALF)],
                                   start=(k == 0), stop=(k == KC - 1))
                mm.then_inc(s_dn, 1)

            with pe.Fori(0, 2) as h:
                encoder_half(h)

            pe.wait_ge(s_pkb, 16)
            with pe.Fori(0, 2) as i:
                pe.wait_ge(s_u, i + 1)
                for n, w in enumerate([A("bcw"), A("xw")[:, 0:P], A("xw")[:, P:DIN]]):
                    rows = w.shape[1]
                    for h in range(2):
                        pe.matmul(bank(2 * n + h)[0:rows], lhsT=w, rhs=u[:, HALF * h:HALF * h + HALF],
                                  start=True, stop=True).then_inc(s_pr, 1)
                    if n == 0:
                        for m in range(TILES):
                            mm = pe.matmul(bank(6)[:, 8 * m:8 * m + 8], lhsT=u[:, P * m:P * m + P], rhs=A("dtw"),
                                           start=True, stop=True)
                        mm.then_inc(s_dtp, 1)
                for n in range(4):
                    pe.wait_ge(s_xp, 6 * i + n + 3)
                    c, h = n // 2, n % 2
                    pe.matmul(bank(2 + n), lhsT=A("zw")[:, P * c:P * c + P], rhs=u[:, HALF * h:HALF * h + HALF],
                              start=True, stop=True).then_inc(s_zp, 1)
                pe.wait_ge(s_R, 2 * i + 2)
                pe.wait_ge(s_xp, 6 * i + 2)
                for h in range(2):
                    for d, side in enumerate(("ufw", "ubw")):
                        mm = pe.matmul(bank(h), lhsT=A(side), rhs=Rm[:, d, 16 * h:16 * h + 16, :].rearrange("p a s -> p (a s)"),
                                       start=(d == 0), stop=(d == 1))
                    mm.then_inc(s_seg, 1)
                pe.wait_ge(s_xs, 4 * i + 2)
                pe.wait_ge(s_nv, i + 1)
                pe.wait_ge(s_zs, 4 * i + 4)
                for d in range(2):
                    for m in range(TILES):
                        mm = pe.matmul(bank((6, 4)[d] + m // 4)[:, P * (m % 4):P * (m % 4) + P], lhsT=Bt[:, P * m:P * m + P],
                                       rhs=Ct[:, P * m + 2 * d:P * m + 2 * d + P], start=True, stop=True)
                        if m % 4 == 3:
                            mm.then_inc(s_GG, 1)
                for n in range(4):
                    c, h = n // 2, n % 2
                    pe.wait_ge(s_xs, 4 * i + c + 3)
                    if n >= 2:
                        pe.wait_ge(s_xe, 4 * i + n - 1)
                    for m in range(4):
                        mm = pe.transpose(bank(2 + h)[:, P * m:P * m + P], xs[:, c, HALF * h + P * m:HALF * h + P * m + P],
                                          G("ident"))
                    mm.then_inc(s_xt, 1)
                pe.wait_ge(s_W, 16 * i + 16)
                for n in range(4):
                    c, h = n // 2, n % 2
                    for k in range(2):
                        mm = pe.matmul(bank(4 + n), lhsT=A("fcd")[:, DIN * k + P * c:DIN * k + P * c + P],
                                       rhs=xs[:, k, HALF * h:HALF * h + HALF], start=(k == 0), stop=(k == 1))
                    mm.then_inc(s_r, 1)
                pe.wait_ge(s_M, 4 * i + 4)
                pe.wait_ge(s_xe, 4 * i + 4)
                for n in range(4):
                    c, h = n // 2, n % 2
                    for m in range(4):
                        for q in range(2):
                            tile, head = 4 * h + m, 2 * c + q
                            mm = pe.matmul(bank(n)[64 * q:64 * q + 64, P * m:P * m + P],
                                           lhsT=xtok[:, tile, 64 * head:64 * head + 64], rhs=M[:, NH * tile + head, :],
                                           start=True, stop=True)
                    mm.then_inc(s_y, 1)
                pe.wait_ge(s_ysq, 2 * i + 2)
                pe.wait_ge(s_t, 4 * i + 4)
                for h in range(2):
                    for c in range(2):
                        mm = pe.matmul(bank(4 + h), lhsT=ones[:, :], rhs=cacc[:, c, HALF * h:HALF * h + HALF],
                                       start=(c == 0), stop=(c == 1))
                    mm.then_inc(s_ss0, 1)
                for h in range(2):
                    for c in range(2):
                        mm = pe.matmul(bank(6 + h), lhsT=outw[:, c, :], rhs=yb[:, c, HALF * h:HALF * h + HALF],
                                       start=(c == 0), stop=(c == 1))
                    mm.then_inc(s_hy, 1)
            pe.wait_ge(s_hf, 1)
            for n in range(2 * KC):
                k, h = n // 2, n % 2
                pe.matmul(bank(n), lhsT=A("wup")[:, P * k:P * k + P],
                          rhs=u[:, :].rearrange("p (s b) -> p b s", b=B)[:, 16 * h:16 * h + 16, :],
                          start=True, stop=True).then_inc(s_up, 1)

            def project(out, w, x):
                for k in range(KC):
                    mm = pe.matmul(out, lhsT=w(k), rhs=x(k), start=(k == 0), stop=(k == KC - 1))
                mm.then_inc(s_pj, 1)

            def key_squares(n):
                pe.wait_ge(s_sq, n + 1)
                if n >= 2:
                    pe.wait_ge(s_kr1, n - 1)
                pe.matmul(bank(4 + n % 2), lhsT=ones[:, :], rhs=ksq[n % 2], start=True, stop=True).then_inc(s_ss, 1)

            pe.wait_ge(s_w[0], 16)
            pe.wait_ge(s_x2, 2 * KC)
            for n in range(KTILES):
                h, g = n // HK, n % HK
                if n >= 4:
                    pe.wait_ge(s_sq, n - 3)
                    pe.wait_ge(s_ab, n - 3)
                project(bank(n % 4), lambda k: wring[:, 0, k, P * g:P * g + P], lambda k: x2T[:, k, HALF * h:HALF * h + HALF])
                if n >= 1:
                    key_squares(n - 1)
            key_squares(KTILES - 1)
            pe.wait_ge(s_w[1], 16)
            for n in range(VTILES):
                m, h = n // 2, n % 2
                if n < 4:
                    pe.wait_ge(s_sq, KTILES - 3 + n)
                    pe.wait_ge(s_ab, KTILES - 3 + n)
                else:
                    pe.wait_ge(s_ve, n - 3)
                project(bank(n % 4), lambda k: x2T[:, k, P * m:P * m + P], lambda k: wring[:, 1, k, HALF * h:HALF * h + HALF])
            pe.wait_ge(s_ve, VTILES)

            def query_squares(i, m):
                g, h = 4 * i + m // 2, m % 2
                pe.wait_ge(s_sq, KTILES + QTILES * i + 4 * m + 4)
                for b in range(16):
                    mm = pe.matmul(bank(7)[:, ds(4 * i + (HK * (16 * h + b) + m // 2), 1)],
                                   lhsT=sqr[h][:, b].rearrange("p r s -> p (r s)"), rhs=ones[:, 0:1], start=True, stop=True)
                mm.then_inc(s_ss, 1)

            with pe.Fori(0, 2) as i:
                for n in range(QTILES):
                    sl, m, r = n // 16, n // 4, n % 4
                    h = m % 2
                    if n % 16 == 0:
                        pe.wait_ge(s_w[sl], 16 * i + 32)
                    pe.wait_ge(s_sq, KTILES + QTILES * i + n - 3)
                    pe.wait_ge(s_ab, KTILES + QTILES * i + n - 3)
                    hd = REP * (m // 2 % 2) + r
                    project(bank(n % 4), lambda k: wring[:, sl, k, P * hd:P * hd + P], lambda k: x2T[:, k, HALF * h:HALF * h + HALF])
                    if r == 0 and m > 0:
                        query_squares(i, m - 1)
                query_squares(i, 7)

            def scores(n, b, j):
                par, g = j // 8 % 2, j % 8
                turn = b // 2 if isinstance(b, int) else None
                if g == 0:
                    pe.wait_ge(s_in[par], 32 * (b // 2) + 32 if isinstance(b, int) else 16 * b + 32 - 16 * par)
                    pe.wait_ge(s_kc, NPP * b + NPP)
                after(pe, s_mx, n - 1)
                q = qring[:, par, P * g:P * g + P]
                s = score(j)
                pe.matmul(s[:, 0:LC].rearrange("p (a c) -> p a c", c=S), lhsT=q,
                          rhs=kring[:, par, 0:NPP, S * g:S * g + S], start=True, stop=True)
                pe.matmul(s[:, LC:LK], lhsT=q, rhs=kring[:, par, NPP, S * g:S * g + S], start=True, stop=True).then_inc(s_sc, 1)

            def transposes(n, j):
                slot = j % 4
                pe.wait_ge(s_pn, n + 1)
                after(pe, s_pt, n - 1)
                after(pe, s_ov, n - 1)
                pe.transpose(bank(6 + j % 2)[0:S, P:2 * P], prob[:, slot, LC:LK], G("ident"))
                for c in range(BPT):
                    mm = pe.transpose(bank(4 + j % 2)[:, P * c:P * c + P], prob[:, slot, P * c:P * c + P], G("ident"))
                mm.then_inc(s_tp, 1)

            def weighted(n, b, j):
                par, g = j // 8 % 2, j % 8
                if g == 0:
                    per = 16 * (NPP + 1)
                    pe.wait_ge(s_v[par], per * (b // 2) + per if isinstance(b, int) else (per // 2) * b + per - (per // 2) * par)
                pe.wait_ge(s_pt, n + 1)
                pe.wait_ge(s_p4, n + 1)
                o = bank(6 + j % 2)[:, 0:P]
                for c in range(BPT):
                    pe.matmul(o, lhsT=vring[:, par, c, D * g:D * g + D], rhs=pT[:, j % 2, P * c:P * c + P],
                              start=(c == 0), stop=False)
                pe.matmul(o, lhsT=vring[0:S, par, BPT, D * g:D * g + D], rhs=pT4[:, j % 2, :],
                          start=False, stop=True).then_inc(s_pv, 1)

            for n in range(3):
                scores(n, 0, n)

            def pe_turn(i):
                for j in range(16):
                    n = 16 * i + j
                    first = isinstance(i, int) and n == 0
                    transposes(n, j)
                    if not first:
                        jj = (j - 1) % 16
                        weighted(n - 1, 2 * i + jj // 8 if j > 0 else 2 * i - 1, jj)
                    if not (isinstance(i, int) and n + 3 >= UNITS):
                        scores(n + 3, 2 * i + (j + 3) // 8, j + 3)

            pe_turn(0)
            with pe.Fori(1, 15) as i:
                pe_turn(i)
            pe_turn(15)
            weighted(UNITS - 1, B - 1, 15)

            pe.wait_ge(s_wo, 16)
            pe.wait_ge(s_ov, UNITS)
            pe.wait_ge(s_pt, UNITS)

            def turn_tokens(n):
                pe.wait_ge(s_ht, n + 1)
                if n >= 2:
                    pe.wait_ge(s_hT, n - 1)
                for k in range(KC):
                    mm = pe.transpose(bank(2 + n % 2)[:, P * k:P * k + P], htok[:, n, P * k:P * k + P], G("ident"))
                mm.then_inc(s_htt, 1)

            for n in range(TILES):
                pe.wait_ge(s_op, n + 1)
                if n >= 2:
                    pe.wait_ge(s_ht, n - 1)
                for h in range(HQ):
                    mm = pe.matmul(bank(n % 2), lhsT=operm[:, n % 2, h].rearrange("p b s -> p (b s)"), rhs=wo[:, h, :],
                                   start=(h == 0), stop=(h == HQ - 1))
                mm.then_inc(s_hp, 1)
                if n >= 1:
                    turn_tokens(n - 1)
            turn_tokens(TILES - 1)
            pe.matmul(bank(4)[0:RDIM, 0:NSLOT], lhsT=G("fwr", BOT), rhs=G("fkeys", BOT), start=True, stop=True).then_inc(s_fp, 1)
            for k in range(KC):
                mm = pe.matmul(bank(5)[:, 0:VB], lhsT=G("fval")[:, NSLOT * k:NSLOT * k + NSLOT], rhs=G("fwvd")[:, VB * k:VB * k + VB],
                               start=(k == 0), stop=(k == KC - 1))
            mm.then_inc(s_fp, 1)
            pe.wait_ge(s_hT, TILES)
            for h in range(2):
                for k in range(KC):
                    mm = pe.matmul(bank(h)[0:BOT], lhsT=G("fwq")[:, BOT * k:BOT * k + BOT], rhs=hT[:, k, HALF * h:HALF * h + HALF],
                                   start=(k == 0), stop=(k == KC - 1))
                mm.then_inc(s_fp, 1)
            for h in range(2):
                pe.wait_ge(s_fe, 3 + h)
                pe.matmul(bank(2 + h)[0:RDIM], lhsT=G("fwr", BOT), rhs=queryT[:, HALF * h:HALF * h + HALF],
                          start=True, stop=True).then_inc(s_fp, 1)
            for h in range(2):
                for k in range(KC):
                    mm = pe.matmul(bank(6 + h), lhsT=G("fwu1")[:, P * k:P * k + P], rhs=hT[:, k, HALF * h:HALF * h + HALF],
                                   start=(k == 0), stop=(k == KC - 1))
                mm.then_inc(s_fp, 1)
            for m in range(2):
                pe.wait_ge(s_fe, 5 + m)
                for n in range(4):
                    tile = 4 * m + n
                    mm = pe.matmul(bank(4 + m)[:, P * n:P * n + P], lhsT=rqT[:, P * tile:P * tile + P], rhs=rkT[:, :],
                                   start=True, stop=True)
                mm.then_inc(s_rsp, 1)
            for m in range(2):
                for n in range(4):
                    tile = 4 * m + n
                    mm = pe.matmul(bank(m)[:, P * n:P * n + P], lhsT=queryT[:, P * tile:P * tile + P], rhs=G("fkeys", BOT),
                                   start=True, stop=True)
                mm.then_inc(s_asp, 1)
            pe.wait_ge(s_fe, 8)
            for n in range(TILES):
                mm = pe.matmul(bank(6)[:, n:n + 1], lhsT=uT[:, P * n:P * n + P], rhs=G("fwu2"), start=True, stop=True)
            mm.then_inc(s_ler, 1)
            pe.wait_ge(s_lv, 1)
            pe.matmul(bank(7)[:, 0:1], lhsT=ones[:, :], rhs=lsum[:, 0:1], start=True, stop=True).then_inc(s_mean, 1)
            for m in range(2):
                for n in range(4):
                    tile = 4 * m + n
                    pe.wait_ge(s_w8, tile + 1)
                    mm = pe.transpose(bank(2 + m)[:, P * n:P * n + P], asc[:, tile, :], G("ident"))
                mm.then_inc(s_wt, 1)
            for h in range(2):
                pe.wait_ge(s_wte, h + 1)
                pe.matmul(bank(h)[0:VB], lhsT=AV[:, :], rhs=wTs[:, HALF * h:HALF * h + HALF], start=True, stop=True).then_inc(s_ax, 1)
            pe.wait_ge(s_axe, 2)
            pe.wait_ge(s_ga, 1)
            for n in range(2 * KC):
                m, h = n // 2, n % 2
                if n >= 4:
                    pe.wait_ge(s_fin, n - 3)
                pe.matmul(bank(4 + n % 4), lhsT=G("fwvu", VB)[:, P * m:P * m + P], rhs=auxT[:, HALF * h:HALF * h + HALF],
                          start=True, stop=True).then_inc(s_fo, 1)


def kernel(x, itok_B_0_7, itok_B_2182_4065, itok_Bx16_0_63, itok_B_207_1644, _lenS, L0_cond_W_sess, L0_cond_b_sess,
           L0_cond_W2, L0_cond_b2, L0_attn_w_down, L0_attn_b_down, L0_attn_w_up, L0_attn_b_up, L0_attn_gate1,
           L0_attn_hy_in_w, L0_attn_hy_conv_w, L0_attn_hy_conv_b, L0_attn_hy_dt_bias, L0_attn_hy_A_log, L0_attn_hy_D,
           L0_attn_hy_fcD_w, L0_attn_hy_norm_w, L0_attn_hy_out_w, L0_cond2_Wq, L0_cond2_Wk, L0_cond2_Wv, L0_cond2_Wo,
           L0_cond2_q_norm_w, L0_cond2_k_norm_w, L0_cond2_k_cache, L0_cond2_v_cache, L0_ffn_Wq, L0_ffn_Wr,
           L0_ffn_aux_keys, L0_ffn_aux_values, L0_ffn_Wvd, L0_ffn_Wvu, L0_ffn_Wu1, L0_ffn_bu1, L0_ffn_Wu2, L0_ffn_bu2,
           L0_ffn_gate_w1, L0_ffn_gate_bias, L0_ffn_log_rel):
    import concourse.bacc as bacc
    from concourse.bass_utils import run_bass_kernel_spmd

    f = np.float32

    def rows(a):
        a = np.asarray(a)
        return a.reshape(-1, P, a.shape[1]).transpose(1, 0, 2).reshape(P, -1)

    def every(a):
        a = np.asarray(a).reshape(1, -1)
        return np.broadcast_to(a, (P, a.shape[1]))

    def pack(cols, total, parts):
        out = np.zeros((P, total), f)
        for name, (at, n) in cols.items():
            a = np.asarray(parts[name])
            assert a.shape[1] == n, (name, a.shape, n)
            out[:a.shape[0], at:at + n] = a
        return out

    p = np.arange(P)
    conv = np.asarray(L0_attn_hy_conv_w)[:, 0, :]
    cb = np.asarray(L0_attn_hy_conv_b).reshape(-1, 1)
    inw = np.asarray(L0_attn_hy_in_w).T
    o = DIN

    def spread(a):
        out = np.zeros((3 * DST, a.shape[1]), f)
        out[0:DST], out[2 * DST:] = a[0:DST], a[DST:]
        return out

    same = p[:, None] // S == p[None, :] // S
    w2 = np.zeros((P, 2 * S), f)
    w2[0:CHID, 0:S] = w2[CHID:, S:] = np.asarray(L0_cond_W2)
    parts_a = {
        "sessidx": p[:, None], "chan": (p % S)[:, None], "tcol": p[:, None] + P * np.arange(KC)[None, :],
        "bsess": np.concatenate([np.asarray(L0_cond_b_sess)] * 2, 1), "w2": w2, "b2": every(L0_cond_b2),
        "wdown": rows(np.asarray(L0_attn_w_down).T), "bdown": np.asarray(L0_attn_b_down)[:, None],
        "srow": every(np.arange(S)),
        "invf": np.tile(1.0 / THETA ** (np.arange(0, D, 2, dtype=f) / D), 2)[:, None],
        "sign": np.where(p < 64, 1.0, -1.0)[:, None],
        "qnw": np.asarray(L0_cond2_q_norm_w)[:, None], "knw": np.asarray(L0_cond2_k_norm_w)[:, None],
        "zw": inw[:, 0:o], "xw": inw[:, o:2 * o], "bcw": spread(inw[:, 2 * o:2 * o + 2 * DST].T).T,
        "dtw": inw[:, 2 * o + 2 * DST:], "convx": rows(conv[0:o]), "convbc": spread(conv[o:]),
        "convbx": rows(cb[0:o]), "convbbc": spread(cb[o:]),
        "dtb": every(np.concatenate([np.asarray(L0_attn_hy_dt_bias)] * 2)), "alog": every(L0_attn_hy_A_log),
        "dskip": rows(np.repeat(np.asarray(L0_attn_hy_D), 64)[:, None]),
        "fcd": rows(np.repeat(np.asarray(L0_attn_hy_fcD_w), 64, axis=0).T),
        "normw": rows(np.asarray(L0_attn_hy_norm_w)[:, None]), "outw": rows(np.asarray(L0_attn_hy_out_w).T),
        "wup": np.asarray(L0_attn_w_up).T, "bup": rows(np.asarray(L0_attn_b_up)[:, None]),
        "gate1": every(L0_attn_gate1),
        "ufw": same & (p[:, None] > p[None, :]), "ubw": same & (p[:, None] < p[None, :]),
        "before": (p % S)[:, None] < np.arange(S)[None, :], "after": (p % S)[:, None] > np.arange(S)[None, :],
    }
    parts_b = {
        "ident": np.eye(P), "iota": every(np.arange(LC)),
        "fwq": rows(np.asarray(L0_ffn_Wq).T), "fwr": np.asarray(L0_ffn_Wr).T, "fkeys": np.asarray(L0_ffn_aux_keys).T,
        "flog": every(L0_ffn_log_rel), "fval": rows(np.asarray(L0_ffn_aux_values).T), "fwvd": rows(np.asarray(L0_ffn_Wvd).T),
        "fwvu": np.asarray(L0_ffn_Wvu).T, "fwu1": rows(np.asarray(L0_ffn_Wu1).T), "fbu1": np.asarray(L0_ffn_bu1)[:, None],
        "fwu2": np.asarray(L0_ffn_Wu2).T, "fbu2": every(L0_ffn_bu2), "fgw": every(L0_ffn_gate_w1),
        "fgb": every(L0_ffn_gate_bias),
    }
    xf = np.asarray(x)
    ints = np.concatenate([np.asarray(a) for a in (itok_B_0_7, _lenS, itok_B_2182_4065, itok_B_207_1644)])
    ins = {
        "x": xf, "xT": xf.reshape(TOK, HID).T, "ints": np.broadcast_to(ints[None, :], (P, INTS)),
        "table": np.asarray(itok_Bx16_0_63).reshape(1, -1), "wsess": np.asarray(L0_cond_W_sess),
        "packa": pack(COL_A, COLS_A, parts_a), "packb": pack(COL_B, COLS_B, parts_b),
        "wqT": np.asarray(L0_cond2_Wq).T, "wkT": np.asarray(L0_cond2_Wk).T, "wvT": np.asarray(L0_cond2_Wv).T,
        "woT": np.asarray(L0_cond2_Wo).T, "kcT": np.asarray(L0_cond2_k_cache).transpose(3, 0, 2, 1),
        "vc": np.asarray(L0_cond2_v_cache),
    }
    ins = {k: np.ascontiguousarray(v) for k, v in ins.items()}
    nc = bacc.Bacc("TRN2", target_bir_lowering=False, num_devices=1)
    t = {k: nc.dram_tensor(f"in_{k}", v.shape, mybir.dt.from_np(v.dtype), kind="ExternalInput").ap() for k, v in ins.items()}
    for k, shape in (("q_s", (B, D, HQ * S)), ("k_s", (B, D, HK * S)), ("v_s", (TOK, HK * D)), ("o_s", (B, D, HQ * S))):
        t[k] = nc.dram_tensor(k, shape, F32, kind="Internal").ap()
    t["out"] = nc.dram_tensor("out", (HID, TOK), F32, kind="ExternalOutput").ap()
    adaln_attention_ffn(nc, t)
    r = run_bass_kernel_spmd(nc, [{f"in_{k}": v for k, v in ins.items()}], core_ids=[0])
    return np.ascontiguousarray(r.results[0]["out"].T).reshape(B, S, HID)
```

```python
from contextlib import ExitStack

import numpy as np
import concourse.bass as bass
from concourse import mybir

F32 = mybir.dt.float32
F16 = mybir.dt.float16
I32 = mybir.dt.int32
ACT = mybir.ActivationFunctionType
ALU = mybir.AluOpType
AXX = mybir.AxisListType.X
ds = bass.ds

P = 128
B, S, HID = 32, 32, 512
TOK = B * S
HALF = TOK // 2
KC = HID // P
SESS, CHID = 8, 64
DM, DIN, DST, NH, DCONV = 128, 256, 16, 4, 7
PADL = S + DCONV - 1
D, HQ, HK = 128, 32, 8
REP = HQ // HK
PAGES, NPP = 64, 16
LC = NPP * S
LK = LC + S
BOT, RDIM, NSLOT, TOPK, VB = 64, 48, 128, 8, 32
SCALE = 1.0 / float(np.sqrt(D))
THETA = 10000.0
TILES = TOK // P
BPT = P // S

PACK_A = [
    ("sessidx", 1), ("chan", 1), ("tcol", KC), ("bsess", P), ("w2", 2 * S), ("b2", S),
    ("wdown", KC * DM), ("bdown", 1), ("srow", S), ("invf", 1), ("sign", 1), ("qnw", 1), ("knw", 1),
    ("dtw", 2 * NH), ("bcw", 3 * DST), ("xw", DIN), ("zw", DIN), ("convx", 2 * DCONV),
    ("convbc", DCONV), ("convbx", 2), ("convbbc", 1), ("dtb", 2 * NH), ("alog", NH), ("dskip", 2),
    ("fcd", 2 * DIN), ("normw", 2), ("outw", 2 * DM), ("wup", HID), ("bup", KC), ("gate1", 1),
    ("ufw", P), ("ubw", P), ("before", S), ("after", S),
]
PACK_B = [
    ("ident", P), ("iota", LC),
]
PACK_C = [
    ("fwq", KC * BOT), ("fwr", RDIM), ("fkeys", NSLOT), ("flog", NSLOT), ("fval", KC * NSLOT),
    ("fwvd", KC * VB), ("fwvu", HID), ("fwu1", KC * P), ("fbu1", 1), ("fwu2", 1), ("fbu2", 1),
    ("fgw", 1), ("fgb", 1),
]


def columns(pack):
    at, out = 0, {}
    for name, n in pack:
        out[name] = (at, n)
        at += n
    return out, at


COL_A, COLS_A = columns(PACK_A)
COL_B, COLS_B = columns(PACK_B)
COL_C, COLS_C = columns(PACK_C)

PI2_A, PI2_B = 6.28125, 0.0019350051879882812
PI2_C = float(2 * np.pi - PI2_A - PI2_B)
ROUND = 12582912.0
PI = 3.1415925
NEG = -1e30
EPS_HYDRA, EPS_QK = 1e-5, 1e-6
INTS = 4 * B
NPAIR = B // 2
NCHAIN = 44
KTILES, VTILES, QTILES = 16, 16, 16
WCOLS = 512
WTILES = 8
WSCALE = 256.0
QTURNS = 4
WSLOTS = [("wkT", n) for n in range(2)] + [("wvT", n) for n in range(2)] + [("wqT", n) for n in range(HK)]
UNITS = B * HK


def adaln_attention_ffn(nc, t):
    with ExitStack() as ctx:
        def sem(name):
            return ctx.enter_context(nc.semaphore(name))

        def sb(stack, name, shape, dt=F32):
            return stack.enter_context(nc.sbuf_tensor(name, shape, dt))

        psum = ctx.enter_context(nc.psum_tensor("psum", [P, 8, 512], F32))

        def bank(n):
            return psum[:, n, :]

        pkb = sb(ctx, "pkb", [P, COLS_B])
        x2T = sb(ctx, "x2T", [P, KC, TOK])
        ints = sb(ctx, "ints", [P, INTS], I32)
        intf = sb(ctx, "intf", [P, INTS])
        table = sb(ctx, "table", [1, B * NPP], I32)
        ones = sb(ctx, "ones", [P, P])
        mean_d = sb(ctx, "mean_d", [P, 1])
        eps_qk = sb(ctx, "eps_qk", [P, 1])
        rq = sb(ctx, "rq", [P, B * HK])
        nrq = sb(ctx, "nrq", [P, B * HK])
        with ExitStack() as c1:
            wland = sb(c1, "wland", [P, 2, KC, WCOLS])
            w16 = sb(c1, "w16", [P, 2, 2, KC, WCOLS], F16)
            tabs = sb(c1, "tabs", [P, 4, TOK])
            with ExitStack() as s1:
                pka = sb(s1, "pka", [P, COLS_A])
                xmid = sb(s1, "xmid", [P, TOK])
                u = sb(s1, "u", [P, TOK])
                with ExitStack() as st:
                    xc = sb(st, "xc", [2 * S, NPAIR, HID])
                    wgat = sb(st, "wgat", [2 * S, NPAIR, P])
                    wst = sb(st, "wst", [2 * S, 2, P])
                    cmask = sb(st, "cmask", [2 * S, NPAIR])
                    tmask = sb(st, "tmask", [P, KC, B])
                    onehot = sb(st, "onehot", [SESS, B])
                    bias1 = sb(st, "bias1", [P, NPAIR])
                    hbuf = sb(st, "hbuf", [P, 2, HID])
                    condT = sb(st, "condT", [P, KC, TOK])
                    ang = sb(st, "ang", [P, TOK])
                    turns = sb(st, "turns", [P, 2, TOK])
                with ExitStack() as st:
                    xpad = sb(st, "xpad", [P, 2, S, PADL])
                    bcpad = sb(st, "bcpad", [3 * DST, S, PADL])
                    cacc = sb(st, "cacc", [P, 3, TOK])
                    xs = sb(st, "xs", [P, 2, TOK])
                    Bt = sb(st, "Bt", [DST, TOK])
                    Ct = sb(st, "Ct", [DST, TOK + 2])
                    zs = sb(st, "zs", [P, 2, TOK])
                    xtok = sb(st, "xtok", [P, TILES, DIN])
                    dtv = sb(st, "dtv", [P, 5, TILES * 2 * NH])
                    dtd = sb(st, "dtd", [P, 4, TILES * NH])
                    negA = sb(st, "negA", [P, NH])
                    Rm = sb(st, "Rm", [P, 2, TILES * NH, S])
                    E = sb(st, "E", [P, TILES * NH, S])
                    W12 = sb(st, "W12", [P, 2, TILES, S])
                    M = sb(st, "M", [P, TILES * NH, P])
                    yb = sb(st, "yb", [P, 2, TOK])
                    rb = sb(st, "rb", [P, 2, HALF])
                    outw = sb(st, "outw", [P, 2, DM])
                    alpha = sb(st, "alpha", [P, 3])
            T12 = Rm
            with ExitStack() as st:
                KT = sb(st, "KT", [P, PAGES * HK * S])
                x16 = sb(st, "x16", [P, 2, KC, TOK], F16)
                stage = sb(st, "stage", [P, 4, REP * HALF])
                ab = sb(st, "ab", [P, 3, 2, HALF])
                kms = sb(st, "kms", [P, KTILES, 4])
                vo = sb(st, "vo", [P, 4, WCOLS])
        with ExitStack() as st:
            kring = sb(st, "kring", [P, 2, NPP + 1, HK * S])
            qring = sb(st, "qring", [P, 2, HQ * S])
            mask = sb(st, "mask", [P, LK])
            sb(st, "gap", [P, 4 * KC * WCOLS + 4 * TOK - 2 * (NPP + 1) * HK * S - 2 * HQ * S - LK])
            sb(st, "KT_place", [P, PAGES * HK * S])
            vring = sb(st, "vring", [P, 2, BPT + 1, HK * D])
            oring = sb(st, "oring", [P, 2, HQ * S])
            prob = sb(st, "prob", [P, 4, LK])
            pT = sb(st, "pT", [P, 2, LC])
            pT4 = sb(st, "pT4", [S, 2, P])
            mx = sb(st, "mx", [P, 4])
            nb = sb(st, "nb", [P, 4])
            rs = sb(st, "rs", [P, 4])
            ri = sb(st, "ri", [P, 4])
        wo = KT[:, :].rearrange("p (h n) -> p h n", h=HQ)
        with ExitStack() as st:
            oin = sb(st, "oin", [P, BPT, HQ * S])
            htok = sb(st, "htok", [P, TILES, HID])
            hT = sb(st, "hT", [P, KC, TOK])
            sb(st, "KT_place2", [P, PAGES * HK * S])
            bn = sb(st, "bn", [P, TILES, 6])
            mv = sb(st, "mv", [P, TILES, 2])
            pkc = sb(st, "pkc", [P, COLS_C])
            with ExitStack() as so:
                oin2 = sb(so, "oin2", [P, BPT, HQ * S])
                operm = sb(so, "operm", [P, 2, HQ, BPT, S])
            queryT = sb(st, "queryT", [BOT, TOK])
            rqT = sb(st, "rqT", [RDIM, TOK])
            rkT = sb(st, "rkT", [RDIM, NSLOT])
            AV = sb(st, "AV", [NSLOT, VB])
            uT = sb(st, "uT", [P, TOK])
            rsc = sb(st, "rsc", [P, TILES, NSLOT])
            rep8 = sb(st, "rep8", [P, TILES, NSLOT])
            asc = sb(st, "asc", [P, TILES, NSLOT])
            top8 = sb(st, "top8", [P, TILES, TOPK])
            amx = sb(st, "amx", [P, TILES])
            wsum = sb(st, "wsum", [P, TILES])
            sm = sb(st, "sm", [P, 10, TILES])
            lsum = sb(st, "lsum", [P, 2])
            wTs = sb(st, "wTs", [NSLOT, TOK])
            auxT = sb(st, "auxT", [VB, TOK])
        oins = [oin, oin2]

        def A(name, rows=P, lo=0):
            a, n = COL_A[name]
            return pka[lo:lo + rows, a:a + n]

        def G(name, rows=P, lo=0):
            a, n = COL_B[name]
            return pkb[lo:lo + rows, a:a + n]

        def C(name, rows=P, lo=0):
            a, n = COL_C[name]
            return pkc[lo:lo + rows, a:a + n]

        s_pka, s_pkb, s_x, s_ids, s_xT = sem("s_pka"), sem("s_pkb"), sem("s_x"), sem("s_ids"), sem("s_xT")
        s_wz, s_gather = sem("s_wz"), sem("s_gather")
        s_prep, s_bias = sem("s_prep"), sem("s_bias")
        s_masks = sem("s_masks")
        s_wst = sem("s_wst")
        s_h1, s_g1 = sem("s_h1"), sem("s_g1")
        s_co, s_ca, s_cT = sem("s_co"), sem("s_ca"), sem("s_cT")
        s_dn, s_xm = sem("s_dn"), sem("s_xm")
        s_xc = sem("s_xc")
        s_ang, s_sin, s_tab = sem("s_ang"), sem("s_sin"), sem("s_tab")
        s_hz, s_hzs = sem("s_hz"), sem("s_hzs")
        s_u = sem("s_u")
        s_hd = sem("s_hd")
        s_pr, s_xp = sem("s_pr"), sem("s_xp")
        s_dtp, s_nv, s_ey = sem("s_dtp"), sem("s_nv"), sem("s_ey")
        s_zp, s_zs, s_cv, s_xs = sem("s_zp"), sem("s_zs"), sem("s_cv"), sem("s_xs")
        s_R, s_seg, s_E, s_GG, s_W = sem("s_R"), sem("s_seg"), sem("s_E"), sem("s_GG"), sem("s_W")
        s_xt, s_xe, s_T, s_Ts, s_M = sem("s_xt"), sem("s_xe"), sem("s_T"), sem("s_Ts"), sem("s_M")
        s_r, s_t, s_y, s_yz, s_ysq = sem("s_r"), sem("s_t"), sem("s_y"), sem("s_yz"), sem("s_ysq")
        s_ss0, s_rr, s_rb, s_hy = sem("s_ss0"), sem("s_rr"), sem("s_rb"), sem("s_hy")
        s_al, s_hf, s_up, s_x2 = sem("s_al"), sem("s_hf"), sem("s_up"), sem("s_x2")
        s_w, s_wh, s_wl = [sem("s_w0"), sem("s_w1")], sem("s_wh"), sem("s_wl")
        s_xh, s_xl, s_pkc = sem("s_xh"), sem("s_xl"), sem("s_pkc")
        s_pj, s_sq, s_ab, s_po, s_ss = sem("s_pj"), sem("s_sq"), sem("s_ab"), sem("s_po"), sem("s_ss")
        s_add, s_kr1, s_kr2, s_kb = sem("s_add"), sem("s_kr1"), sem("s_kr2"), sem("s_kb")
        s_kst, s_qst = sem("s_kst"), [sem("s_qst0"), sem("s_qst1")]
        s_ve, s_vst = sem("s_ve"), [sem("s_vst0"), sem("s_vst1"), sem("s_vst2"), sem("s_vst3")]
        s_rms, s_rq = sem("s_rms"), sem("s_rq")
        s_KT, s_in, s_v = sem("s_KT"), [sem("s_in0"), sem("s_in1")], [sem("s_v0"), sem("s_v1")]
        s_kc, s_msk = sem("s_kc"), sem("s_msk")
        s_sc, s_mx, s_nb, s_ex = sem("s_sc"), sem("s_mx"), sem("s_nb"), sem("s_ex")
        s_rc, s_pn, s_tp, s_pt, s_p4 = sem("s_rc"), sem("s_pn"), sem("s_tp"), sem("s_pt"), sem("s_p4")
        s_pv, s_ov = sem("s_pv"), sem("s_ov")
        s_ost = [sem("s_ost0"), sem("s_ost1")]
        s_wo, s_oin = sem("s_wo"), [sem("s_oin0"), sem("s_oin1")]
        s_hp, s_ht, s_htt, s_hT, s_bn = sem("s_hp"), sem("s_ht"), sem("s_htt"), sem("s_hT"), sem("s_bn")
        s_fp, s_fe, s_fd, s_fa = sem("s_fp"), sem("s_fe"), sem("s_fd"), sem("s_fa")
        s_rsp, s_rse, s_asp, s_ase = sem("s_rsp"), sem("s_rse"), sem("s_asp"), sem("s_ase")
        s_ler, s_am, s_exw, s_w8, s_wt, s_wte = sem("s_ler"), sem("s_am"), sem("s_exw"), sem("s_w8"), sem("s_wt"), sem("s_wte")
        s_lv, s_ls, s_sg, s_ga, s_gb, s_gate = sem("s_lv"), sem("s_ls"), sem("s_sg"), sem("s_ga"), sem("s_gb"), sem("s_gate")
        s_ax, s_axe, s_fo, s_fin, s_out = sem("s_ax"), sem("s_axe"), sem("s_fo"), sem("s_fin"), sem("s_out")
        s_mean, s_ab0, s_op = sem("s_mean"), sem("s_ab0"), sem("s_op")
        s_seen = sem("s_seen")

        block = ctx.enter_context(nc.Block())

        def after(eng, sem, value):
            if not isinstance(value, int) or value > 0:
                eng.wait_ge(sem, value)

        def page_number(eng, b, n):
            return eng.value_load(table[0:1, ds(NPP * b + n, 1)], min_val=0, max_val=PAGES - 1)

        def bc(ap, axis, shape):
            return ap.unsqueeze(axis).to_broadcast(shape)

        def score(j):
            return psum[:, 2 * (j % 2):2 * (j % 2) + 2, :].rearrange("p a n -> p (a n)")[:, 0:LK]

        def by_batch(ap):
            return ap.rearrange("p (b s) -> p b s", s=S)

        ko = [stage[:, 2 * h:2 * h + 2, :].rearrange("p a n -> p (a n)").rearrange("p (b g s) -> p b g s", g=HK, s=S)
              for h in range(2)]
        sqr = [stage[:, n, :].rearrange("p (b r s) -> p b r s", r=REP, s=S) for n in range(2)]
        qor = [stage[:, 2 + n, :].rearrange("p (b r s) -> p b r s", r=REP, s=S) for n in range(2)]
        ksq = [vo[:, n, :] for n in range(2)]
        diag = [vo[:, 2 + n, :].rearrange("p (a c) -> p a c", c=P) for n in range(2)]

        @block.sync
        def _(sp):
            sp.dma_start(ints[:, :], t["ints"]).then_inc(s_ids, 16)
            sp.dma_start(pka[:, :], t["packa"]).then_inc(s_pka, 16)
            xv = t["x"].rearrange("(p j) c w -> (j c) p w", j=2)
            for j in range(2):
                sp.dma_start(xc[S * j:S * j + S, :, :],
                             t["x"].rearrange("(p j) c w -> j c p w", j=2)[j]).then_inc(s_x, 16)
            sp.wait_ge(s_ids, 16)
            sp.wait_ge(s_wz, 1)
            with sp.Fori(0, NPAIR) as p:
                for j in range(2):
                    sid = sp.value_load(ints[0:1, ds(2 * p + j, 1)], min_val=0, max_val=SESS - 1)
                    sp.dma_start(wgat[S * j:S * j + S, ds(p, 1), CHID * j:CHID * j + CHID],
                                 t["wsess"][ds(sid, 1), :, :].rearrange("a c h -> c a h")).then_inc(s_gather, 16)
            sp.dma_start(x2T[:, :, :], t["xT"].rearrange("(k p) n -> p k n", p=P)).then_inc(s_xT, 16)
            sp.dma_start(pkb[:, :], t["packb"]).then_inc(s_pkb, 16)
            sp.dma_start(table[:, :], t["table"]).then_inc(s_ids, 16)
            def load_weights(n):
                if n >= 2:
                    sp.wait_ge(s_wh, n - 1)
                    sp.wait_ge(s_wl, n - 1)
                name, at = WSLOTS[n]
                sp.dma_start(wland[:, n % 2], t[name].rearrange("(k p) n -> p k n", p=P)[:, :, WCOLS * at:WCOLS * at + WCOLS]).then_inc(s_w[n % 2], 16)

            for n in range(3):
                load_weights(n)

            sp.wait_ge(s_x2, 2 * KC)
            sp.dma_start(KT[:, :], t["kcT"].rearrange("d a g s -> d (a g s)")).then_inc(s_KT, 16)
            load_weights(3)
            kv = t["k_s"].rearrange("b p n -> p b n")
            for h in range(2):
                sp.wait_ge(s_po, 12 + 4 * h)
                for q in range(2):
                    done = s_kst if h == 0 else s_qst[q]
                    sp.dma_start(kv[:, 16 * h + 8 * q:16 * h + 8 * q + 8, :],
                                 ko[h][:, 8 * q:8 * q + 8].rearrange("p b g s -> p b (g s)")).then_inc(done, 16)
            for n in range(VTILES):
                s0, m = n // TILES, n % TILES
                if n % WTILES == 1:
                    load_weights(4 + n // WTILES)
                sp.wait_ge(s_ve, n + 1)
                sp.dma_start(t["v_s"][P * m:P * m + P, WCOLS * s0:WCOLS * s0 + WCOLS], vo[:, n % 4, :]).then_inc(s_vst[n % 4], 16)
            qv = t["q_s"].rearrange("b p n -> p b n")
            for g in range(HK):
                if g < HK - 2:
                    load_weights(6 + g)
                for h in range(2):
                    sp.wait_ge(s_po, KTILES + 8 * g + 4 * h + 4)
                    sp.dma_start(qv[:, 16 * h:16 * h + 16, P * g:P * g + P],
                                 qor[h].rearrange("p b r s -> p b (r s)")).then_inc(s_qst[h], 16)

            pages = t["vc"].rearrange("a s g d -> a s (g d)")

            def load_keys(b, par):
                after(sp, s_sc, 8 * b - 8)
                sp.dma_start(qring[:, par, :], t["q_s"][ds(b, 1)].rearrange("a p n -> p (a n)")).then_inc(s_in[par], 16)
                sp.dma_start(kring[:, par, NPP, :], t["k_s"][ds(b, 1)].rearrange("a p n -> p (a n)")).then_inc(s_in[par], 16)

            def load_values(b, par):
                after(sp, s_pv, 8 * b - 8)
                sp.dma_start(vring[0:S, par, BPT, :], t["v_s"][ds(S * b, S), :]).then_inc(s_v[par], 16)
                for n in range(NPP):
                    page = page_number(sp, b, n)
                    sp.dma_start(vring[S * (n % BPT):S * (n % BPT) + S, par, n // BPT, :],
                                 pages[ds(page, 1)].rearrange("a s n -> s (a n)")).then_inc(s_v[par], 16)

            def store(b, par):
                sp.wait_ge(s_ov, 8 * b + 8)
                sp.dma_start(t["o_s"][ds(b, 1)].rearrange("a p n -> p (a n)"), oring[:, par, :]).then_inc(s_ost[par], 16)

            sp.wait_ge(s_ab, KTILES + QTURNS * QTILES)
            sp.wait_ge(s_qst[0], 16 * (HK + 1))
            sp.wait_ge(s_qst[1], 16 * (HK + 1))
            sp.wait_ge(s_kst, 32)
            for b in range(2):
                load_keys(b, b)
            sp.wait_ge(s_ss, KTILES + 16)
            sp.wait_ge(s_po, KTILES + QTURNS * QTILES)
            for n in range(4):
                sp.wait_ge(s_vst[n], 16 * VTILES // 4)
            for b in range(2):
                load_values(b, b)
            with sp.Fori(0, B // 2 - 1) as i:
                for par in range(2):
                    store(2 * i + par, par)
                    load_keys(2 * i + 2 + par, par)
                    load_values(2 * i + 2 + par, par)
            sp.wait_ge(s_kc, NPP * B)
            sp.dma_start(wo, t["woT"].rearrange("(h p) n -> p h n", p=P)).then_inc(s_wo, 16)
            store(B - 2, 0)
            store(B - 1, 1)
            for par in range(2):
                sp.wait_ge(s_ost[par], 16 * (B // 2))
            sp.dma_start(pkc[:, :], t["packc"]).then_inc(s_pkc, 16)
            for n in range(TILES):
                if n >= 2:
                    sp.wait_ge(s_op, n - 1)
                sp.dma_start(oins[n % 2][:, :, :],
                             t["o_s"][BPT * n:BPT * n + BPT].rearrange("b p n -> p b n")).then_inc(s_oin[n % 2], 16)
            for n in range(2 * KC):
                m, h = n // 2, n % 2
                sp.wait_ge(s_fin, n + 1)
                sp.dma_start(t["out"][P * m:P * m + P, HALF * h:HALF * h + HALF],
                             hT[:, m, HALF * h:HALF * h + HALF]).then_inc(s_out, 16)
            sp.wait_ge(s_out, 16 * 2 * KC)

        @block.gpsimd
        def _(pool):
            pool.memset(wgat[:, :, :], 0.0).then_inc(s_wz, 1)
            pool.memset(ones[:, :], 1.0).then_inc(s_wz, 1)
            pool.memset(mean_d[:, :], 1.0 / D).then_inc(s_wz, 1)
            pool.memset(eps_qk[:, :], EPS_QK).then_inc(s_wz, 1)
            pool.wait_ge(s_xT, 16)
            with pool.Fori(0, 2) as h:
                for k in range(KC):
                    pool.wait_ge(s_cT, KC * h + k + 1)
                    pool.tensor_tensor(x2T[:, k, ds(HALF * h, HALF)], x2T[:, k, ds(HALF * h, HALF)],
                                       condT[:, k, ds(HALF * h, HALF)], ALU.add).then_inc(s_xc, 1)
            pool.wait_ge(s_xc, 2 * KC)
            pool.wait_ge(s_xm, 2)
            pool.wait_ge(s_tab, 4)
            pool.memset(xpad[:, :, :, 0:DCONV - 1], 0.0).then_inc(s_hz, 1)
            pool.memset(bcpad[:, :, 0:DCONV - 1], 0.0).then_inc(s_hz, 1)
            pool.memset(Ct[:, 0:1], 0.0).then_inc(s_hz, 1)
            pool.memset(Ct[:, TOK + 1:TOK + 2], 0.0).then_inc(s_hz, 1)
            pool.memset(M[:, :, :], 0.0).then_inc(s_hz, 1)
            with pool.Fori(0, 2) as i:
                pool.wait_ge(s_W, 16 * i + 16)
                pool.wait_ge(s_seg, 2 * i + 2)
                w4 = bc(W12[:, 1], 2, [P, TILES, NH, S])
                d4 = bc(dtd[:, 1].rearrange("p (a h) -> p a h", h=NH), 3, [P, TILES, NH, S])
                pool.tensor_tensor(T12[:, 1].rearrange("p (a h) s -> p a h s", h=NH), w4, d4, ALU.mult).then_inc(s_T, 1)
                pool.wait_ge(s_T, 3 * i + 2)
                pool.tensor_tensor(T12[:, 0], T12[:, 0], T12[:, 1], ALU.add).then_inc(s_T, 1)

            pool.wait_ge(s_x2, 2 * KC)
            for n in range(2 * KC):
                h, k = n // KC, n % KC
                sl = slice(HALF * h, HALF * h + HALF)
                pool.wait_ge(s_xh, n + 1)
                pool.tensor_tensor(x16[:, 1, k, sl], x2T[:, k, sl], x16[:, 0, k, sl], ALU.subtract).then_inc(s_xl, 1)
            for n in range(KTILES):
                pool.wait_ge(s_ab, n + 1)
                pool.tensor_tensor(ab[:, n % 3, 0, :], ab[:, n % 3, 0, :], ab[:, n % 3, 1, :], ALU.add).then_inc(s_add, 1)
            with pool.Fori(0, QTURNS) as i:
                for n in range(QTILES):
                    m, r = n // 4, n % 4
                    if r == 0:
                        pool.wait_ge(s_qst[m % 2], 32 * i + 16 * (m // 2 + 1))
                    pool.wait_ge(s_ab, KTILES + QTILES * i + n + 1)
                    pool.tensor_tensor(qor[m % 2][:, :, r, :], by_batch(ab[:, n % 2, 0, :]),
                                       by_batch(ab[:, n % 2, 1, :]), ALU.add).then_inc(s_po, 1)

            def normalise(n, slot):
                pool.wait_ge(s_rc, n + 1)
                pool.sem_inc(s_seen, 1)
                pool.tensor_scalar(prob[:, slot, :], prob[:, slot, :], ri[:, slot:slot + 1], 1.0,
                                   ALU.mult, ALU.mult).then_inc(s_pn, 1)

            normalise(0, 0)
            normalise(1, 1)

            def pool_turn(i):
                for j in range(16):
                    n = 16 * i + j
                    if not (isinstance(i, int) and n + 2 >= UNITS):
                        normalise(n + 2, (j + 2) % 4)

            pool_turn(0)
            with pool.Fori(1, 15) as i:
                pool_turn(i)
            pool_turn(15)
            pool.wait_ge(s_hT, TILES)
            pool.tensor_tensor(x2T[:, :, :], x2T[:, :, :], hT[:, :, :], ALU.add).then_inc(s_fa, 1)

        @block.scalar
        def _(act):
            with act.Fori(0, 2) as h:
                for p in range(8):
                    n = 8 * h + p
                    if p == 0:
                        act.wait_ge(s_prep, 9)
                    act.wait_ge(s_h1, n + 1)
                    if p >= 2:
                        act.wait_ge(s_co, KC * (n - 1))
                    act.activation(hbuf[:, p % 2, :], bank(p % 2), ACT.Gelu,
                                   bias=bias1[:, ds(n, 1)]).then_inc(s_g1, 1)
                act.wait_ge(s_dn, h + 1)
                act.activation(xmid[:, :].rearrange("p (s b) -> p b s", b=B)[:, ds(16 * h, 16), :],
                               by_batch(bank(6)), ACT.Gelu, bias=A("bdown")).then_inc(s_xm, 1)
            act.wait_ge(s_ang, 2)
            for n in range(2):
                act.activation(turns[:, n, :], turns[:, n, :], ACT.Sin).then_inc(s_sin, 1)
            def split_weights(n, par):
                par %= 2
                act.wait_ge(s_w[par], 8 * n + 16 - 8 * par)
                after(act, s_pj, WTILES * (n - 1))
                act.activation(w16[:, par, 0], wland[:, par], ACT.Copy, scale=WSCALE).then_inc(s_wh, 1)

            split_weights(0, 0)
            act.wait_ge(s_hz, 5)
            act.activation(alpha[:, 0:1], A("gate1"), ACT.Sigmoid).then_inc(s_al, 1)
            act.activation(negA[:, :], A("alog"), ACT.Exp).then_inc(s_al, 1)

            with act.Fori(0, 2) as i:
                for n, (dst, c) in enumerate([(bcpad, None), (xpad, 0), (xpad, 1)]):
                    for h in range(2):
                        act.wait_ge(s_pr, 6 * i + 2 * n + h + 1)
                        src = bank(2 * n + h)[0:3 * DST] if c is None else bank(2 * n + h)
                        out = bcpad[:, 16 * h:16 * h + 16, DCONV - 1:] if c is None else \
                            xpad[:, c, 16 * h:16 * h + 16, DCONV - 1:]
                        act.activation(out, by_batch(src), ACT.Copy).then_inc(s_xp, 1)
                act.wait_ge(s_nv, i + 1)
                act.activation(dtv[:, 2, :], dtv[:, 1, :], ACT.Exp).then_inc(s_ey, 1)
                for n in range(4):
                    act.wait_ge(s_zp, 4 * i + n + 1)
                    act.activation(zs[:, n // 2, HALF * (n % 2):HALF * (n % 2) + HALF], bank(2 + n),
                                   ACT.Silu).then_inc(s_zs, 1)
                act.wait_ge(s_cv, 3 * i + 1)
                act.activation(Bt[:, :], cacc[0:DST, 2, :], ACT.Silu, bias=A("convbbc", DST)).then_inc(s_xs, 1)
                act.activation(Ct[:, 1:TOK + 1], cacc[2 * DST:3 * DST, 2, :], ACT.Silu,
                               bias=A("convbbc", DST, 2 * DST)).then_inc(s_xs, 1)
                for h in range(2):
                    act.wait_ge(s_seg, 2 * i + h + 1)
                    act.activation(E[:, 16 * h:16 * h + 16, :], by_batch(bank(h)), ACT.Exp).then_inc(s_E, 1)
                for c in range(2):
                    act.wait_ge(s_cv, 3 * i + c + 2)
                    act.activation(xs[:, c, :], cacc[:, c, :], ACT.Silu, bias=A("convbx")[:, c:c + 1]).then_inc(s_xs, 1)
                for n in range(4):
                    act.wait_ge(s_xt, 4 * i + n + 1)
                    act.activation(xtok[:, 4 * (n % 2):4 * (n % 2) + 4, P * (n // 2):P * (n // 2) + P],
                                   bank(2 + n % 2).rearrange("p (a c) -> p a c", a=4), ACT.Copy).then_inc(s_xe, 1)
                act.wait_ge(s_yz, 4 * i + 4)
                for c in range(2):
                    act.activation(cacc[:, c, :], yb[:, c, :], ACT.Square).then_inc(s_ysq, 1)
                for h in range(2):
                    act.wait_ge(s_rr, 2 * i + h + 1)
                    act.activation(rb[:, h, :], rb[:, h, :], ACT.Sqrt).then_inc(s_rb, 1)

            act.wait_ge(s_x2, 2 * KC)
            for n in range(2 * KC):
                h, k = n // KC, n % KC
                sl = slice(HALF * h, HALF * h + HALF)
                act.activation(x16[:, 0, k, sl], x2T[:, k, sl], ACT.Copy).then_inc(s_xh, 1)

            def key_rms(n):
                act.wait_ge(s_ss, n + 1)
                act.activation(kms[:, n, :], bank(6 + n % 2)[:, 0:4], ACT.Sqrt, bias=eps_qk[:, :]).then_inc(s_kr1, 1)

            for n in range(KTILES):
                act.wait_ge(s_pj, n + 1)
                if n >= 2:
                    act.wait_ge(s_ss, n - 1)
                act.activation(ksq[n % 2], bank(n % 4), ACT.Square, scale=1 / WSCALE).then_inc(s_sq, 1)
                if n % WTILES == 1:
                    split_weights(n // WTILES + 1, n // WTILES + 1)
                if n >= 1:
                    key_rms(n - 1)
            key_rms(KTILES - 1)
            act.wait_ge(s_ss, KTILES)
            act.wait_ge(s_kb, KTILES)
            for n in range(VTILES):
                act.wait_ge(s_pj, KTILES + n + 1)
                if n >= 4:
                    act.wait_ge(s_vst[n % 4], 16 * (n // 4))
                act.activation(vo[:, n % 4, :], bank(n % 4), ACT.Copy, scale=1 / WSCALE).then_inc(s_ve, 1)
                if n % WTILES == 1:
                    split_weights(3 + n // WTILES, 3 + n // WTILES)
            act.wait_ge(s_kst, 32)

            def act_queries(i):
                for n in range(QTILES):
                    m, r = n // 4, n % 4
                    act.wait_ge(s_pj, KTILES + VTILES + QTILES * i + n + 1)
                    if r == 0:
                        act.wait_ge(s_ss, KTILES + 4 * i + m - 1)
                    act.activation(sqr[m % 2][:, :, r, :], by_batch(bank(n % 4)), ACT.Square, scale=1 / WSCALE).then_inc(s_sq, 1)
                    slot = 4 + 2 * i + n // WTILES
                    if n % WTILES == 1 and not (isinstance(i, int) and slot == len(WSLOTS) - 1):
                        split_weights(slot + 1, n // WTILES + 1)

            with act.Fori(0, QTURNS - 1) as i:
                act_queries(i)
            act_queries(QTURNS - 1)
            act.wait_ge(s_ss, KTILES + 16)
            act.activation(rq[:, :], bank(7)[:, 0:B * HK], ACT.Sqrt, bias=eps_qk[:, :]).then_inc(s_rms, 1)

            def exponentials(n, col, slot):
                act.wait_ge(s_nb, n + 1)
                act.activation(prob[:, slot, :], prob[:, slot, :], ACT.Exp, bias=nb[:, slot:slot + 1],
                               scale=rq[:, col], accum_out=rs[:, slot:slot + 1]).then_inc(s_ex, 1)


            for n in range(3):
                exponentials(n, slice(n, n + 1), n)

            def act_turn(i):
                for j in range(16):
                    n = 16 * i + j
                    act.wait_ge(s_tp, n + 1)
                    after(act, s_pv, n - 1)
                    act.activation(pT4[:, j % 2, :], bank(6 + j % 2)[0:S, P:2 * P], ACT.Copy).then_inc(s_p4, 1)
                    if not (isinstance(i, int) and n == 0):
                        jj = (j - 1) % 16
                        act.wait_ge(s_pv, n)
                        if jj % 8 == 0:
                            turn = i if j > 0 else i - 1
                            after(act, s_ost[jj // 8], 16 * turn)
                        act.activation(oring[:, jj // 8, P * (jj % 8):P * (jj % 8) + P], bank(6 + jj % 2)[:, 0:P],
                                       ACT.Copy).then_inc(s_ov, 1)
                    if not (isinstance(i, int) and n + 3 >= UNITS):
                        exponentials(n + 3, ds(n + 3, 1) if not isinstance(i, int) else slice(n + 3, n + 4), (j + 3) % 4)

            act_turn(0)
            with act.Fori(1, 15) as i:
                act_turn(i)
            act_turn(15)
            act.wait_ge(s_pv, UNITS)
            act.activation(oring[:, 1, P * 7:P * 8], bank(7)[:, 0:P], ACT.Copy).then_inc(s_ov, 1)

            act.wait_ge(s_ost[0], 16 * B // 2)
            act.wait_ge(s_ost[1], 16 * B // 2)
            for n in range(TILES):
                act.wait_ge(s_hp, n + 1)
                act.activation(htok[:, n, :], bank(n % 2), ACT.Copy).then_inc(s_ht, 1)
            act.wait_ge(s_fp, 1)
            act.activation(rkT[:, :], bank(4)[0:RDIM, 0:NSLOT], ACT.Copy).then_inc(s_fe, 1)
            act.wait_ge(s_fp, 2)
            act.activation(AV[:, :], bank(5)[:, 0:VB], ACT.Copy).then_inc(s_fe, 1)
            for h in range(2):
                act.wait_ge(s_fp, 3 + h)
                act.activation(queryT[:, HALF * h:HALF * h + HALF], bank(h)[0:BOT], ACT.Copy).then_inc(s_fe, 1)
            for h in range(2):
                act.wait_ge(s_fp, 5 + h)
                act.activation(rqT[:, HALF * h:HALF * h + HALF], bank(2 + h)[0:RDIM], ACT.Copy).then_inc(s_fe, 1)
            for h in range(2):
                act.wait_ge(s_fp, 7 + h)
                act.activation(uT[:, HALF * h:HALF * h + HALF], bank(6 + h), ACT.Gelu_apprx_tanh,
                               bias=C("fbu1")).then_inc(s_fe, 1)
            act.wait_ge(s_bn, TILES)
            act.activation(sm[:, 0, :], mv[:, :, 1], ACT.Ln, bias=1.0, accum_out=lsum[:, 0:1]).then_inc(s_lv, 1)
            act.wait_ge(s_ler, 1)
            act.activation(sm[:, 1, :], bank(6)[:, 0:TILES], ACT.Sigmoid, bias=C("fbu2")).then_inc(s_sg, 1)
            act.wait_ge(s_ga, 1)
            act.activation(sm[:, 4, :], sm[:, 3, :], ACT.Sigmoid, bias=C("fgb"), scale=C("fgw")).then_inc(s_gb, 1)
            act.wait_ge(s_am, 1)
            for n in range(TILES):
                act.activation(asc[:, n, :], asc[:, n, :], ACT.Exp, bias=amx[:, n:n + 1],
                               accum_out=wsum[:, n:n + 1]).then_inc(s_exw, 1)
            for n in range(2):
                act.wait_ge(s_wt, n + 1)
                act.activation(wTs[:, HALF * n:HALF * n + HALF], bank(2 + n), ACT.Copy).then_inc(s_wte, 1)
            for h in range(2):
                act.wait_ge(s_ax, h + 1)
                act.activation(auxT[:, HALF * h:HALF * h + HALF], bank(h)[0:VB], ACT.Copy).then_inc(s_axe, 1)

        @block.vector
        def _(dve):
            done = [0]

            def prep(ins):
                done[0] += 1
                ins.then_inc(s_prep, 1)
                dve.wait_ge(s_prep, done[0])

            dve.wait_ge(s_ids, 16)
            prep(dve.tensor_copy(intf[:, :], ints[:, :]))
            dve.wait_ge(s_pka, 16)
            dve.tensor_scalar(onehot[:, :], intf[0:SESS, 0:B], A("sessidx", SESS), None, ALU.is_equal).then_inc(s_masks, 1)
            for j in range(2):
                dve.tensor_scalar(cmask[S * j:S * j + S, :], intf[S * j:S * j + S, B + j:2 * B:2],
                                  A("chan", S, S * j), None, ALU.is_gt).then_inc(s_prep, 1)
            for k in range(KC):
                dve.tensor_scalar(tmask[:, k, :], intf[:, 2 * B:3 * B], A("tcol")[:, k:k + 1], None,
                                  ALU.is_gt).then_inc(s_prep, 1)
            done[0] += 2 + KC
            dve.wait_ge(s_prep, done[0])
            dve.wait_ge(s_bias, 1)
            for j in range(2):
                dve.tensor_copy(bias1[CHID * j:CHID * j + CHID, :], bank(7)[CHID * j:CHID * j + CHID, j:B:2]).then_inc(s_prep, 1)
            done[0] += 2
            dve.wait_ge(s_prep, done[0])
            dve.wait_ge(s_gather, 16 * B)

            with dve.Fori(0, 2) as h:
                for p in range(8):
                    n = 8 * h + p
                    if p >= 2:
                        dve.wait_ge(s_h1, n - 1)
                    dve.tensor_scalar(wst[:, p % 2, :], wgat[:, ds(n, 1), :].rearrange("p a n -> p (a n)"),
                                      cmask[:, ds(n, 1)], None, ALU.mult).then_inc(s_wst, 1)
                for k in range(KC):
                    dve.wait_ge(s_co, 8 * KC * h + 7 * KC + k + 1)
                    out = condT[:, k, ds(HALF * h, HALF)].rearrange("p (b s) -> p b s", s=S)
                    dve.tensor_tensor(out, by_batch(bank(2 + k)), bc(A("b2"), 1, [P, 16, S]), ALU.add).then_inc(s_ca, 1)
                    dve.wait_ge(s_ca, KC * h + k + 1)
                    dve.tensor_tensor(out, out, bc(tmask[:, k, ds(16 * h, 16)], 2, [P, 16, S]),
                                      ALU.mult).then_inc(s_cT, 1)

            prep(dve.tensor_tensor(by_batch(ang[:, :]), bc(intf[:, 3 * B:4 * B], 2, [P, B, S]),
                                   bc(A("srow"), 1, [P, B, S]), ALU.add))
            prep(dve.tensor_scalar(ang[:, :], ang[:, :], A("invf"), None, ALU.mult))
            for n in range(2):
                tn = turns[:, n, :]
                count = condT[:, n, :]
                if n == 0:
                    dve.wait_ge(s_xc, 2 * KC)
                    dve.wait_ge(s_dn, 2)
                prep(dve.tensor_scalar(count, ang[:, :], float(1 / (2 * np.pi)), 0.25 * n, ALU.mult, ALU.add))
                prep(dve.tensor_scalar(count, count, ROUND, ROUND, ALU.add, ALU.subtract))
                prep(dve.scalar_tensor_tensor(out=tn, in0=count, scalar=-PI2_A, in1=ang[:, :], op0=ALU.mult, op1=ALU.add))
                prep(dve.scalar_tensor_tensor(out=tn, in0=count, scalar=-PI2_B, in1=tn, op0=ALU.mult, op1=ALU.add))
                prep(dve.scalar_tensor_tensor(out=tn, in0=count, scalar=-PI2_C, in1=tn, op0=ALU.mult, op1=ALU.add))
                if n == 1:
                    prep(dve.tensor_scalar(tn, tn, float(np.pi / 2), None, ALU.add))
                dve.tensor_scalar(tn, tn, PI, -PI, ALU.min, ALU.max).then_inc(s_ang, 1)
            for n in range(4):
                sine = n % 2
                dve.wait_ge(s_sin, 2 - sine)
                dve.tensor_scalar(tabs[:, n, :], turns[:, 1 - sine, :], A("qnw") if n < 2 else A("knw"),
                                  A("sign") if sine else 1 / WSCALE, ALU.mult, ALU.mult).then_inc(s_tab, 1)

            def split_weights(n, par):
                par %= 2
                dve.wait_ge(s_wh, n + 1)
                dve.scalar_tensor_tensor(out=w16[:, par, 1], in0=wland[:, par], scalar=WSCALE, in1=w16[:, par, 0],
                                         op0=ALU.mult, op1=ALU.subtract).then_inc(s_wl, 1)

            split_weights(0, 0)
            dve.wait_ge(s_xm, 2)
            dve.wait_ge(s_al, 2)
            prep(dve.tensor_scalar(negA[:, :], negA[:, :], -1.0, None, ALU.mult))
            prep(dve.tensor_scalar(alpha[:, 1:2], alpha[:, 0:1], 1.0, None, ALU.add))
            prep(dve.tensor_scalar(alpha[:, 2:3], alpha[:, 0:1], -1.0, 1.0, ALU.mult, ALU.add))
            for c in range(2):
                prep(dve.tensor_scalar(outw[:, c, :], A("outw")[:, DM * c:DM * c + DM], A("normw")[:, c:c + 1],
                                       None, ALU.mult))
            dve.wait_ge(s_hz, 5)
            dve.tensor_copy(u[:, :], xmid[:, :]).then_inc(s_u, 1)

            ta = "p (a h) -> p a h"
            with dve.Fori(0, 2) as i:
                steps = [0]

                def step(ins):
                    steps[0] += 1
                    ins.then_inc(s_hd, 1)
                    dve.wait_ge(s_hd, NCHAIN * i + steps[0])

                dve.wait_ge(s_dtp, i + 1)
                step(dve.tensor_tensor(dtv[:, 0, :].rearrange(ta, h=8), bank(6)[:, 0:8 * TILES].rearrange(ta, h=8),
                                       bc(A("dtb"), 1, [P, TILES, 8]), ALU.add))
                dve.scalar_tensor_tensor(out=dtv[:, 1, :], in0=dtv[:, 0, :], scalar=-1.0, in1=dtv[:, 0, :],
                                         op0=ALU.mult, op1=ALU.min).then_inc(s_nv, 1)

                def convolve(src, w, dst):
                    out = dst.rearrange("p (a s) -> p a s", s=S)
                    step(dve.tensor_scalar(out, src[:, :, 0:S], w[:, 0:1], None, ALU.mult))
                    for k in range(1, DCONV):
                        ins = dve.scalar_tensor_tensor(out=out, in0=src[:, :, k:k + S], scalar=w[:, k:k + 1],
                                                       in1=out, op0=ALU.mult, op1=ALU.add)
                        if k < DCONV - 1:
                            step(ins)
                    ins.then_inc(s_cv, 1)

                dve.wait_ge(s_xp, 6 * i + 2)
                convolve(bcpad, A("convbc", 3 * DST), cacc[0:3 * DST, 2, :])

                dve.wait_ge(s_ey, i + 1)
                y, z, z2, p = dtv[:, 2, :], dtv[:, 3, :], dtv[:, 4, :], dtv[:, 1, :]
                step(dve.tensor_scalar(z, y, 2.0, None, ALU.add))
                step(dve.reciprocal(z, z))
                step(dve.tensor_tensor(z, z, y, ALU.mult))
                step(dve.tensor_tensor(z2, z, z, ALU.mult))
                step(dve.tensor_scalar(p, z2, 1.0 / 15, None, ALU.mult))
                for c in (13, 11, 9, 7, 5, 3):
                    step(dve.scalar_tensor_tensor(out=p, in0=p, scalar=1.0 / c, in1=z2, op0=ALU.add, op1=ALU.mult))
                step(dve.scalar_tensor_tensor(out=p, in0=p, scalar=1.0, in1=z, op0=ALU.add, op1=ALU.mult))
                step(dve.tensor_scalar(y, dtv[:, 0, :], 0.0, None, ALU.max))
                step(dve.scalar_tensor_tensor(out=y, in0=p, scalar=2.0, in1=y, op0=ALU.mult, op1=ALU.add))
                y8 = y.rearrange(ta, h=8)
                for d in range(2):
                    step(dve.tensor_copy(dtd[:, d, :].rearrange(ta, h=NH), y8[:, :, NH * d:NH * d + NH]))
                    step(dve.tensor_tensor(dtd[:, 2 + d, :].rearrange(ta, h=NH), y8[:, :, NH * d:NH * d + NH],
                                           bc(negA[:, :], 1, [P, TILES, NH]), ALU.mult))
                for d, side in enumerate(("before", "after")):
                    dve.tensor_tensor(Rm[:, d], bc(dtd[:, 2 + d, :], 2, [P, TILES * NH, S]),
                                      bc(A(side), 1, [P, TILES * NH, S]), ALU.mult).then_inc(s_R, 1)

                dve.wait_ge(s_xp, 6 * i + 4)
                convolve(xpad[:, 0], A("convx")[:, 0:DCONV], cacc[:, 0, :])

                for d, side in enumerate(("before", "after")):
                    for m in range(2):
                        dve.wait_ge(s_GG, 4 * i + 2 * d + m + 1)
                        src = bank((6, 4)[d] + m).rearrange("p (a c) -> p a c", a=4)
                        for q in range(BPT):
                            lo = S * q
                            dve.tensor_tensor(W12[lo:lo + S, d, 4 * m:4 * m + 4, :], src[lo:lo + S, :, lo:lo + S],
                                              bc(A(side, S, lo), 1, [S, 4, S]), ALU.mult).then_inc(s_W, 1)

                dve.wait_ge(s_xp, 6 * i + 6)
                convolve(xpad[:, 1], A("convx")[:, DCONV:2 * DCONV], cacc[:, 1, :])

                dve.wait_ge(s_W, 16 * i + 16)
                dve.wait_ge(s_seg, 2 * i + 2)
                dve.tensor_tensor(T12[:, 0].rearrange("p (a h) s -> p a h s", h=NH),
                                  bc(W12[:, 0], 2, [P, TILES, NH, S]),
                                  bc(dtd[:, 0].rearrange(ta, h=NH), 3, [P, TILES, NH, S]), ALU.mult).then_inc(s_T, 1)
                dve.wait_ge(s_T, 3 * i + 3)
                dve.wait_ge(s_E, 2 * i + 2)
                for q in range(BPT):
                    lo = S * q
                    dve.tensor_tensor(M[lo:lo + S, :, lo:lo + S], T12[lo:lo + S, 0], E[lo:lo + S], ALU.mult).then_inc(s_M, 1)
                for n in range(4):
                    c, h = n // 2, n % 2
                    sl = slice(HALF * h, HALF * h + HALF)
                    dve.wait_ge(s_r, 4 * i + n + 1)
                    dve.scalar_tensor_tensor(out=yb[:, c, sl], in0=bank(4 + n), scalar=A("dskip")[:, c:c + 1],
                                             in1=xs[:, c, sl], op0=ALU.add, op1=ALU.mult).then_inc(s_t, 1)
                for n in range(4):
                    c, h = n // 2, n % 2
                    sl = slice(HALF * h, HALF * h + HALF)
                    dve.wait_ge(s_y, 4 * i + n + 1)
                    dve.wait_ge(s_t, 4 * i + n + 1)
                    step(dve.tensor_tensor(yb[:, c, sl], bank(n), yb[:, c, sl], ALU.add))
                    dve.tensor_tensor(yb[:, c, sl], yb[:, c, sl], zs[:, c, sl], ALU.mult).then_inc(s_yz, 1)
                for h in range(2):
                    dve.wait_ge(s_ss0, 2 * i + h + 1)
                    step(dve.tensor_scalar(rb[:, h, :], bank(4 + h), 1.0 / DIN, EPS_HYDRA, ALU.mult, ALU.add))
                    dve.reciprocal(rb[:, h, :], rb[:, h, :]).then_inc(s_rr, 1)
                for h in range(2):
                    sl = slice(HALF * h, HALF * h + HALF)
                    dve.wait_ge(s_hy, 2 * i + h + 1)
                    dve.wait_ge(s_rb, 2 * i + h + 1)
                    ins = dve.tensor_tensor(u[:, sl], bank(6 + h), rb[:, h, :], ALU.mult)
                    if h == 0:
                        step(ins)
                ins.then_inc(s_u, 1)
                assert steps[0] == NCHAIN, steps
            dve.wait_ge(s_u, 3)
            prep(dve.tensor_scalar(u[:, :], u[:, :], alpha[:, 2:3], None, ALU.mult))
            dve.scalar_tensor_tensor(out=u[:, :], in0=xmid[:, :], scalar=alpha[:, 1:2], in1=u[:, :],
                                     op0=ALU.mult, op1=ALU.add).then_inc(s_hf, 1)
            for n in range(2 * KC):
                h, k = n // KC, n % KC
                sl = slice(HALF * h, HALF * h + HALF)
                dve.wait_ge(s_up, n + 1)
                if n == 0:
                    dve.wait_ge(s_xc, 2 * KC)
                dve.scalar_tensor_tensor(out=x2T[:, k, sl], in0=bank(n), scalar=A("bup")[:, k:k + 1],
                                         in1=x2T[:, k, sl], op0=ALU.add, op1=ALU.add).then_inc(s_x2, 1)

            def rotate(tile, slot, h, tab):
                sl = slice(HALF * h, HALF * h + HALF)
                dve.tensor_tensor(ab[:, slot, 0, :], tile, tabs[:, tab, sl], ALU.mult).then_inc(s_ab0, 1)
                dve.tensor_tensor(ab[0:64, slot, 1, :], tile[64:P], tabs[64:P, tab + 1, sl], ALU.mult).then_inc(s_ab0, 1)
                dve.tensor_tensor(ab[64:P, slot, 1, :], tile[0:64], tabs[0:64, tab + 1, sl], ALU.mult).then_inc(s_ab, 1)

            def key_diagonal(n):
                dve.wait_ge(s_kr1, n + 1)
                prep(dve.reciprocal(kms[:, n, :], kms[:, n, :]))
                if n >= 2:
                    dve.wait_ge(s_kb, n - 1)
                dve.tensor_tensor(diag[n % 2], bc(G("ident"), 1, [P, 4, P]), bc(kms[:, n, :], 2, [P, 4, P]),
                                  ALU.mult).then_inc(s_kr2, 1)

            def normalise_key(n):
                h, g = n // 4 % 2, 4 * (n // 8) + n % 4
                dve.wait_ge(s_add, n + 1)
                dve.wait_ge(s_kb, n + 1)
                dve.tensor_tensor(ko[h][:, :, g, :], by_batch(ab[:, n % 3, 0, :]), by_batch(bank(4 + n % 2)),
                                  ALU.mult).then_inc(s_po, 1)

            for n in range(KTILES + 2):
                if n < KTILES:
                    dve.wait_ge(s_sq, n + 1)
                    if n >= 3:
                        dve.wait_ge(s_po, n - 2)
                    rotate(bank(n % 4), n % 3, n // 4 % 2, 2)
                    if n % WTILES == 1:
                        split_weights(n // WTILES + 1, n // WTILES + 1)
                if 1 <= n <= KTILES:
                    key_diagonal(n - 1)
                if n >= 2:
                    normalise_key(n - 2)
            for n in range(2):
                split_weights(3 + n, 3 + n)

            def copy_page(par, n, page):
                dve.tensor_copy(kring[:, par, n, :], KT[:, ds(page * (HK * S), HK * S)]).then_inc(s_kc, 1)

            def dve_queries(i):
                for n in range(QTILES):
                    dve.wait_ge(s_sq, KTILES + QTILES * i + n + 1)
                    dve.wait_ge(s_po, KTILES + QTILES * i + n - 1)
                    rotate(bank(n % 4), n % 2, n // 4 % 2, 0)
                    slot = 4 + 2 * i + n // WTILES
                    if n % WTILES == 1 and not (isinstance(i, int) and slot == len(WSLOTS) - 1):
                        split_weights(slot + 1, n // WTILES + 1)
                    if isinstance(i, int) and n >= QTILES - 6:
                        if n == QTILES - 6:
                            dve.wait_ge(s_pj, KTILES + VTILES + QTURNS * QTILES - 8)
                            dve.wait_ge(s_ids, 32)
                            dve.wait_ge(s_KT, 16)
                        for c in range([0, 3, 6, 9, 12, 14][n - QTILES + 6], [3, 6, 9, 12, 14, 16][n - QTILES + 6]):
                            copy_page(0, c, page_number(dve, 0, c))

            with dve.Fori(0, QTURNS - 1) as i:
                dve_queries(i)
            dve_queries(QTURNS - 1)
            dve.wait_ge(s_rms, 1)
            prep(dve.reciprocal(rq[:, :], rq[:, :]))
            prep(dve.tensor_scalar(nrq[:, :], rq[:, :], -SCALE, None, ALU.mult))
            dve.tensor_scalar(rq[:, :], rq[:, :], SCALE, None, ALU.mult).then_inc(s_rq, 1)

            def cached_mask(b):
                dve.tensor_scalar(mask[:, 0:LC], G("iota"), b, NEG, ALU.is_ge, ALU.mult).then_inc(s_msk, 1)

            def col(tensor, n):
                return tensor[:, n:n + 1] if isinstance(n, int) else tensor[:, ds(n, 1)]

            def masked_max(n, b, j):
                slot = j % 4
                if j % 8 == 0:
                    after(dve, s_mx, n)
                    cached_mask(col(intf, 3 * B + b))
                    dve.wait_ge(s_msk, b + 2)
                dve.wait_ge(s_sc, n + 1)
                after(dve, s_tp, n - 3)
                dve.sem_inc(s_seen, 1)
                dve.tensor_tensor_reduce(out=prob[:, slot, :], in0=score(j), in1=mask[:, :], scale=1.0,
                                         scalar=-3e38, op0=ALU.add, op1=ALU.max,
                                         accum_out=mx[:, slot:slot + 1]).then_inc(s_mx, 1)

            def exponent_bias(n, j):
                slot = j % 4
                dve.wait_ge(s_mx, n + 1)
                dve.tensor_tensor(nb[:, slot:slot + 1], mx[:, slot:slot + 1], col(nrq, n), ALU.mult).then_inc(s_nb, 1)

            def inverse(n, j):
                dve.wait_ge(s_ex, n + 1)
                dve.reciprocal(ri[:, j % 4:j % 4 + 1], rs[:, j % 4:j % 4 + 1]).then_inc(s_rc, 1)

            dve.wait_ge(s_pkb, 16)
            dve.wait_ge(s_qst[0], 16 * (HK + 1))
            dve.wait_ge(s_qst[1], 16 * (HK + 1))
            for n in range(4):
                dve.wait_ge(s_vst[n], 16 * VTILES // 4)
            dve.wait_ge(s_rq, 1)
            dve.memset(mask[:, LC:LK], 0.0).then_inc(s_msk, 1)
            for n in range(3):
                masked_max(n, 0, n)
                exponent_bias(n, n)
                for m in range(2 * n, 2 * n + 2):
                    copy_page(1, m, page_number(dve, 1, m))
            inverse(0, 0)
            inverse(1, 1)

            def dve_turn(i):
                for j in range(16):
                    n = 16 * i + j
                    b, lo = (j + 3) // 8 + 1, 2 * ((j + 3) % 8)
                    copies = not (isinstance(i, int) and 2 * i + b >= B)
                    dve.wait_ge(s_tp, n + 1)
                    after(dve, s_pv, n - 1)
                    dve.tensor_copy(pT[:, j % 2, :], bank(4 + j % 2)).then_inc(s_pt, 1)
                    if copies:
                        page0 = page_number(dve, 2 * i + b, lo)
                    if not (isinstance(i, int) and n + 2 >= UNITS):
                        inverse(n + 2, j + 2)
                    if not (isinstance(i, int) and n + 3 >= UNITS):
                        masked_max(n + 3, 2 * i + (j + 3) // 8, j + 3)
                        if copies:
                            page1 = page_number(dve, 2 * i + b, lo + 1)
                        exponent_bias(n + 3, j + 3)
                    if copies:
                        copy_page(b % 2, lo, page0)
                        copy_page(b % 2, lo + 1, page1)

            dve_turn(0)
            with dve.Fori(1, 15) as i:
                dve_turn(i)
            dve_turn(15)

            dve.wait_ge(s_pv, UNITS)
            dve.wait_ge(s_ost[0], 16 * B // 2)
            dve.wait_ge(s_ost[1], 16 * B // 2)
            def reorder(n):
                dve.wait_ge(s_oin[n % 2], 16 * (n // 2) + 16)
                if n >= 2:
                    dve.wait_ge(s_hp, n - 1)
                dve.tensor_copy(operm[:, n % 2], oins[n % 2][:, :, :].rearrange("p b (h s) -> p h b s", s=S)).then_inc(s_op, 1)

            reorder(0)
            for n in range(TILES + 1):
                if n + 1 < TILES:
                    reorder(n + 1)
                if n < TILES:
                    dve.wait_ge(s_ht, n + 1)
                    prep(dve.bn_stats(bn[:, n, :], htok[:, n, :]))
                    dve.bn_aggr(mv[:, n, :], bn[:, n, :]).then_inc(s_bn, 1)
                if n >= 1:
                    m = n - 1
                    dve.wait_ge(s_htt, m + 1)
                    dve.tensor_copy(hT[:, :, P * m:P * m + P],
                                    bank(2 + m % 2).rearrange("p (k c) -> p k c", k=KC)).then_inc(s_hT, 1)
            for n in range(TILES):
                q = P * (n % 4)
                dve.wait_ge(s_rsp, n // 4 + 1)
                dve.scalar_tensor_tensor(out=rsc[:, n, :], in0=bank(4 + n // 4)[:, q:q + P], scalar=float(1 / np.sqrt(RDIM)),
                                         in1=C("flog"), op0=ALU.mult, op1=ALU.add).then_inc(s_rse, 1)
            for n in range(TILES):
                dve.wait_ge(s_rse, n + 1)
                prep(dve.max(top8[:, n, :], rsc[:, n, :]))
                dve.match_replace(out=rep8[:, n, :], in_to_replace=top8[:, n, :], in_values=rsc[:, n, :],
                                  imm_value=-3e38).then_inc(s_rse, 1)
            for n in range(TILES):
                q = P * (n % 4)
                dve.wait_ge(s_asp, n // 4 + 1)
                dve.scalar_tensor_tensor(out=asc[:, n, :], in0=bank(n // 4)[:, q:q + P], scalar=float(1 / np.sqrt(BOT)),
                                         in1=C("flog"), op0=ALU.mult, op1=ALU.add).then_inc(s_ase, 1)
            dve.wait_ge(s_rse, 2 * TILES)
            dve.wait_ge(s_ase, TILES)
            prep(dve.tensor_tensor(rep8[:, :, :], rsc[:, :, :], rep8[:, :, :], ALU.not_equal))
            prep(dve.tensor_tensor(asc[:, :, :], asc[:, :, :], rep8[:, :, :], ALU.mult))
            prep(dve.tensor_scalar(rep8[:, :, :], rep8[:, :, :], -NEG, NEG, ALU.mult, ALU.add))
            prep(dve.tensor_tensor(asc[:, :, :], asc[:, :, :], rep8[:, :, :], ALU.add))
            prep(dve.tensor_reduce(amx[:, :], asc[:, :, :], AXX, ALU.max))
            dve.tensor_scalar(amx[:, :], amx[:, :], -1.0, None, ALU.mult).then_inc(s_am, 1)
            dve.wait_ge(s_mean, 1)
            prep(dve.tensor_scalar(lsum[:, 1:2], bank(7)[:, 0:1], 1.0 / TOK, 1e-6, ALU.mult, ALU.add))
            prep(dve.reciprocal(lsum[:, 1:2], lsum[:, 1:2]))
            prep(dve.tensor_scalar(sm[:, 2, :], sm[:, 0, :], lsum[:, 1:2], 0.5, ALU.mult, ALU.mult))
            dve.wait_ge(s_sg, 1)
            prep(dve.scalar_tensor_tensor(out=sm[:, 3, :], in0=sm[:, 1, :], scalar=2.5, in1=sm[:, 2, :],
                                          op0=ALU.mult, op1=ALU.add))
            prep(dve.tensor_scalar(sm[:, 3, :], sm[:, 3, :], 0.0, 5.0, ALU.max, ALU.min))
            prep(dve.tensor_scalar(sm[:, 3, :], sm[:, 3, :], 0.5, 1.0 / 1.5, ALU.subtract, ALU.mult))
            dve.tensor_scalar(sm[:, 3, :], sm[:, 3, :], 0.0, 1.0, ALU.max, ALU.min).then_inc(s_ga, 1)
            dve.wait_ge(s_gb, 1)
            prep(dve.scalar_tensor_tensor(out=sm[:, 5, :], in0=sm[:, 4, :], scalar=0.05, in1=sm[:, 4, :],
                                          op0=ALU.is_ge, op1=ALU.mult))
            dve.wait_ge(s_exw, TILES)
            prep(dve.reciprocal(sm[:, 6, :], wsum[:, :]))
            prep(dve.tensor_tensor(sm[:, 7, :], sm[:, 6, :], sm[:, 5, :], ALU.mult))
            for n in range(TILES):
                dve.tensor_scalar(asc[:, n, :], asc[:, n, :], sm[:, 7, n:n + 1], None, ALU.mult).then_inc(s_w8, 1)
            dve.wait_ge(s_fa, 1)
            for n in range(2 * KC):
                m, h = n // 2, n % 2
                sl = slice(HALF * h, HALF * h + HALF)
                dve.wait_ge(s_fo, n + 1)
                dve.tensor_tensor(hT[:, m, sl], bank(4 + n % 4), x2T[:, m, sl], ALU.add).then_inc(s_fin, 1)

        @block.tensor
        def _(pe):
            pe.wait_ge(s_masks, 1)
            pe.matmul(bank(7)[:, 0:B], lhsT=A("bsess", SESS), rhs=onehot[:, :], start=True, stop=True).then_inc(s_bias, 1)
            for j in range(2):
                pe.wait_ge(s_x, 32)

            def encoder_out(n, p):
                pe.wait_ge(s_g1, n + 1)
                for k in range(KC):
                    pe.matmul(bank(2 + k)[:, 2 * S * p:2 * S * p + 2 * S], lhsT=hbuf[:, p % 2, P * k:P * k + P],
                              rhs=A("w2"), start=True, stop=True).then_inc(s_co, 1)

            def encoder_half(h):
                for p in range(8):
                    n = 8 * h + p
                    pe.wait_ge(s_wst, n + 1)
                    if p >= 2:
                        pe.wait_ge(s_g1, n - 1)
                    pe.matmul(bank(p % 2), lhsT=wst[:, p % 2, :], rhs=xc[:, ds(n, 1), :].rearrange("p a n -> p (a n)"),
                              start=True, stop=True).then_inc(s_h1, 1)
                    if p >= 1:
                        encoder_out(n - 1, p - 1)
                encoder_out(8 * h + 7, 7)
                pe.wait_ge(s_cT, KC * h + KC)
                for k in range(KC):
                    mm = pe.matmul(bank(6), lhsT=A("wdown")[:, DM * k:DM * k + DM], rhs=condT[:, k, ds(HALF * h, HALF)],
                                   start=(k == 0), stop=(k == KC - 1))
                mm.then_inc(s_dn, 1)

            with pe.Fori(0, 2) as h:
                encoder_half(h)

            pe.wait_ge(s_pkb, 16)
            with pe.Fori(0, 2) as i:
                pe.wait_ge(s_u, i + 1)
                for n, w in enumerate([A("bcw"), A("xw")[:, 0:P], A("xw")[:, P:DIN]]):
                    rows = w.shape[1]
                    for h in range(2):
                        pe.matmul(bank(2 * n + h)[0:rows], lhsT=w, rhs=u[:, HALF * h:HALF * h + HALF],
                                  start=True, stop=True).then_inc(s_pr, 1)
                    if n == 0:
                        for m in range(TILES):
                            mm = pe.matmul(bank(6)[:, 8 * m:8 * m + 8], lhsT=u[:, P * m:P * m + P], rhs=A("dtw"),
                                           start=True, stop=True)
                        mm.then_inc(s_dtp, 1)
                for n in range(4):
                    pe.wait_ge(s_xp, 6 * i + n + 3)
                    c, h = n // 2, n % 2
                    pe.matmul(bank(2 + n), lhsT=A("zw")[:, P * c:P * c + P], rhs=u[:, HALF * h:HALF * h + HALF],
                              start=True, stop=True).then_inc(s_zp, 1)
                pe.wait_ge(s_R, 2 * i + 2)
                pe.wait_ge(s_xp, 6 * i + 2)
                for h in range(2):
                    for d, side in enumerate(("ufw", "ubw")):
                        mm = pe.matmul(bank(h), lhsT=A(side), rhs=Rm[:, d, 16 * h:16 * h + 16, :].rearrange("p a s -> p (a s)"),
                                       start=(d == 0), stop=(d == 1))
                    mm.then_inc(s_seg, 1)
                pe.wait_ge(s_xs, 4 * i + 2)
                pe.wait_ge(s_nv, i + 1)
                pe.wait_ge(s_zs, 4 * i + 4)
                for d in range(2):
                    for m in range(TILES):
                        mm = pe.matmul(bank((6, 4)[d] + m // 4)[:, P * (m % 4):P * (m % 4) + P], lhsT=Bt[:, P * m:P * m + P],
                                       rhs=Ct[:, P * m + 2 * d:P * m + 2 * d + P], start=True, stop=True)
                        if m % 4 == 3:
                            mm.then_inc(s_GG, 1)
                for n in range(4):
                    c, h = n // 2, n % 2
                    pe.wait_ge(s_xs, 4 * i + c + 3)
                    if n >= 2:
                        pe.wait_ge(s_xe, 4 * i + n - 1)
                    for m in range(4):
                        mm = pe.transpose(bank(2 + h)[:, P * m:P * m + P], xs[:, c, HALF * h + P * m:HALF * h + P * m + P],
                                          G("ident"))
                    mm.then_inc(s_xt, 1)
                pe.wait_ge(s_W, 16 * i + 16)
                for n in range(4):
                    c, h = n // 2, n % 2
                    for k in range(2):
                        mm = pe.matmul(bank(4 + n), lhsT=A("fcd")[:, DIN * k + P * c:DIN * k + P * c + P],
                                       rhs=xs[:, k, HALF * h:HALF * h + HALF], start=(k == 0), stop=(k == 1))
                    mm.then_inc(s_r, 1)
                pe.wait_ge(s_M, 4 * i + 4)
                pe.wait_ge(s_xe, 4 * i + 4)
                for n in range(4):
                    c, h = n // 2, n % 2
                    for m in range(4):
                        for q in range(2):
                            tile, head = 4 * h + m, 2 * c + q
                            mm = pe.matmul(bank(n)[64 * q:64 * q + 64, P * m:P * m + P],
                                           lhsT=xtok[:, tile, 64 * head:64 * head + 64], rhs=M[:, NH * tile + head, :],
                                           start=True, stop=True)
                    mm.then_inc(s_y, 1)
                pe.wait_ge(s_ysq, 2 * i + 2)
                pe.wait_ge(s_t, 4 * i + 4)
                for h in range(2):
                    for c in range(2):
                        mm = pe.matmul(bank(4 + h), lhsT=ones[:, :], rhs=cacc[:, c, HALF * h:HALF * h + HALF],
                                       start=(c == 0), stop=(c == 1))
                    mm.then_inc(s_ss0, 1)
                for h in range(2):
                    for c in range(2):
                        mm = pe.matmul(bank(6 + h), lhsT=outw[:, c, :], rhs=yb[:, c, HALF * h:HALF * h + HALF],
                                       start=(c == 0), stop=(c == 1))
                    mm.then_inc(s_hy, 1)
            pe.wait_ge(s_hf, 1)
            for n in range(2 * KC):
                h, k = n // KC, n % KC
                pe.matmul(bank(n), lhsT=A("wup")[:, P * k:P * k + P],
                          rhs=u[:, :].rearrange("p (s b) -> p b s", b=B)[:, 16 * h:16 * h + 16, :],
                          start=True, stop=True).then_inc(s_up, 1)

            def project(out, operands):
                for k in range(KC):
                    for a, b in ((0, 0), (0, 1), (1, 0)):
                        lhsT, rhs = operands(k, a, b)
                        mm = pe.matmul(out, lhsT=lhsT, rhs=rhs, start=(k == 0 and a + b == 0), stop=(k == KC - 1 and a == 1))
                mm.then_inc(s_pj, 1)

            def next_weights(n):
                pe.wait_ge(s_wh, n + 1)
                pe.wait_ge(s_wl, n + 1)

            def key_squares(n):
                pe.wait_ge(s_sq, n + 1)
                if n >= 2:
                    pe.wait_ge(s_kr1, n - 1)
                for c in range(4):
                    mm = pe.matmul(bank(6 + n % 2)[:, c:c + 1], lhsT=ksq[n % 2][:, P * c:P * c + P], rhs=mean_d[:, :],
                                   start=True, stop=True)
                mm.then_inc(s_ss, 1)

            def spread_key_scale(n):
                pe.wait_ge(s_kr2, n + 1)
                if n >= 2:
                    pe.wait_ge(s_po, n - 1)
                pe.matmul(bank(4 + n % 2), lhsT=ones[:, :], rhs=diag[n % 2].rearrange("p a c -> p (a c)"),
                          start=True, stop=True).then_inc(s_kb, 1)

            for n in range(KTILES):
                h, c = n // 4 % 2, P * (n % 4)
                if n % WTILES == 0:
                    next_weights(n // WTILES)
                if n in (0, 4):
                    pe.wait_ge(s_xl, n + KC)
                if n >= 4:
                    pe.wait_ge(s_sq, n - 3)
                    pe.wait_ge(s_ab, n - 3)
                project(bank(n % 4), lambda k, a, b: (w16[:, n // WTILES, a, k, c:c + P],
                                                      x16[:, b, k, HALF * h:HALF * h + HALF]))
                if n >= 1:
                    key_squares(n - 1)
                if n >= 2:
                    spread_key_scale(n - 2)
            key_squares(KTILES - 1)
            spread_key_scale(KTILES - 2)
            spread_key_scale(KTILES - 1)
            for n in range(VTILES):
                m = n % TILES
                if n % WTILES == 0:
                    next_weights(2 + n // WTILES)
                if n < 4:
                    pe.wait_ge(s_sq, KTILES - 3 + n)
                    pe.wait_ge(s_ab, KTILES - 3 + n)
                else:
                    pe.wait_ge(s_ve, n - 3)
                project(bank(n % 4), lambda k, a, b: (x16[:, a, k, P * m:P * m + P], w16[:, n // WTILES, b, k, :]))
            pe.wait_ge(s_ve, VTILES)
            pe.wait_ge(s_kr1, KTILES)

            def query_squares(i, m, part):
                h = m % 2
                if part == 0:
                    pe.wait_ge(s_sq, KTILES + QTILES * i + 4 * m + 4)
                for b in range(4 * part, 4 * part + 4):
                    c = 2 * i + (HK * (16 * h + b) + m // 2)
                    mm = pe.matmul(bank(7)[:, c:c + 1] if isinstance(i, int) else bank(7)[:, ds(c, 1)],
                                   lhsT=sqr[h][:, b].rearrange("p r s -> p (r s)"), rhs=mean_d[:, :], start=True, stop=True)
                if part == 3:
                    mm.then_inc(s_ss, 1)

            def pe_queries(i):
                for n in range(QTILES):
                    sl, m = n // WTILES, n // 4
                    h, c = m % 2, P * (n % 4)
                    if n % WTILES == 0:
                        next_weights(4 + 2 * i + sl)
                    pe.wait_ge(s_sq, KTILES + QTILES * i + n - 3)
                    pe.wait_ge(s_ab, KTILES + QTILES * i + n - 3)
                    project(bank(n % 4), lambda k, a, b: (w16[:, sl, a, k, c:c + P], x16[:, b, k, HALF * h:HALF * h + HALF]))
                    if m > 0:
                        query_squares(i, m - 1, n % 4)
                    elif not isinstance(i, int) or i > 0:
                        query_squares(i - 1, 3, n % 4)

            pe_queries(0)
            with pe.Fori(1, QTURNS - 1) as i:
                pe_queries(i)
            pe_queries(QTURNS - 1)
            for part in range(4):
                query_squares(QTURNS - 1, 3, part)

            def scores(n, b, j):
                par, g = j // 8 % 2, j % 8
                turn = b // 2 if isinstance(b, int) else None
                if g == 0:
                    pe.wait_ge(s_in[par], 32 * (b // 2) + 32 if isinstance(b, int) else 16 * b + 32 - 16 * par)
                    pe.wait_ge(s_kc, NPP * b + NPP)
                after(pe, s_mx, n - 1)
                q = qring[:, par, P * g:P * g + P]
                s = score(j)
                pe.matmul(s[:, 0:LC].rearrange("p (a c) -> p a c", c=S), lhsT=q,
                          rhs=kring[:, par, 0:NPP, S * g:S * g + S], start=True, stop=True)
                pe.matmul(s[:, LC:LK], lhsT=q, rhs=kring[:, par, NPP, S * g:S * g + S], start=True, stop=True).then_inc(s_sc, 1)

            def transposes(n, j):
                slot = j % 4
                pe.wait_ge(s_pn, n + 1)
                after(pe, s_pt, n - 1)
                after(pe, s_ov, n - 1)
                pe.transpose(bank(6 + j % 2)[0:S, P:2 * P], prob[:, slot, LC:LK], G("ident"))
                for c in range(BPT):
                    mm = pe.transpose(bank(4 + j % 2)[:, P * c:P * c + P], prob[:, slot, P * c:P * c + P], G("ident"))
                mm.then_inc(s_tp, 1)

            def weighted(n, b, j):
                par, g = j // 8 % 2, j % 8
                if g == 0:
                    per = 16 * (NPP + 1)
                    pe.wait_ge(s_v[par], per * (b // 2) + per if isinstance(b, int) else (per // 2) * b + per - (per // 2) * par)
                pe.wait_ge(s_pt, n + 1)
                pe.wait_ge(s_p4, n + 1)
                o = bank(6 + j % 2)[:, 0:P]
                for c in range(BPT):
                    pe.matmul(o, lhsT=vring[:, par, c, D * g:D * g + D], rhs=pT[:, j % 2, P * c:P * c + P],
                              start=(c == 0), stop=False)
                pe.matmul(o, lhsT=vring[0:S, par, BPT, D * g:D * g + D], rhs=pT4[:, j % 2, :],
                          start=False, stop=True).then_inc(s_pv, 1)

            for n in range(3):
                scores(n, 0, n)

            def pe_turn(i):
                for j in range(16):
                    n = 16 * i + j
                    first = isinstance(i, int) and n == 0
                    transposes(n, j)
                    if not first:
                        jj = (j - 1) % 16
                        weighted(n - 1, 2 * i + jj // 8 if j > 0 else 2 * i - 1, jj)
                    if not (isinstance(i, int) and n + 3 >= UNITS):
                        scores(n + 3, 2 * i + (j + 3) // 8, j + 3)

            pe_turn(0)
            with pe.Fori(1, 15) as i:
                pe_turn(i)
            pe_turn(15)
            weighted(UNITS - 1, B - 1, 15)

            pe.wait_ge(s_wo, 16)
            pe.wait_ge(s_ov, UNITS)
            pe.wait_ge(s_pt, UNITS)

            def turn_tokens(n):
                pe.wait_ge(s_ht, n + 1)
                if n >= 2:
                    pe.wait_ge(s_hT, n - 1)
                for k in range(KC):
                    mm = pe.transpose(bank(2 + n % 2)[:, P * k:P * k + P], htok[:, n, P * k:P * k + P], G("ident"))
                mm.then_inc(s_htt, 1)

            for n in range(TILES):
                pe.wait_ge(s_op, n + 1)
                if n >= 2:
                    pe.wait_ge(s_ht, n - 1)
                for h in range(HQ):
                    mm = pe.matmul(bank(n % 2), lhsT=operm[:, n % 2, h].rearrange("p b s -> p (b s)"), rhs=wo[:, h, :],
                                   start=(h == 0), stop=(h == HQ - 1))
                mm.then_inc(s_hp, 1)
                if n >= 1:
                    turn_tokens(n - 1)
            turn_tokens(TILES - 1)
            pe.wait_ge(s_pkc, 16)
            pe.matmul(bank(4)[0:RDIM, 0:NSLOT], lhsT=C("fwr", BOT), rhs=C("fkeys", BOT), start=True, stop=True).then_inc(s_fp, 1)
            for k in range(KC):
                mm = pe.matmul(bank(5)[:, 0:VB], lhsT=C("fval")[:, NSLOT * k:NSLOT * k + NSLOT], rhs=C("fwvd")[:, VB * k:VB * k + VB],
                               start=(k == 0), stop=(k == KC - 1))
            mm.then_inc(s_fp, 1)
            pe.wait_ge(s_hT, TILES)
            for h in range(2):
                for k in range(KC):
                    mm = pe.matmul(bank(h)[0:BOT], lhsT=C("fwq")[:, BOT * k:BOT * k + BOT], rhs=hT[:, k, HALF * h:HALF * h + HALF],
                                   start=(k == 0), stop=(k == KC - 1))
                mm.then_inc(s_fp, 1)
            for h in range(2):
                pe.wait_ge(s_fe, 3 + h)
                pe.matmul(bank(2 + h)[0:RDIM], lhsT=C("fwr", BOT), rhs=queryT[:, HALF * h:HALF * h + HALF],
                          start=True, stop=True).then_inc(s_fp, 1)
            for h in range(2):
                for k in range(KC):
                    mm = pe.matmul(bank(6 + h), lhsT=C("fwu1")[:, P * k:P * k + P], rhs=hT[:, k, HALF * h:HALF * h + HALF],
                                   start=(k == 0), stop=(k == KC - 1))
                mm.then_inc(s_fp, 1)
            for m in range(2):
                pe.wait_ge(s_fe, 5 + m)
                for n in range(4):
                    tile = 4 * m + n
                    mm = pe.matmul(bank(4 + m)[:, P * n:P * n + P], lhsT=rqT[:, P * tile:P * tile + P], rhs=rkT[:, :],
                                   start=True, stop=True)
                mm.then_inc(s_rsp, 1)
            for m in range(2):
                for n in range(4):
                    tile = 4 * m + n
                    mm = pe.matmul(bank(m)[:, P * n:P * n + P], lhsT=queryT[:, P * tile:P * tile + P], rhs=C("fkeys", BOT),
                                   start=True, stop=True)
                mm.then_inc(s_asp, 1)
            pe.wait_ge(s_fe, 8)
            for n in range(TILES):
                mm = pe.matmul(bank(6)[:, n:n + 1], lhsT=uT[:, P * n:P * n + P], rhs=C("fwu2"), start=True, stop=True)
            mm.then_inc(s_ler, 1)
            pe.wait_ge(s_lv, 1)
            pe.matmul(bank(7)[:, 0:1], lhsT=ones[:, :], rhs=lsum[:, 0:1], start=True, stop=True).then_inc(s_mean, 1)
            for m in range(2):
                for n in range(4):
                    tile = 4 * m + n
                    pe.wait_ge(s_w8, tile + 1)
                    mm = pe.transpose(bank(2 + m)[:, P * n:P * n + P], asc[:, tile, :], G("ident"))
                mm.then_inc(s_wt, 1)
            for h in range(2):
                pe.wait_ge(s_wte, h + 1)
                pe.matmul(bank(h)[0:VB], lhsT=AV[:, :], rhs=wTs[:, HALF * h:HALF * h + HALF], start=True, stop=True).then_inc(s_ax, 1)
            pe.wait_ge(s_axe, 2)
            pe.wait_ge(s_ga, 1)
            for n in range(2 * KC):
                m, h = n // 2, n % 2
                if n >= 4:
                    pe.wait_ge(s_fin, n - 3)
                pe.matmul(bank(4 + n % 4), lhsT=C("fwvu", VB)[:, P * m:P * m + P], rhs=auxT[:, HALF * h:HALF * h + HALF],
                          start=True, stop=True).then_inc(s_fo, 1)


def kernel(x, itok_B_0_7, itok_B_2182_4065, itok_Bx16_0_63, itok_B_207_1644, _lenS, L0_cond_W_sess, L0_cond_b_sess,
           L0_cond_W2, L0_cond_b2, L0_attn_w_down, L0_attn_b_down, L0_attn_w_up, L0_attn_b_up, L0_attn_gate1,
           L0_attn_hy_in_w, L0_attn_hy_conv_w, L0_attn_hy_conv_b, L0_attn_hy_dt_bias, L0_attn_hy_A_log, L0_attn_hy_D,
           L0_attn_hy_fcD_w, L0_attn_hy_norm_w, L0_attn_hy_out_w, L0_cond2_Wq, L0_cond2_Wk, L0_cond2_Wv, L0_cond2_Wo,
           L0_cond2_q_norm_w, L0_cond2_k_norm_w, L0_cond2_k_cache, L0_cond2_v_cache, L0_ffn_Wq, L0_ffn_Wr,
           L0_ffn_aux_keys, L0_ffn_aux_values, L0_ffn_Wvd, L0_ffn_Wvu, L0_ffn_Wu1, L0_ffn_bu1, L0_ffn_Wu2, L0_ffn_bu2,
           L0_ffn_gate_w1, L0_ffn_gate_bias, L0_ffn_log_rel):
    import concourse.bacc as bacc
    from concourse.bass_utils import run_bass_kernel_spmd

    f = np.float32

    def rows(a):
        a = np.asarray(a)
        return a.reshape(-1, P, a.shape[1]).transpose(1, 0, 2).reshape(P, -1)

    def every(a):
        a = np.asarray(a).reshape(1, -1)
        return np.broadcast_to(a, (P, a.shape[1]))

    def pack(cols, total, parts):
        out = np.zeros((P, total), f)
        for name, (at, n) in cols.items():
            a = np.asarray(parts[name])
            assert a.shape[1] == n, (name, a.shape, n)
            out[:a.shape[0], at:at + n] = a
        return out

    p = np.arange(P)
    conv = np.asarray(L0_attn_hy_conv_w)[:, 0, :]
    cb = np.asarray(L0_attn_hy_conv_b).reshape(-1, 1)
    inw = np.asarray(L0_attn_hy_in_w).T
    o = DIN

    def spread(a):
        out = np.zeros((3 * DST, a.shape[1]), f)
        out[0:DST], out[2 * DST:] = a[0:DST], a[DST:]
        return out

    same = p[:, None] // S == p[None, :] // S
    w2 = np.zeros((P, 2 * S), f)
    w2[0:CHID, 0:S] = w2[CHID:, S:] = np.asarray(L0_cond_W2)
    parts_a = {
        "sessidx": p[:, None], "chan": (p % S)[:, None], "tcol": p[:, None] + P * np.arange(KC)[None, :],
        "bsess": np.concatenate([np.asarray(L0_cond_b_sess)] * 2, 1), "w2": w2, "b2": every(L0_cond_b2),
        "wdown": rows(np.asarray(L0_attn_w_down).T), "bdown": np.asarray(L0_attn_b_down)[:, None],
        "srow": every(np.arange(S)),
        "invf": np.tile(1.0 / THETA ** (np.arange(0, D, 2, dtype=f) / D), 2)[:, None],
        "sign": np.where(p < 64, 1 / WSCALE, -1 / WSCALE)[:, None],
        "qnw": np.asarray(L0_cond2_q_norm_w)[:, None], "knw": np.asarray(L0_cond2_k_norm_w)[:, None],
        "zw": inw[:, 0:o], "xw": inw[:, o:2 * o], "bcw": spread(inw[:, 2 * o:2 * o + 2 * DST].T).T,
        "dtw": inw[:, 2 * o + 2 * DST:], "convx": rows(conv[0:o]), "convbc": spread(conv[o:]),
        "convbx": rows(cb[0:o]), "convbbc": spread(cb[o:]),
        "dtb": every(np.concatenate([np.asarray(L0_attn_hy_dt_bias)] * 2)), "alog": every(L0_attn_hy_A_log),
        "dskip": rows(np.repeat(np.asarray(L0_attn_hy_D), 64)[:, None]),
        "fcd": rows(np.repeat(np.asarray(L0_attn_hy_fcD_w), 64, axis=0).T),
        "normw": rows(np.asarray(L0_attn_hy_norm_w)[:, None]), "outw": rows(np.asarray(L0_attn_hy_out_w).T),
        "wup": np.asarray(L0_attn_w_up).T, "bup": rows(np.asarray(L0_attn_b_up)[:, None]),
        "gate1": every(L0_attn_gate1),
        "ufw": same & (p[:, None] > p[None, :]), "ubw": same & (p[:, None] < p[None, :]),
        "before": (p % S)[:, None] < np.arange(S)[None, :], "after": (p % S)[:, None] > np.arange(S)[None, :],
    }
    parts_b = {
        "ident": np.eye(P), "iota": every(np.arange(LC)),
    }
    parts_c = {
        "fwq": rows(np.asarray(L0_ffn_Wq).T), "fwr": np.asarray(L0_ffn_Wr).T, "fkeys": np.asarray(L0_ffn_aux_keys).T,
        "flog": every(L0_ffn_log_rel), "fval": rows(np.asarray(L0_ffn_aux_values).T), "fwvd": rows(np.asarray(L0_ffn_Wvd).T),
        "fwvu": np.asarray(L0_ffn_Wvu).T, "fwu1": rows(np.asarray(L0_ffn_Wu1).T), "fbu1": np.asarray(L0_ffn_bu1)[:, None],
        "fwu2": np.asarray(L0_ffn_Wu2).T, "fbu2": every(L0_ffn_bu2), "fgw": every(L0_ffn_gate_w1),
        "fgb": every(L0_ffn_gate_bias),
    }
    xf = np.asarray(x)
    ints = np.concatenate([np.asarray(a) for a in (itok_B_0_7, _lenS, itok_B_2182_4065, itok_B_207_1644)])
    ins = {
        "x": xf, "xT": xf.reshape(TOK, HID).T, "ints": np.broadcast_to(ints[None, :], (P, INTS)),
        "table": np.asarray(itok_Bx16_0_63).reshape(1, -1), "wsess": np.asarray(L0_cond_W_sess),
        "packa": pack(COL_A, COLS_A, parts_a), "packb": pack(COL_B, COLS_B, parts_b),
        "packc": pack(COL_C, COLS_C, parts_c),
        "wqT": np.asarray(L0_cond2_Wq).T, "wkT": np.asarray(L0_cond2_Wk).T, "wvT": np.asarray(L0_cond2_Wv).T,
        "woT": np.asarray(L0_cond2_Wo).T, "kcT": np.asarray(L0_cond2_k_cache).transpose(3, 0, 2, 1),
        "vc": np.asarray(L0_cond2_v_cache),
    }
    ins = {k: np.ascontiguousarray(v) for k, v in ins.items()}
    nc = bacc.Bacc("TRN2", target_bir_lowering=False, num_devices=1)
    t = {k: nc.dram_tensor(f"in_{k}", v.shape, mybir.dt.from_np(v.dtype), kind="ExternalInput").ap() for k, v in ins.items()}
    for k, shape in (("q_s", (B, D, HQ * S)), ("k_s", (B, D, HK * S)), ("v_s", (TOK, HK * D)), ("o_s", (B, D, HQ * S))):
        t[k] = nc.dram_tensor(k, shape, F32, kind="Internal").ap()
    t["out"] = nc.dram_tensor("out", (HID, TOK), F32, kind="ExternalOutput").ap()
    adaln_attention_ffn(nc, t)
    r = run_bass_kernel_spmd(nc, [{f"in_{k}": v for k, v in ins.items()}], core_ids=[0])
    return np.ascontiguousarray(r.results[0]["out"].T).reshape(B, S, HID)
```

```python
from contextlib import ExitStack

import numpy as np
import concourse.bass as bass
from concourse import mybir

F32 = mybir.dt.float32
F16 = mybir.dt.float16
I32 = mybir.dt.int32
ACT = mybir.ActivationFunctionType
ALU = mybir.AluOpType
AXX = mybir.AxisListType.X
SP = mybir.EngineType.SP
ds = bass.ds

P = 128
B, S, HID = 32, 32, 512
TOK = B * S
HALF = TOK // 2
KC = HID // P
SESS, CHID = 8, 64
DM, DIN, DST, NH, DCONV = 128, 256, 16, 4, 7
PADL = S + DCONV - 1
D, HQ, HK = 128, 32, 8
REP = HQ // HK
PAGES, NPP = 64, 16
LC = NPP * S
LK = LC + S
BOT, RDIM, NSLOT, TOPK, VB = 64, 48, 128, 8, 32
SCALE = 1.0 / float(np.sqrt(D))
THETA = 10000.0
TILES = TOK // P
BPT = P // S

PACK_A = [
    ("sessidx", 1), ("chan", 1), ("tcol", KC), ("bsess", P), ("w2", 2 * S), ("b2", S),
    ("wdown", KC * DM), ("bdown", 1), ("srow", S), ("invf", 1), ("sign", 1), ("qnw", 1), ("knw", 1),
    ("dtw", 2 * NH), ("bcw", 3 * DST), ("xw", DIN), ("zw", DIN), ("convx", 2 * DCONV),
    ("convbc", DCONV), ("convbx", 2), ("convbbc", 1), ("dtb", 2 * NH), ("alog", NH), ("dskip", 2),
    ("fcd", 2 * DIN), ("normw", 2), ("outw", 2 * DM), ("wup", HID), ("bup", KC), ("gate1", 1),
    ("ufw", P), ("ubw", P), ("before", S), ("after", S),
]
PACK_B = [
    ("ident", P), ("iota", LC),
]
PACK_C = [
    ("fwq", KC * BOT), ("fwr", RDIM), ("fkeys", NSLOT), ("flog", NSLOT), ("fval", KC * NSLOT),
    ("fwvd", KC * VB), ("fwvu", HID), ("fwu1", KC * P), ("fbu1", 1), ("fwu2", 1), ("fbu2", 1),
    ("fgw", 1), ("fgb", 1),
]


def columns(pack):
    at, out = 0, {}
    for name, n in pack:
        out[name] = (at, n)
        at += n
    return out, at


COL_A, COLS_A = columns(PACK_A)
COL_B, COLS_B = columns(PACK_B)
COL_C, COLS_C = columns(PACK_C)

PI2_A, PI2_B = 6.28125, 0.0019350051879882812
PI2_C = float(2 * np.pi - PI2_A - PI2_B)
ROUND = 12582912.0
PI = 3.1415925
NEG = -1e30
EPS_HYDRA, EPS_QK = 1e-5, 1e-6
INTS = 4 * B
NPAIR = B // 2
NCHAIN = 38
KTILES, VTILES, QTILES = 16, 16, 16
WCOLS = 512
WTILES = 8
WSCALE = 256.0
QTURNS = 4
WSLOTS = [("wkT", n) for n in range(2)] + [("wvT", n) for n in range(2)] + [("wqT", n) for n in range(HK)]
UNITS = B * HK


def encoder_attention_memory(nc, t):
    with ExitStack() as ctx:
        def sem(name):
            return ctx.enter_context(nc.semaphore(name))

        def sb(stack, name, shape, dt=F32):
            return stack.enter_context(nc.sbuf_tensor(name, shape, dt))

        psum = ctx.enter_context(nc.psum_tensor("psum", [P, 8, 512], F32))

        def bank(n):
            return psum[:, n, :]

        pkb = sb(ctx, "pkb", [P, COLS_B])
        x2T = sb(ctx, "x2T", [P, KC, TOK])
        ints = sb(ctx, "ints", [P, INTS], I32)
        intf = sb(ctx, "intf", [P, INTS])
        table = sb(ctx, "table", [1, B * NPP], I32)
        ones = sb(ctx, "ones", [P, P])
        mean_d = sb(ctx, "mean_d", [P, 1])
        eps_qk = sb(ctx, "eps_qk", [P, 1])
        rq = sb(ctx, "rq", [P, B * HK])
        nrq = sb(ctx, "nrq", [P, B * HK])
        with ExitStack() as c1:
            wland = sb(c1, "wland", [P, 2, KC, WCOLS])
            w16 = sb(c1, "w16", [P, 2, 2, KC, WCOLS], F16)
            tabs = sb(c1, "tabs", [P, 4, TOK])
            with ExitStack() as s1:
                pka = sb(s1, "pka", [P, COLS_A])
                xmid = sb(s1, "xmid", [P, TOK])
                u = sb(s1, "u", [P, TOK])
                negA = sb(s1, "negA", [P, NH])
                outw = sb(s1, "outw", [P, 2, DM])
                alpha = sb(s1, "alpha", [P, 3])
                with ExitStack() as st:
                    xc = sb(st, "xc", [2 * S, NPAIR, HID])
                    wgat = sb(st, "wgat", [2 * S, NPAIR, P])
                    xs16 = sb(st, "xs16", [P, NPAIR, HID], F16)
                    whi = sb(st, "whi", [P, 2, P], F16)
                    wlo = sb(st, "wlo", [2 * S, 2, P], F16)
                    cmask = sb(st, "cmask", [2 * S, NPAIR])
                    tmask = sb(st, "tmask", [P, KC, B])
                    onehot = sb(st, "onehot", [SESS, B])
                    bias1 = sb(st, "bias1", [P, NPAIR])
                    hbuf = sb(st, "hbuf", [P, 2, HID])
                    condT = sb(st, "condT", [P, KC, TOK])
                    ang = sb(st, "ang", [P, TOK])
                    turns = sb(st, "turns", [P, 2, TOK])
                with ExitStack() as st:
                    xpad = sb(st, "xpad", [P, 2, S, PADL])
                    bcpad = sb(st, "bcpad", [3 * DST, S, PADL])
                    cacc = sb(st, "cacc", [P, 3, TOK])
                    xs = sb(st, "xs", [P, 2, TOK])
                    Bt = sb(st, "Bt", [DST, TOK])
                    Ct = sb(st, "Ct", [DST, TOK + 2])
                    zs = sb(st, "zs", [P, 2, TOK])
                    xtok = sb(st, "xtok", [P, TILES, DIN])
                    dtv = sb(st, "dtv", [P, 5, TILES * 2 * NH])
                    dtd = sb(st, "dtd", [P, 4, TILES * NH])
                    Rm = sb(st, "Rm", [P, 2, TILES * NH, S])
                    E = sb(st, "E", [P, TILES * NH, S])
                    W12 = sb(st, "W12", [P, 2, TILES, S])
                    M = sb(st, "M", [P, TILES * NH, P])
                    yb = sb(st, "yb", [P, 2, TOK])
                    rb = sb(st, "rb", [P, 2, HALF])
            T12 = Rm
            with ExitStack() as st:
                KT = sb(st, "KT", [P, PAGES * HK * S])
                x16 = sb(st, "x16", [P, 2, KC, TOK], F16)
                stage = sb(st, "stage", [P, 4, REP * HALF])
                ab = sb(st, "ab", [P, 3, 2, HALF])
                kms = sb(st, "kms", [P, KTILES, 4])
                vo = sb(st, "vo", [P, 4, WCOLS])
        with ExitStack() as st:
            kring = sb(st, "kring", [P, 2, NPP + 1, HK * S])
            mask = sb(st, "mask", [P, LK])
            sb(st, "gap", [P, 4 * KC * WCOLS + 4 * TOK - 2 * (NPP + 1) * HK * S - 2 * HQ * S - LK])
            q16 = sb(st, "q16", [P, 2, 2, HQ * S], F16)
            sb(st, "KT_place", [P, PAGES * HK * S])
            vring = sb(st, "vring", [P, 2, BPT + 1, HK * D])
            oring = sb(st, "oring", [P, 2, HQ * S])
            prob = sb(st, "prob", [P, 4, LK])
            pT = sb(st, "pT", [P, 2, LC])
            pT4 = sb(st, "pT4", [S, 2, P])
            mx = sb(st, "mx", [P, 4])
            nb = sb(st, "nb", [P, 4])
            rs = sb(st, "rs", [P, 4])
            ri = sb(st, "ri", [P, 4])
            qland = sb(st, "qland", [P, HQ * S])
            kland = sb(st, "kland", [P, HK * S])
        with ExitStack() as st:
            oland = sb(st, "oland", [P, 2, B, REP * S])
            wol1 = sb(st, "wol1", [P, REP, HID])
            bn = sb(st, "bn", [P, TILES, 6])
            mv = sb(st, "mv", [P, TILES, 2])
            sb(st, "gap2", [P, 4 * KC * WCOLS + 4 * TOK - 2 * B * REP * S - REP * HID - 8 * TILES])
            o16 = sb(st, "o16", [P, 2, 2, REP, TOK], F16)
            wo16 = sb(st, "wo16", [P, 2, 2, REP, HID], F16)
            htok = sb(st, "htok", [P, TILES, HID])
            hT = sb(st, "hT", [P, KC, TOK])
            pkc = sb(st, "pkc", [P, COLS_C])
            queryT = sb(st, "queryT", [BOT, TOK])
            rqT = sb(st, "rqT", [RDIM, TOK])
            rkT = sb(st, "rkT", [RDIM, NSLOT])
            AV = sb(st, "AV", [NSLOT, VB])
            uT = sb(st, "uT", [P, TOK])
            rsc = sb(st, "rsc", [P, TILES, NSLOT])
            rep8 = sb(st, "rep8", [P, TILES, NSLOT])
            asc = sb(st, "asc", [P, TILES, NSLOT])
            top8 = sb(st, "top8", [P, TILES, TOPK])
            amx = sb(st, "amx", [P, TILES])
            wsum = sb(st, "wsum", [P, TILES])
            sm = sb(st, "sm", [P, 10, TILES])
            lsum = sb(st, "lsum", [P, 2])
            wTs = sb(st, "wTs", [NSLOT, TOK])
            aux16 = sb(st, "aux16", [3 * VB, TOK], F16)
            wvu16 = sb(st, "wvu16", [3 * VB, HID], F16)
        wolands = [htok[:, 0:REP, :], wol1[:, :, :]]
        K16 = KT[:, :].bitcast(F16).rearrange("p (a l n) -> p a l n", l=2, n=HK * S)
        kring16 = kring[:, :, :, :].rearrange("p r a n -> p (r a n)").bitcast(F16).rearrange(
            "p (r a l n) -> p r a l n", r=2, l=2, n=HK * S)

        def A(name, rows=P, lo=0):
            a, n = COL_A[name]
            return pka[lo:lo + rows, a:a + n]

        def G(name, rows=P, lo=0):
            a, n = COL_B[name]
            return pkb[lo:lo + rows, a:a + n]

        def C(name, rows=P, lo=0):
            a, n = COL_C[name]
            return pkc[lo:lo + rows, a:a + n]

        s_pka, s_pkb, s_x, s_ids, s_xT = sem("s_pka"), sem("s_pkb"), sem("s_x"), sem("s_ids"), sem("s_xT")
        s_wz = sem("s_wz")
        s_gather = [sem(f"s_gather{q}") for q in range(4)]
        s_prep, s_bias = sem("s_prep"), sem("s_bias")
        s_xsp = sem("s_xsp")
        s_masks = sem("s_masks")
        s_wst = sem("s_wst")
        s_h1, s_g1 = sem("s_h1"), sem("s_g1")
        s_co, s_cT = sem("s_co"), sem("s_cT")
        s_dn, s_xm = sem("s_dn"), sem("s_xm")
        s_xc = sem("s_xc")
        s_ang, s_sin, s_tab = sem("s_ang"), sem("s_sin"), sem("s_tab")
        s_hz = sem("s_hz")
        s_u = sem("s_u")
        s_hd = sem("s_hd")
        s_pr, s_xp = sem("s_pr"), sem("s_xp")
        s_dtp, s_nv, s_ey = sem("s_dtp"), sem("s_nv"), sem("s_ey")
        s_tap, s_cp = sem("s_tap"), sem("s_cp")
        s_zp, s_zs, s_cv, s_xs = sem("s_zp"), sem("s_zs"), sem("s_cv"), sem("s_xs")
        s_R, s_seg, s_E, s_GG, s_W = sem("s_R"), sem("s_seg"), sem("s_E"), sem("s_GG"), sem("s_W")
        s_xt, s_xe, s_T, s_M = sem("s_xt"), sem("s_xe"), sem("s_T"), sem("s_M")
        s_r, s_t, s_y, s_yz, s_ysq = sem("s_r"), sem("s_t"), sem("s_y"), sem("s_yz"), sem("s_ysq")
        s_ss0, s_rr, s_rb, s_hy = sem("s_ss0"), sem("s_rr"), sem("s_rb"), sem("s_hy")
        s_al, s_hf, s_up, s_x2 = sem("s_al"), sem("s_hf"), sem("s_up"), sem("s_x2")
        s_w, s_wh, s_wl = [sem("s_w0"), sem("s_w1")], sem("s_wh"), sem("s_wl")
        s_xh, s_xl, s_pkc = sem("s_xh"), sem("s_xl"), sem("s_pkc")
        s_pj, s_sq, s_ab, s_po, s_ss = sem("s_pj"), sem("s_sq"), sem("s_ab"), sem("s_po"), sem("s_ss")
        s_add, s_kr1, s_kr2, s_kb = sem("s_add"), sem("s_kr1"), sem("s_kr2"), sem("s_kb")
        s_kst, s_qst = sem("s_kst"), [sem("s_qst0"), sem("s_qst1")]
        s_ve, s_vst = sem("s_ve"), [sem("s_vst0"), sem("s_vst1"), sem("s_vst2"), sem("s_vst3")]
        s_rms = sem("s_rms")
        s_KT, s_in, s_v = [sem(f"s_KT{n}") for n in range(4)], sem("s_in"), [sem("s_v0"), sem("s_v1")]
        s_kh, s_kl, s_qh, s_ql = sem("s_kh"), sem("s_kl"), sem("s_qh"), sem("s_ql")
        s_kc, s_msk = sem("s_kc"), sem("s_msk")
        s_sc, s_mx, s_nb, s_ex = sem("s_sc"), sem("s_mx"), sem("s_nb"), sem("s_ex")
        s_rc, s_pn, s_tp, s_pt, s_p4 = sem("s_rc"), sem("s_pn"), sem("s_tp"), sem("s_pt"), sem("s_p4")
        s_pv, s_ov, s_t4 = sem("s_pv"), sem("s_ov"), sem("s_t4")
        s_ost = [sem("s_ost0"), sem("s_ost1")]
        s_wo = [sem("s_wo0"), sem("s_wo1")]
        s_oin, s_oin2 = [sem("s_oin0"), sem("s_oin1")], [sem("s_oin20"), sem("s_oin21")]
        s_woh, s_wol, s_oh, s_ol, s_hg = sem("s_woh"), sem("s_wol"), sem("s_oh"), sem("s_ol"), sem("s_hg")
        s_hp, s_ht, s_htt, s_hT, s_bn = sem("s_hp"), sem("s_ht"), sem("s_htt"), sem("s_hT"), sem("s_bn")
        s_fp, s_fe, s_fa = sem("s_fp"), sem("s_fe"), sem("s_fa")
        s_rsp, s_rse, s_asp, s_ase = sem("s_rsp"), sem("s_rse"), sem("s_asp"), sem("s_ase")
        s_ler, s_am, s_exw, s_w8, s_wt, s_wte = sem("s_ler"), sem("s_am"), sem("s_exw"), sem("s_w8"), sem("s_wt"), sem("s_wte")
        s_lv, s_sg, s_ga, s_gb = sem("s_lv"), sem("s_sg"), sem("s_ga"), sem("s_gb")
        s_ax, s_axe, s_fo, s_fin, s_out = sem("s_ax"), sem("s_axe"), sem("s_fo"), sem("s_fin"), sem("s_out")
        s_top, s_wvh, s_wvl, s_axl = sem("s_top"), sem("s_wvh"), sem("s_wvl"), sem("s_axl")
        s_mean = sem("s_mean")
        s_seen = sem("s_seen")

        block = ctx.enter_context(nc.Block())

        def after(eng, sem, value):
            if not isinstance(value, int) or value > 0:
                eng.wait_ge(sem, value)

        def page_number(eng, b, n):
            return eng.value_load(table[0:1, ds(NPP * b + n, 1)], min_val=0, max_val=PAGES - 1)

        def bc(ap, axis, shape):
            return ap.unsqueeze(axis).to_broadcast(shape)

        def score(j):
            return psum[:, 2 * (j % 2):2 * (j % 2) + 2, :].rearrange("p a n -> p (a n)")[:, 0:LK]

        def by_batch(ap):
            return ap.rearrange("p (b s) -> p b s", s=S)

        taps = [yb[:, n, :].rearrange("p (a s) -> p a s", s=S) for n in range(2)] + \
            [xtok[:, 4 * n:4 * n + 4, :].rearrange("p a (b s) -> p (a b) s", s=S) for n in range(2)]
        ko = [stage[:, 2 * h:2 * h + 2, :].rearrange("p a n -> p (a n)").rearrange("p (b g s) -> p b g s", g=HK, s=S)
              for h in range(2)]
        sqr = [stage[:, n, :].rearrange("p (b r s) -> p b r s", r=REP, s=S) for n in range(2)]
        qor = [stage[:, 2 + n, :].rearrange("p (b r s) -> p b r s", r=REP, s=S) for n in range(2)]
        ksq = [vo[:, n, :] for n in range(2)]
        diag = [vo[:, 2 + n, :].rearrange("p (a c) -> p a c", c=P) for n in range(2)]

        EARLY = P * (HK - 2)

        def start_load(eng, b):
            eng.dma_start(qland[:, :], t["q_s"][ds(b, 1)].rearrange("a p n -> p (a n)")).then_inc(s_in, 16)
            eng.dma_start(kland[:, :], t["k_s"][ds(b, 1)].rearrange("a p n -> p (a n)")).then_inc(s_in, 16)

        def landed(par, h):
            return oland[:, par, B // 2 * h:B // 2 * (h + 1)].rearrange("p b (r s) -> p b r s", r=REP)

        def head_major(part, h):
            return part[:, :, HALF * h:HALF * h + HALF].rearrange("p r (b s) -> p b r s", s=S)

        def gather(eng, j, q):
            with eng.Fori(4 * q, 4 * q + 4) as p:
                sid = eng.value_load(ints[0:1, ds(2 * p + j, 1)], min_val=0, max_val=SESS - 1)
                eng.dma_start(wgat[S * j:S * j + S, ds(p, 1), CHID * j:CHID * j + CHID],
                              t["wsess"][ds(sid, 1), :, :].rearrange("a c h -> c a h")).then_inc(s_gather[q], 16)

        @block.sync
        def _(sp):
            sp.dma_start(ints[:, :], t["ints"]).then_inc(s_ids, 16)
            sp.dma_start(pka[:, :], t["packa"]).then_inc(s_pka, 16)
            for j in range(2):
                sp.dma_start(xc[S * j:S * j + S, :, :],
                             t["x"].rearrange("(p j) c w -> j c p w", j=2)[j]).then_inc(s_x, 16)
            sp.wait_ge(s_ids, 16)
            sp.wait_ge(s_wz, 1)
            for q in range(4):
                gather(sp, 0, q)
            sp.dma_start(x2T[:, :, :], t["xT"].rearrange("(k p) n -> p k n", p=P)).then_inc(s_xT, 16)
            sp.dma_start(pkb[:, :], t["packb"]).then_inc(s_pkb, 16)
            sp.dma_start(table[:, :], t["table"]).then_inc(s_ids, 16)
            def load_weights(n):
                if n >= 2:
                    sp.wait_ge(s_wh, n - 1)
                    sp.wait_ge(s_wl, n - 1)
                name, at = WSLOTS[n]
                sp.dma_start(wland[:, n % 2], t[name].rearrange("(k p) n -> p k n", p=P)[:, :, WCOLS * at:WCOLS * at + WCOLS]).then_inc(s_w[n % 2], 16)

            for n in range(3):
                load_weights(n)

            load_weights(3)
            kv = t["k_s"].rearrange("b p n -> p b n")
            for h in range(2):
                sp.wait_ge(s_po, 12 + 4 * h)
                for q in range(2):
                    done = s_kst if h == 0 else s_qst[q]
                    sp.dma_start(kv[:, 16 * h + 8 * q:16 * h + 8 * q + 8, :],
                                 ko[h][:, 8 * q:8 * q + 8].rearrange("p b g s -> p b (g s)")).then_inc(done, 16)
            for n in range(VTILES):
                s0, m = n // TILES, n % TILES
                if n % WTILES == 1:
                    load_weights(4 + n // WTILES)
                sp.wait_ge(s_ve, n + 1)
                sp.dma_start(t["v_s"][P * m:P * m + P, WCOLS * s0:WCOLS * s0 + WCOLS], vo[:, n % 4, :]).then_inc(s_vst[n % 4], 16)

            def page_numbers(b):
                return nc.values_load_multi_w_load_instructions(table[0:1, ds(NPP * b, NPP)], engines=(SP,),
                                                                min_val=0, max_val=PAGES - 1)[1]

            first_numbers = page_numbers(0)
            qv = t["q_s"].rearrange("b p n -> p b n")
            for g in range(HK):
                if g < HK - 2:
                    load_weights(6 + g)
                for h in range(2):
                    sp.wait_ge(s_po, KTILES + 8 * g + 4 * h + 4)
                    sp.dma_start(qv[:, 16 * h:16 * h + 16, P * g:P * g + P],
                                 qor[h].rearrange("p b r s -> p b (r s)")).then_inc(s_qst[h], 16)

            pages = t["vc"].rearrange("a s g d -> a s (g d)")

            def load_keys(b):
                after(sp, s_ql, 3 * b)
                start_load(sp, b)

            def load_values(b, par):
                numbers = first_numbers if isinstance(b, int) and b == 0 else page_numbers(b)
                if isinstance(b, int) and b == 0:
                    sp.wait_ge(s_pj, KTILES + VTILES + QTURNS * QTILES)
                after(sp, s_pv, 8 * b - 8)
                for n, page in enumerate(numbers):
                    sp.dma_start(vring[S * (n % BPT):S * (n % BPT) + S, par, n // BPT, :],
                                 pages[ds(page, 1)].rearrange("a s n -> s (a n)")).then_inc(s_v[par], 16)
                if isinstance(b, int) and b == 0:
                    sp.wait_ge(s_ss, KTILES + 16)
                    for n in range(4):
                        sp.wait_ge(s_vst[n], 16 * VTILES // 4)
                sp.dma_start(vring[0:S, par, BPT, :], t["v_s"][ds(S * b, S), :]).then_inc(s_v[par], 16)

            def store(b, par):
                sp.wait_ge(s_ov, 8 * b + 8)
                sp.dma_start(t["o_s"][ds(b, 1)].rearrange("a p n -> p (a n)"), oring[:, par, :]).then_inc(s_ost[par], 16)

            load_values(0, 0)
            sp.wait_ge(s_po, KTILES + QTURNS * QTILES)
            sp.wait_ge(s_qst[0], 16 * (HK + 1))
            sp.wait_ge(s_qst[1], 16 * (HK + 1))
            sp.wait_ge(s_kst, 32)
            load_keys(1)
            load_values(1, 1)
            with sp.Fori(0, B // 2 - 1) as i:
                for par in range(2):
                    load_keys(2 * i + 2 + par)
                    store(2 * i + par, par)
                    load_values(2 * i + 2 + par, par)
            ov = t["o_s"].rearrange("b p n -> p b n")
            early = B - 4

            def load_output_weights(g):
                sp.dma_start(wolands[g % 2],
                             t["woT"][REP * D * g:REP * D * (g + 1), :].rearrange("(h p) n -> p h n", p=P)).then_inc(s_wo[g % 2], 16)

            def load_outputs(g, lo, hi, done):
                sp.dma_start(oland[:, g % 2, lo:hi, :], ov[:, lo:hi, P * g:P * g + P]).then_inc(done[g % 2], 16)

            sp.wait_ge(s_kc, NPP * B)
            load_output_weights(0)
            sp.wait_ge(s_sc, UNITS - HK)
            for par in range(2):
                sp.wait_ge(s_ost[par], 16 * (B // 2 - 2))
            load_outputs(0, 0, early, s_oin)
            store(B - 2, 0)
            store(B - 1, 1)
            for par in range(2):
                sp.wait_ge(s_ost[par], 16 * (B // 2))
            load_outputs(0, early, B, s_oin2)
            for g in range(1, HK):
                if g >= 2:
                    sp.wait_ge(s_woh, g - 1)
                    sp.wait_ge(s_wol, g - 1)
                    sp.wait_ge(s_oh, 2 * (g - 1))
                    sp.wait_ge(s_ol, 2 * (g - 1))
                load_output_weights(g)
                load_outputs(g, 0, early, s_oin)
                load_outputs(g, early, B, s_oin2)
            sp.dma_start(pkc[:, :], t["packc"]).then_inc(s_pkc, 16)
            for n in range(2 * KC):
                m, h = n // 2, n % 2
                sp.wait_ge(s_fin, n + 1)
                sp.dma_start(t["out"][P * m:P * m + P, HALF * h:HALF * h + HALF],
                             hT[:, m, HALF * h:HALF * h + HALF]).then_inc(s_out, 16)
            sp.wait_ge(s_out, 16 * 2 * KC)

        @block.gpsimd
        def _(pool):
            pool.memset(wgat[:, :, :], 0.0).then_inc(s_wz, 1)
            pool.memset(ones[:, :], 1.0).then_inc(s_wz, 1)
            pool.memset(mean_d[:, :], 1.0 / D).then_inc(s_wz, 1)
            pool.memset(eps_qk[:, :], EPS_QK).then_inc(s_wz, 1)
            pool.wait_ge(s_x, 32)
            with pool.Fori(0, NPAIR) as p:
                pool.tensor_copy(xs16[0:2 * S, ds(p, 1), :], xc[:, ds(p, 1), :]).then_inc(s_xsp, 1)
                pool.wait_ge(s_xsp, 2 * p + 1)
                pool.tensor_tensor(xs16[2 * S:P, ds(p, 1), :], xc[:, ds(p, 1), :], xs16[0:2 * S, ds(p, 1), :],
                                   ALU.subtract).then_inc(s_xsp, 1)
            pool.wait_ge(s_xT, 16)
            pool.wait_ge(s_xsp, 2 * NPAIR)
            with pool.Fori(0, 2) as h:
                for k in range(KC):
                    pool.wait_ge(s_cT, 2 * KC * h + 2 * k + 2)
                    pool.tensor_tensor(x2T[:, k, ds(HALF * h, HALF)], x2T[:, k, ds(HALF * h, HALF)],
                                       condT[:, k, ds(HALF * h, HALF)], ALU.add).then_inc(s_xc, 1)
            pool.wait_ge(s_xc, 2 * KC)
            pool.wait_ge(s_xm, 2)
            pool.wait_ge(s_tab, 4)
            pool.memset(xpad[:, :, :, 0:DCONV - 1], 0.0).then_inc(s_hz, 1)
            pool.memset(bcpad[:, :, 0:DCONV - 1], 0.0).then_inc(s_hz, 1)
            pool.memset(Ct[:, 0:1], 0.0).then_inc(s_hz, 1)
            pool.memset(Ct[:, TOK + 1:TOK + 2], 0.0).then_inc(s_hz, 1)
            pool.memset(M[:, :, :], 0.0).then_inc(s_hz, 1)
            with pool.Fori(0, 2) as i:
                out = cacc[:, 1, :].rearrange("p (a s) -> p a s", s=S)
                for k in range(1, DCONV):
                    pool.wait_ge(s_tap, DCONV * i + k + 1)
                    if k >= 2:
                        pool.wait_ge(s_cp, (DCONV - 1) * i + k - 1)
                    pool.tensor_tensor(out, out, taps[k % 4], ALU.add).then_inc(s_cp, 1)
                pool.wait_ge(s_W, 16 * i + 16)
                pool.wait_ge(s_seg, 2 * i + 2)
                w4 = bc(W12[:, 1], 2, [P, TILES, NH, S])
                d4 = bc(dtd[:, 1].rearrange("p (a h) -> p a h", h=NH), 3, [P, TILES, NH, S])
                pool.tensor_tensor(T12[:, 1].rearrange("p (a h) s -> p a h s", h=NH), w4, d4, ALU.mult).then_inc(s_T, 1)

            for n in range(2 * KC):
                h, k = n // KC, n % KC
                sl = slice(HALF * h, HALF * h + HALF)
                pool.wait_ge(s_xh, n + 1)
                pool.tensor_tensor(x16[:, 1, k, sl], x2T[:, k, sl], x16[:, 0, k, sl], ALU.subtract).then_inc(s_xl, 1)
            for n in range(KTILES):
                pool.wait_ge(s_ab, n + 1)
                pool.tensor_tensor(ab[:, n % 3, 0, :], ab[:, n % 3, 0, :], ab[:, n % 3, 1, :], ALU.add).then_inc(s_add, 1)

            def pool_queries(i, pages=False):
                for n in range(QTILES):
                    m, r = n // 4, n % 4
                    if r == 0:
                        pool.wait_ge(s_qst[m % 2], 32 * i + 16 * (m // 2 + 1))
                    pool.wait_ge(s_ab, KTILES + QTILES * i + n + 1)
                    pool.tensor_tensor(qor[m % 2][:, :, r, :], by_batch(ab[:, n % 2, 0, :]),
                                       by_batch(ab[:, n % 2, 1, :]), ALU.add).then_inc(s_po, 1)
                    if pages:
                        pc = QTILES * i + n
                        pool.wait_ge(s_kh, pc + 1)
                        pool.tensor_tensor(K16[:, ds(2 * pc, 2), 1, :], vo[:, n % 4, :].rearrange("p (a n) -> p a n", a=2),
                                           K16[:, ds(2 * pc, 2), 0, :], ALU.subtract).then_inc(s_kl, 1)
                    if isinstance(i, int) and i == QTURNS - 1 and n == WTILES + 4:
                        pool.wait_ge(s_qh, 2)
                        pool.tensor_tensor(kring16[:, 0, NPP, 1, :], kland[:, :], kring16[:, 0, NPP, 0, :],
                                           ALU.subtract).then_inc(s_ql, 1)
                    elif isinstance(i, int) and i == QTURNS - 1 and n == WTILES + 5:
                        pool.tensor_tensor(q16[:, 0, 1, 0:EARLY], qland[:, 0:EARLY], q16[:, 0, 0, 0:EARLY],
                                           ALU.subtract).then_inc(s_ql, 1)

            with pool.Fori(0, 2) as i:
                pool_queries(i, pages=True)
            pool_queries(2)
            pool_queries(3)

            def normalise(n, slot):
                pool.wait_ge(s_rc, n + 1)
                pool.sem_inc(s_seen, 1)
                pool.tensor_scalar(prob[:, slot, :], prob[:, slot, :], ri[:, slot:slot + 1], 1.0,
                                   ALU.mult, ALU.mult).then_inc(s_pn, 1)

            def split_queries(b, par, part):
                if part == 0:
                    pool.wait_ge(s_qh, 2 * b + 3)
                if part < 2:
                    half = slice(HQ * S // 2 * part, HQ * S // 2 * (part + 1))
                    pool.tensor_tensor(q16[:, par, 1, half], qland[:, half], q16[:, par, 0, half], ALU.subtract).then_inc(s_ql, 1)
                else:
                    pool.tensor_tensor(kring16[:, par, NPP, 1, :], kland[:, :], kring16[:, par, NPP, 0, :],
                                       ALU.subtract).then_inc(s_ql, 1)

            normalise(0, 0)
            normalise(1, 1)
            pool.wait_ge(s_qh, 3)
            pool.tensor_tensor(q16[:, 0, 1, EARLY:], qland[:, EARLY:], q16[:, 0, 0, EARLY:], ALU.subtract).then_inc(s_ql, 1)

            def pool_turn(i):
                for j in range(16):
                    n = 16 * i + j
                    if not (isinstance(i, int) and n + 2 >= UNITS):
                        normalise(n + 2, (j + 2) % 4)
                    b = j // 8 + 1
                    if j % 8 in (1, 2, 3) and not (isinstance(i, int) and 2 * i + b >= B):
                        split_queries(2 * i + b, b % 2, j % 8 - 1)

            pool_turn(0)
            with pool.Fori(1, 15) as i:
                pool_turn(i)
            pool_turn(15)
            pool.wait_ge(s_hT, TILES)
            pool.tensor_tensor(x2T[:, :, :], x2T[:, :, :], hT[:, :, :], ALU.add).then_inc(s_fa, 1)

        @block.scalar
        def _(act):
            act.wait_ge(s_ids, 16)
            act.wait_ge(s_wz, 1)
            for q in range(4):
                gather(act, 1, q)
            act.wait_ge(s_pka, 16)
            act.activation(negA[:, :], A("alog"), ACT.Exp).then_inc(s_al, 1)
            act.activation(alpha[:, 0:1], A("gate1"), ACT.Sigmoid).then_inc(s_al, 1)
            act.wait_ge(s_ang, 2)
            for n in range(2):
                act.activation(turns[:, n, :], turns[:, n, :], ACT.Sin).then_inc(s_sin, 1)
            with act.Fori(0, 2) as h:
                for p in range(8):
                    n = 8 * h + p
                    if p == 0:
                        act.wait_ge(s_prep, 9)
                    act.wait_ge(s_h1, n + 1)
                    if p >= 2:
                        act.wait_ge(s_co, KC * (n - 1))
                    act.activation(hbuf[:, p % 2, :], bank(p % 2), ACT.Gelu,
                                   bias=bias1[:, ds(n, 1)], scale=1 / WSCALE).then_inc(s_g1, 1)
                act.wait_ge(s_dn, h + 1)
                act.activation(xmid[:, :].rearrange("p (s b) -> p b s", b=B)[:, ds(16 * h, 16), :],
                               by_batch(bank(6)), ACT.Gelu, bias=A("bdown")).then_inc(s_xm, 1)

            def split_weights(n, par):
                par %= 2
                act.wait_ge(s_w[par], 8 * n + 16 - 8 * par)
                after(act, s_pj, WTILES * (n - 1))
                act.activation(w16[:, par, 0], wland[:, par], ACT.Copy, scale=WSCALE).then_inc(s_wh, 1)

            act.wait_ge(s_hz, 4)

            with act.Fori(0, 2) as i:
                for n, (dst, c) in enumerate([(bcpad, None), (xpad, 0), (xpad, 1)]):
                    for h in range(2):
                        act.wait_ge(s_pr, 6 * i + 2 * n + h + 1)
                        src = bank(2 * n + h)[0:3 * DST] if c is None else bank(2 * n + h)
                        out = bcpad[:, 16 * h:16 * h + 16, DCONV - 1:] if c is None else \
                            xpad[:, c, 16 * h:16 * h + 16, DCONV - 1:]
                        act.activation(out, by_batch(src), ACT.Copy).then_inc(s_xp, 1)
                    if n == 0:
                        act.wait_ge(s_nv, i + 1)
                        act.activation(dtv[:, 2, :], dtv[:, 1, :], ACT.Exp).then_inc(s_ey, 1)
                act.wait_ge(s_xp, 6 * i + 6)
                for k in range(DCONV):
                    if k > 4:
                        act.wait_ge(s_cp, (DCONV - 1) * i + k - 4)
                    out = cacc[:, 1, :].rearrange("p (a s) -> p a s", s=S) if k == 0 else taps[k % 4]
                    act.activation(out, xpad[:, 1, :, k:k + S], ACT.Copy,
                                   scale=A("convx")[:, DCONV + k:DCONV + k + 1]).then_inc(s_tap, 1)
                for n in range(4):
                    act.wait_ge(s_zp, 4 * i + n + 1)
                    act.activation(zs[:, n // 2, HALF * (n % 2):HALF * (n % 2) + HALF], bank(2 + n),
                                   ACT.Silu).then_inc(s_zs, 1)
                act.wait_ge(s_cv, 2 * i + 1)
                act.activation(Bt[:, :], cacc[0:DST, 2, :], ACT.Silu, bias=A("convbbc", DST)).then_inc(s_xs, 1)
                act.activation(Ct[:, 1:TOK + 1], cacc[2 * DST:3 * DST, 2, :], ACT.Silu,
                               bias=A("convbbc", DST, 2 * DST)).then_inc(s_xs, 1)
                for h in range(2):
                    act.wait_ge(s_seg, 2 * i + h + 1)
                    act.activation(E[:, 16 * h:16 * h + 16, :], by_batch(bank(h)), ACT.Exp).then_inc(s_E, 1)
                for c in range(2):
                    if c == 0:
                        act.wait_ge(s_cv, 2 * i + 2)
                    else:
                        act.wait_ge(s_cp, (DCONV - 1) * (i + 1))
                    act.activation(xs[:, c, :], cacc[:, c, :], ACT.Silu, bias=A("convbx")[:, c:c + 1]).then_inc(s_xs, 1)
                for n in range(4):
                    act.wait_ge(s_xt, 4 * i + n + 1)
                    act.activation(xtok[:, 4 * (n % 2):4 * (n % 2) + 4, P * (n // 2):P * (n // 2) + P],
                                   bank(2 + n % 2).rearrange("p (a c) -> p a c", a=4), ACT.Copy).then_inc(s_xe, 1)
                act.wait_ge(s_yz, 4 * i + 4)
                for c in range(2):
                    act.activation(cacc[:, c, :], yb[:, c, :], ACT.Square).then_inc(s_ysq, 1)
                for h in range(2):
                    act.wait_ge(s_rr, 2 * i + h + 1)
                    act.activation(rb[:, h, :], rb[:, h, :], ACT.Sqrt).then_inc(s_rb, 1)

            split_weights(0, 0)
            for n in range(2 * KC):
                h, k = n // KC, n % KC
                sl = slice(HALF * h, HALF * h + HALF)
                act.wait_ge(s_x2, n + 1)
                act.activation(x16[:, 0, k, sl], x2T[:, k, sl], ACT.Copy).then_inc(s_xh, 1)

            def key_rms(n):
                act.wait_ge(s_ss, n + 1)
                act.activation(kms[:, n, :], bank(6 + n % 2)[:, 0:4], ACT.Sqrt, bias=eps_qk[:, :]).then_inc(s_kr1, 1)

            for n in range(KTILES):
                act.wait_ge(s_pj, n + 1)
                if n >= 2:
                    act.wait_ge(s_ss, n - 1)
                act.activation(ksq[n % 2], bank(n % 4), ACT.Square, scale=1 / WSCALE).then_inc(s_sq, 1)
                if n % WTILES == 1:
                    split_weights(n // WTILES + 1, n // WTILES + 1)
                if n >= 1:
                    key_rms(n - 1)
            key_rms(KTILES - 1)
            act.wait_ge(s_ss, KTILES)
            act.wait_ge(s_kb, KTILES)
            for n in range(VTILES):
                act.wait_ge(s_pj, KTILES + n + 1)
                if n >= 4:
                    act.wait_ge(s_vst[n % 4], 16 * (n // 4))
                act.activation(vo[:, n % 4, :], bank(n % 4), ACT.Copy, scale=1 / WSCALE).then_inc(s_ve, 1)
                if n % WTILES == 1:
                    split_weights(3 + n // WTILES, 3 + n // WTILES)
            act.wait_ge(s_kst, 32)

            def load_pages(pc, at):
                act.wait_ge(s_kl, pc + 1)
                act.dma_start(vo[:, at % 4, :].rearrange("p (a n) -> p a n", a=2),
                              t["kcT"].rearrange("d a g s -> d a (g s)")[:, ds(2 * pc, 2)]).then_inc(s_KT[at % 4], 16)

            def split_queries(b, par):
                act.wait_ge(s_in, 32 * b + 48)
                after(act, s_sc, 8 * b - 8)
                act.activation(q16[:, par, 0, :], qland[:, :], ACT.Copy).then_inc(s_qh, 1)

            def split_new_keys(b, par):
                act.activation(kring16[:, par, NPP, 0, :], kland[:, :], ACT.Copy).then_inc(s_qh, 1)

            def act_queries(i, pages=False):
                if pages:
                    for n in range(3):
                        load_pages(QTILES * i + n, n)
                for n in range(QTILES):
                    m, r = n // 4, n % 4
                    act.wait_ge(s_pj, KTILES + VTILES + QTILES * i + n + 1)
                    if r == 0:
                        act.wait_ge(s_ss, KTILES + 4 * i + m - 1)
                    act.activation(sqr[m % 2][:, :, r, :], by_batch(bank(n % 4)), ACT.Square, scale=1 / WSCALE).then_inc(s_sq, 1)
                    slot = 4 + 2 * i + n // WTILES
                    if n % WTILES == 1 and not (isinstance(i, int) and slot == len(WSLOTS) - 1):
                        split_weights(slot + 1, n // WTILES + 1)
                    if pages:
                        pc = QTILES * i + n
                        act.wait_ge(s_KT[n % 4], 64 * i + 16 * (n // 4) + 16)
                        act.activation(K16[:, ds(2 * pc, 2), 0, :], vo[:, n % 4, :].rearrange("p (a n) -> p a n", a=2),
                                       ACT.Copy).then_inc(s_kh, 1)
                        if n + 3 < QTILES:
                            load_pages(pc + 3, n + 3)
                    if isinstance(i, int) and i == QTURNS - 1 and n == WTILES + 1:
                        act.wait_ge(s_kst, 32)
                        act.wait_ge(s_qst[0], 16 * (HK - 1))
                        act.wait_ge(s_qst[1], 16 * (HK - 1))
                        act.dma_start(kland[:, :], t["k_s"][0]).then_inc(s_in, 16)
                        act.dma_start(qland[:, 0:EARLY], t["q_s"][0, :, 0:EARLY]).then_inc(s_in, 16)
                    elif isinstance(i, int) and i == QTURNS - 1 and n == WTILES + 4:
                        act.wait_ge(s_in, 32)
                        act.activation(q16[:, 0, 0, 0:EARLY], qland[:, 0:EARLY], ACT.Copy).then_inc(s_qh, 1)
                        split_new_keys(0, 0)

            for n in range(4):
                act.wait_ge(s_vst[n], 16 * VTILES // 4)
            act.sem_inc(s_kl, 4)
            with act.Fori(0, 2) as i:
                act_queries(i, pages=True)
            act_queries(2)
            act_queries(3)
            act.wait_ge(s_ss, KTILES + 16)
            act.activation(rq[:, :], bank(7)[:, 0:B * HK], ACT.Sqrt, bias=eps_qk[:, :]).then_inc(s_rms, 1)

            def exponentials(n, col, slot):
                act.wait_ge(s_nb, n + 1)
                act.activation(prob[:, slot, :], prob[:, slot, :], ACT.Exp, bias=nb[:, slot:slot + 1],
                               scale=rq[:, col], accum_out=rs[:, slot:slot + 1]).then_inc(s_ex, 1)

            act.wait_ge(s_qst[0], 16 * (HK + 1))
            act.wait_ge(s_qst[1], 16 * (HK + 1))
            act.dma_start(qland[:, EARLY:], t["q_s"][0, :, EARLY:]).then_inc(s_in, 16)
            for n in range(2):
                exponentials(n, slice(n, n + 1), n)
            act.wait_ge(s_in, 48)
            act.activation(q16[:, 0, 0, EARLY:], qland[:, EARLY:], ACT.Copy).then_inc(s_qh, 1)

            def split_output_weights(g):
                act.wait_ge(s_wo[g % 2], 16 * (g // 2) + 16)
                after(act, s_hg, g - 1)
                act.activation(wo16[:, g % 2, 0], wolands[g % 2], ACT.Copy, scale=WSCALE).then_inc(s_woh, 1)

            def split_outputs(g, h):
                act.wait_ge((s_oin, s_oin2)[h][g % 2], 16 * (g // 2) + 16)
                act.activation(head_major(o16[:, g % 2, 0], h), landed(g % 2, h), ACT.Copy).then_inc(s_oh, 1)

            def act_turn(i):
                for j in range(16):
                    n = 16 * i + j
                    act.wait_ge(s_t4, n + 1)
                    after(act, s_pv, n - 1)
                    act.activation(pT4[:, j % 2, :], bank(6 + (j + 1) % 2)[0:S, P:2 * P], ACT.Copy).then_inc(s_p4, 1)
                    if not (isinstance(i, int) and n + 2 >= UNITS):
                        exponentials(n + 2, ds(n + 2, 1) if not isinstance(i, int) else slice(n + 2, n + 3), (j + 2) % 4)
                    if not (isinstance(i, int) and n == 0):
                        jj = (j - 1) % 16
                        act.wait_ge(s_pv, n)
                        if jj % 8 == 0:
                            turn = i if j > 0 else i - 1
                            after(act, s_ost[jj // 8], 16 * turn)
                        act.activation(oring[:, jj // 8, P * (jj % 8):P * (jj % 8) + P], bank(6 + jj % 2)[:, 0:P],
                                       ACT.Copy).then_inc(s_ov, 1)
                    b = j // 8 + 1
                    if not (isinstance(i, int) and 2 * i + b >= B):
                        if j % 8 == 0:
                            split_queries(2 * i + b, b % 2)
                        elif j % 8 == 1:
                            split_new_keys(2 * i + b, b % 2)
                    if isinstance(i, int) and n == UNITS - 2:
                        split_output_weights(0)
                    elif isinstance(i, int) and n == UNITS - 1:
                        split_outputs(0, 0)

            act_turn(0)
            with act.Fori(1, 15) as i:
                act_turn(i)
            act_turn(15)
            act.wait_ge(s_pv, UNITS)
            act.activation(oring[:, 1, P * 7:P * 8], bank(7)[:, 0:P], ACT.Copy).then_inc(s_ov, 1)

            for g in range(HK):
                if g > 0:
                    split_output_weights(g)
                    split_outputs(g, 0)
                split_outputs(g, 1)
            act.wait_ge(s_ost[0], 16 * B // 2)
            act.wait_ge(s_ost[1], 16 * B // 2)
            for n in range(TILES):
                act.wait_ge(s_hp, n + 1)
                act.activation(htok[:, n, :], bank(n), ACT.Copy, scale=1 / WSCALE).then_inc(s_ht, 1)
            act.wait_ge(s_pkc, 16)
            for row in (0, VB):
                act.activation(wvu16[row:row + VB, :], C("fwvu", VB), ACT.Copy, scale=WSCALE).then_inc(s_wvh, 1)
            act.wait_ge(s_fp, 1)
            act.activation(rkT[:, :], bank(4)[0:RDIM, 0:NSLOT], ACT.Copy).then_inc(s_fe, 1)
            act.wait_ge(s_fp, 2)
            act.activation(AV[:, :], bank(5)[:, 0:VB], ACT.Copy).then_inc(s_fe, 1)
            for h in range(2):
                act.wait_ge(s_fp, 3 + h)
                act.activation(queryT[:, HALF * h:HALF * h + HALF], bank(h)[0:BOT], ACT.Copy).then_inc(s_fe, 1)
            for h in range(2):
                act.wait_ge(s_fp, 5 + h)
                act.activation(rqT[:, HALF * h:HALF * h + HALF], bank(2 + h)[0:RDIM], ACT.Copy).then_inc(s_fe, 1)
            for h in range(2):
                act.wait_ge(s_fp, 7 + h)
                act.activation(uT[:, HALF * h:HALF * h + HALF], bank(6 + h), ACT.Gelu_apprx_tanh,
                               bias=C("fbu1")).then_inc(s_fe, 1)
            act.wait_ge(s_bn, TILES)
            act.activation(sm[:, 0, :], mv[:, :, 1], ACT.Ln, bias=1.0, accum_out=lsum[:, 0:1]).then_inc(s_lv, 1)
            act.wait_ge(s_ler, 1)
            act.activation(sm[:, 1, :], bank(6)[:, 0:TILES], ACT.Sigmoid, bias=C("fbu2")).then_inc(s_sg, 1)
            act.wait_ge(s_ga, 1)
            act.activation(sm[:, 4, :], sm[:, 3, :], ACT.Sigmoid, bias=C("fgb"), scale=C("fgw")).then_inc(s_gb, 1)
            act.wait_ge(s_am, 1)
            for n in range(TILES):
                act.activation(asc[:, n, :], asc[:, n, :], ACT.Exp, bias=amx[:, n:n + 1],
                               accum_out=wsum[:, n:n + 1]).then_inc(s_exw, 1)
            for n in range(2):
                act.wait_ge(s_wt, n + 1)
                act.activation(wTs[:, HALF * n:HALF * n + HALF], bank(2 + n), ACT.Copy).then_inc(s_wte, 1)
            for h in range(2):
                act.wait_ge(s_ax, h + 1)
                for row in (0, 2 * VB):
                    act.activation(aux16[row:row + VB, HALF * h:HALF * h + HALF], bank(h)[0:VB], ACT.Copy).then_inc(s_axe, 1)

        @block.vector
        def _(dve):
            done = [0]

            def prep(ins):
                done[0] += 1
                ins.then_inc(s_prep, 1)
                dve.wait_ge(s_prep, done[0])

            dve.wait_ge(s_ids, 16)
            prep(dve.tensor_copy(intf[:, :], ints[:, :]))
            dve.wait_ge(s_pka, 16)
            dve.tensor_scalar(onehot[:, :], intf[0:SESS, 0:B], A("sessidx", SESS), None, ALU.is_equal).then_inc(s_masks, 1)
            for j in range(2):
                dve.tensor_scalar(cmask[S * j:S * j + S, :], intf[S * j:S * j + S, B + j:2 * B:2],
                                  A("chan", S, S * j), WSCALE, ALU.is_gt, ALU.mult).then_inc(s_prep, 1)
            for k in range(KC):
                dve.tensor_scalar(tmask[:, k, :], intf[:, 2 * B:3 * B], A("tcol")[:, k:k + 1], None,
                                  ALU.is_gt).then_inc(s_prep, 1)
            done[0] += 2 + KC
            dve.wait_ge(s_prep, done[0])
            dve.wait_ge(s_bias, 1)
            for j in range(2):
                dve.tensor_copy(bias1[CHID * j:CHID * j + CHID, :], bank(7)[CHID * j:CHID * j + CHID, j:B:2]).then_inc(s_prep, 1)
            done[0] += 2
            dve.wait_ge(s_prep, done[0])
            prep(dve.tensor_tensor(by_batch(ang[:, :]), bc(intf[:, 3 * B:4 * B], 2, [P, B, S]),
                                   bc(A("srow"), 1, [P, B, S]), ALU.add))
            prep(dve.tensor_scalar(ang[:, :], ang[:, :], A("invf"), None, ALU.mult))
            for n in range(2):
                tn = turns[:, n, :]
                count = tabs[:, n, :]
                prep(dve.tensor_scalar(count, ang[:, :], float(1 / (2 * np.pi)), 0.25 * n, ALU.mult, ALU.add))
                prep(dve.tensor_scalar(count, count, ROUND, ROUND, ALU.add, ALU.subtract))
                prep(dve.scalar_tensor_tensor(out=tn, in0=count, scalar=-PI2_A, in1=ang[:, :], op0=ALU.mult, op1=ALU.add))
                prep(dve.scalar_tensor_tensor(out=tn, in0=count, scalar=-PI2_B, in1=tn, op0=ALU.mult, op1=ALU.add))
                prep(dve.scalar_tensor_tensor(out=tn, in0=count, scalar=-PI2_C, in1=tn, op0=ALU.mult, op1=ALU.add))
                if n == 1:
                    prep(dve.tensor_scalar(tn, tn, float(np.pi / 2), None, ALU.add))
                dve.tensor_scalar(tn, tn, PI, -PI, ALU.min, ALU.max).then_inc(s_ang, 1)
            dve.wait_ge(s_al, 2)
            prep(dve.tensor_scalar(negA[:, :], negA[:, :], -1.0, None, ALU.mult))
            prep(dve.tensor_scalar(alpha[:, 1:2], alpha[:, 0:1], 1.0, None, ALU.add))
            prep(dve.tensor_scalar(alpha[:, 2:3], alpha[:, 0:1], -1.0, 1.0, ALU.mult, ALU.add))
            for c in range(2):
                prep(dve.tensor_scalar(outw[:, c, :], A("outw")[:, DM * c:DM * c + DM], A("normw")[:, c:c + 1],
                                       None, ALU.mult))

            def rope_tables():
                for n in range(4):
                    sine = n % 2
                    dve.wait_ge(s_sin, 2 - sine)
                    dve.tensor_scalar(tabs[:, n, :], turns[:, 1 - sine, :], A("qnw") if n < 2 else A("knw"),
                                      A("sign") if sine else 1 / WSCALE, ALU.mult, ALU.mult).then_inc(s_tab, 1)

            for h in range(2):
                for p in range(8):
                    n = 8 * h + p
                    if p % 4 == 0:
                        dve.wait_ge(s_gather[n // 4], 16 * 8)
                    after(dve, s_h1, n - 1)
                    for row in (0, 2 * S):
                        dve.tensor_scalar(whi[row:row + 2 * S, p % 2, :], wgat[:, n, :], cmask[:, n:n + 1], None,
                                          ALU.mult).then_inc(s_wst, 1)
                    dve.wait_ge(s_wst, 3 * n + 2)
                    dve.scalar_tensor_tensor(out=wlo[:, p % 2, :], in0=wgat[:, n, :], scalar=cmask[:, n:n + 1],
                                             in1=whi[0:2 * S, p % 2, :], op0=ALU.mult, op1=ALU.subtract).then_inc(s_wst, 1)
                if h == 0:
                    rope_tables()
                for k in range(KC):
                    dve.wait_ge(s_co, 8 * KC * h + 7 * KC + k + 1)
                    out = condT[:, k, HALF * h:HALF * h + HALF].rearrange("p (b s) -> p b s", s=S)
                    dve.tensor_tensor(out, by_batch(bank(2 + k)), bc(A("b2"), 1, [P, 16, S]), ALU.add).then_inc(s_cT, 1)
                    dve.wait_ge(s_cT, 2 * (KC * h + k) + 1)
                    dve.tensor_tensor(out, out, bc(tmask[:, k, 16 * h:16 * h + 16], 2, [P, 16, S]),
                                      ALU.mult).then_inc(s_cT, 1)

            def split_weights(n, par):
                par %= 2
                dve.wait_ge(s_wh, n + 1)
                dve.scalar_tensor_tensor(out=w16[:, par, 1], in0=wland[:, par], scalar=WSCALE, in1=w16[:, par, 0],
                                         op0=ALU.mult, op1=ALU.subtract).then_inc(s_wl, 1)

            dve.wait_ge(s_xm, 2)
            dve.tensor_copy(u[:, :], xmid[:, :]).then_inc(s_u, 1)
            dve.wait_ge(s_xc, 2 * KC)

            ta = "p (a h) -> p a h"
            with dve.Fori(0, 2) as i:
                steps = [0]

                def step(ins):
                    steps[0] += 1
                    ins.then_inc(s_hd, 1)
                    dve.wait_ge(s_hd, NCHAIN * i + steps[0])

                dve.wait_ge(s_dtp, i + 1)
                step(dve.tensor_tensor(dtv[:, 0, :].rearrange(ta, h=8), bank(6)[:, 0:8 * TILES].rearrange(ta, h=8),
                                       bc(A("dtb"), 1, [P, TILES, 8]), ALU.add))
                dve.scalar_tensor_tensor(out=dtv[:, 1, :], in0=dtv[:, 0, :], scalar=-1.0, in1=dtv[:, 0, :],
                                         op0=ALU.mult, op1=ALU.min).then_inc(s_nv, 1)

                def convolve(src, w, dst):
                    out = dst.rearrange("p (a s) -> p a s", s=S)
                    step(dve.tensor_scalar(out, src[:, :, 0:S], w[:, 0:1], None, ALU.mult))
                    for k in range(1, DCONV):
                        ins = dve.scalar_tensor_tensor(out=out, in0=src[:, :, k:k + S], scalar=w[:, k:k + 1],
                                                       in1=out, op0=ALU.mult, op1=ALU.add)
                        if k < DCONV - 1:
                            step(ins)
                    ins.then_inc(s_cv, 1)

                dve.wait_ge(s_xp, 6 * i + 2)
                convolve(bcpad, A("convbc", 3 * DST), cacc[0:3 * DST, 2, :])

                dve.wait_ge(s_ey, i + 1)
                y, z, z2, p = dtv[:, 2, :], dtv[:, 3, :], dtv[:, 4, :], dtv[:, 1, :]
                step(dve.tensor_scalar(z, y, 2.0, None, ALU.add))
                step(dve.reciprocal(z, z))
                step(dve.tensor_tensor(z, z, y, ALU.mult))
                step(dve.tensor_tensor(z2, z, z, ALU.mult))
                step(dve.tensor_scalar(p, z2, 1.0 / 15, None, ALU.mult))
                for c in (13, 11, 9, 7, 5, 3):
                    step(dve.scalar_tensor_tensor(out=p, in0=p, scalar=1.0 / c, in1=z2, op0=ALU.add, op1=ALU.mult))
                step(dve.scalar_tensor_tensor(out=p, in0=p, scalar=1.0, in1=z, op0=ALU.add, op1=ALU.mult))
                step(dve.tensor_scalar(y, dtv[:, 0, :], 0.0, None, ALU.max))
                step(dve.scalar_tensor_tensor(out=y, in0=p, scalar=2.0, in1=y, op0=ALU.mult, op1=ALU.add))
                y8 = y.rearrange(ta, h=8)
                for d in range(2):
                    step(dve.tensor_copy(dtd[:, d, :].rearrange(ta, h=NH), y8[:, :, NH * d:NH * d + NH]))
                    step(dve.tensor_tensor(dtd[:, 2 + d, :].rearrange(ta, h=NH), y8[:, :, NH * d:NH * d + NH],
                                           bc(negA[:, :], 1, [P, TILES, NH]), ALU.mult))
                for d, side in enumerate(("before", "after")):
                    dve.tensor_tensor(Rm[:, d], bc(dtd[:, 2 + d, :], 2, [P, TILES * NH, S]),
                                      bc(A(side), 1, [P, TILES * NH, S]), ALU.mult).then_inc(s_R, 1)

                dve.wait_ge(s_xp, 6 * i + 4)
                convolve(xpad[:, 0], A("convx")[:, 0:DCONV], cacc[:, 0, :])

                for d, side in enumerate(("before", "after")):
                    for m in range(2):
                        dve.wait_ge(s_GG, 4 * i + 2 * d + m + 1)
                        src = bank((6, 4)[d] + m).rearrange("p (a c) -> p a c", a=4)
                        for q in range(BPT):
                            lo = S * q
                            dve.tensor_tensor(W12[lo:lo + S, d, 4 * m:4 * m + 4, :], src[lo:lo + S, :, lo:lo + S],
                                              bc(A(side, S, lo), 1, [S, 4, S]), ALU.mult).then_inc(s_W, 1)

                dve.wait_ge(s_W, 16 * i + 16)
                dve.wait_ge(s_seg, 2 * i + 2)
                dve.tensor_tensor(T12[:, 0].rearrange("p (a h) s -> p a h s", h=NH),
                                  bc(W12[:, 0], 2, [P, TILES, NH, S]),
                                  bc(dtd[:, 0].rearrange(ta, h=NH), 3, [P, TILES, NH, S]), ALU.mult).then_inc(s_T, 1)
                dve.wait_ge(s_T, 3 * i + 2)
                dve.tensor_tensor(T12[:, 0], T12[:, 0], T12[:, 1], ALU.add).then_inc(s_T, 1)
                dve.wait_ge(s_T, 3 * i + 3)
                dve.wait_ge(s_E, 2 * i + 2)
                dve.wait_ge(s_hz, 5)
                for q in range(BPT):
                    lo = S * q
                    dve.tensor_tensor(M[lo:lo + S, :, lo:lo + S], T12[lo:lo + S, 0], E[lo:lo + S], ALU.mult).then_inc(s_M, 1)
                for n in range(4):
                    c, h = n // 2, n % 2
                    sl = slice(HALF * h, HALF * h + HALF)
                    dve.wait_ge(s_r, 4 * i + n + 1)
                    dve.scalar_tensor_tensor(out=yb[:, c, sl], in0=bank(4 + n), scalar=A("dskip")[:, c:c + 1],
                                             in1=xs[:, c, sl], op0=ALU.add, op1=ALU.mult).then_inc(s_t, 1)
                for n in range(4):
                    c, h = n // 2, n % 2
                    sl = slice(HALF * h, HALF * h + HALF)
                    dve.wait_ge(s_y, 4 * i + n + 1)
                    dve.wait_ge(s_t, 4 * i + n + 1)
                    step(dve.tensor_tensor(yb[:, c, sl], bank(n), yb[:, c, sl], ALU.add))
                    dve.tensor_tensor(yb[:, c, sl], yb[:, c, sl], zs[:, c, sl], ALU.mult).then_inc(s_yz, 1)
                for h in range(2):
                    dve.wait_ge(s_ss0, 2 * i + h + 1)
                    step(dve.tensor_scalar(rb[:, h, :], bank(4 + h), 1.0 / DIN, EPS_HYDRA, ALU.mult, ALU.add))
                    dve.reciprocal(rb[:, h, :], rb[:, h, :]).then_inc(s_rr, 1)
                for h in range(2):
                    sl = slice(HALF * h, HALF * h + HALF)
                    dve.wait_ge(s_hy, 2 * i + h + 1)
                    dve.wait_ge(s_rb, 2 * i + h + 1)
                    ins = dve.tensor_tensor(u[:, sl], bank(6 + h), rb[:, h, :], ALU.mult)
                    if h == 0:
                        step(ins)
                ins.then_inc(s_u, 1)
                assert steps[0] == NCHAIN, steps
            split_weights(0, 0)
            dve.wait_ge(s_u, 3)
            prep(dve.tensor_scalar(u[:, :], u[:, :], alpha[:, 2:3], None, ALU.mult))
            dve.scalar_tensor_tensor(out=u[:, :], in0=xmid[:, :], scalar=alpha[:, 1:2], in1=u[:, :],
                                     op0=ALU.mult, op1=ALU.add).then_inc(s_hf, 1)
            for n in range(2 * KC):
                h, k = n // KC, n % KC
                sl = slice(HALF * h, HALF * h + HALF)
                dve.wait_ge(s_up, n + 1)
                if n == 0:
                    dve.wait_ge(s_xc, 2 * KC)
                dve.scalar_tensor_tensor(out=x2T[:, k, sl], in0=bank(n), scalar=A("bup")[:, k:k + 1],
                                         in1=x2T[:, k, sl], op0=ALU.add, op1=ALU.add).then_inc(s_x2, 1)

            def rotate(tile, slot, h, tab):
                sl = slice(HALF * h, HALF * h + HALF)
                dve.tensor_tensor(ab[:, slot, 0, :], tile, tabs[:, tab, sl], ALU.mult)
                dve.tensor_tensor(ab[0:64, slot, 1, :], tile[64:P], tabs[64:P, tab + 1, sl], ALU.mult)
                dve.tensor_tensor(ab[64:P, slot, 1, :], tile[0:64], tabs[0:64, tab + 1, sl], ALU.mult).then_inc(s_ab, 1)

            def key_diagonal(n):
                dve.wait_ge(s_kr1, n + 1)
                prep(dve.reciprocal(kms[:, n, :], kms[:, n, :]))
                if n >= 2:
                    dve.wait_ge(s_kb, n - 1)
                dve.tensor_tensor(diag[n % 2], bc(G("ident"), 1, [P, 4, P]), bc(kms[:, n, :], 2, [P, 4, P]),
                                  ALU.mult).then_inc(s_kr2, 1)

            def normalise_key(n):
                h, g = n // 4 % 2, 4 * (n // 8) + n % 4
                dve.wait_ge(s_add, n + 1)
                dve.wait_ge(s_kb, n + 1)
                dve.tensor_tensor(ko[h][:, :, g, :], by_batch(ab[:, n % 3, 0, :]), by_batch(bank(4 + n % 2)),
                                  ALU.mult).then_inc(s_po, 1)

            for n in range(KTILES + 2):
                if n < KTILES:
                    dve.wait_ge(s_sq, n + 1)
                    if n >= 3:
                        dve.wait_ge(s_po, n - 2)
                    rotate(bank(n % 4), n % 3, n // 4 % 2, 2)
                    if n % WTILES == 1:
                        split_weights(n // WTILES + 1, n // WTILES + 1)
                if 1 <= n <= KTILES:
                    key_diagonal(n - 1)
                if n >= 2:
                    normalise_key(n - 2)
            for n in range(2):
                split_weights(3 + n, 3 + n)

            def copy_page(par, n, page):
                dve.tensor_copy(kring[:, par, n, :], KT[:, ds(page * (HK * S), HK * S)]).then_inc(s_kc, 1)

            def dve_queries(i):
                for n in range(QTILES):
                    dve.wait_ge(s_sq, KTILES + QTILES * i + n + 1)
                    dve.wait_ge(s_po, KTILES + QTILES * i + n - 1)
                    rotate(bank(n % 4), n % 2, n // 4 % 2, 0)
                    slot = 4 + 2 * i + n // WTILES
                    if n % WTILES == 1 and not (isinstance(i, int) and slot == len(WSLOTS) - 1):
                        split_weights(slot + 1, n // WTILES + 1)
                    if isinstance(i, int) and n >= QTILES - 6:
                        if n == QTILES - 6:
                            dve.wait_ge(s_pj, KTILES + VTILES + QTURNS * QTILES - 8)
                            dve.wait_ge(s_ids, 32)
                            dve.wait_ge(s_kl, PAGES // 2 + 4)
                        for c in range([0, 3, 6, 9, 12, 14][n - QTILES + 6], [3, 6, 9, 12, 14, 16][n - QTILES + 6]):
                            copy_page(0, c, page_number(dve, 0, c))

            with dve.Fori(0, QTURNS - 1) as i:
                dve_queries(i)
            dve_queries(QTURNS - 1)
            def cached_mask(b):
                dve.tensor_scalar(mask[:, 0:LC], G("iota"), b, NEG, ALU.is_ge, ALU.mult).then_inc(s_msk, 1)

            def col(tensor, n):
                return tensor[:, n:n + 1] if isinstance(n, int) else tensor[:, ds(n, 1)]

            def masked_max(n, b, j):
                slot = j % 4
                if j % 8 == 0:
                    after(dve, s_mx, n)
                    cached_mask(col(intf, 3 * B + b))
                    dve.wait_ge(s_msk, b + 2)
                dve.wait_ge(s_sc, n + 1)
                after(dve, s_tp, n - 3)
                dve.sem_inc(s_seen, 1)
                dve.tensor_tensor_reduce(out=prob[:, slot, :], in0=score(j), in1=mask[:, :], scale=1.0,
                                         scalar=-3e38, op0=ALU.add, op1=ALU.max,
                                         accum_out=mx[:, slot:slot + 1]).then_inc(s_mx, 1)

            def exponent_bias(n, j):
                slot = j % 4
                dve.wait_ge(s_mx, n + 1)
                dve.tensor_tensor(nb[:, slot:slot + 1], mx[:, slot:slot + 1], col(nrq, n), ALU.mult).then_inc(s_nb, 1)

            def inverse(n, j):
                dve.wait_ge(s_ex, n + 1)
                dve.reciprocal(ri[:, j % 4:j % 4 + 1], rs[:, j % 4:j % 4 + 1]).then_inc(s_rc, 1)

            dve.wait_ge(s_pkb, 16)
            dve.wait_ge(s_po, KTILES + QTURNS * QTILES)
            dve.memset(mask[:, LC:LK], 0.0).then_inc(s_msk, 1)
            masked_max(0, 0, 0)
            masked_max(1, 0, 1)
            dve.wait_ge(s_rms, 1)
            prep(dve.reciprocal(rq[:, :], rq[:, :]))
            prep(dve.tensor_scalar(nrq[:, :], rq[:, :], -SCALE, None, ALU.mult))
            dve.tensor_scalar(rq[:, :], rq[:, :], SCALE, None, ALU.mult)

            exponent_bias(0, 0)
            exponent_bias(1, 1)
            masked_max(2, 0, 2)
            exponent_bias(2, 2)
            inverse(0, 0)
            inverse(1, 1)

            def dve_turn(i):
                for j in range(16):
                    n = 16 * i + j
                    b, lo = (j + 3) // 8 + 1, 2 * ((j + 3) % 8)
                    copies = not (isinstance(i, int) and 2 * i + b >= B)
                    dve.wait_ge(s_tp, n + 1)
                    after(dve, s_pv, n - 1)
                    dve.tensor_copy(pT[:, j % 2, :], bank(4 + j % 2)).then_inc(s_pt, 1)
                    if copies:
                        page0 = page_number(dve, 2 * i + b, lo)
                    if not (isinstance(i, int) and n + 2 >= UNITS):
                        inverse(n + 2, j + 2)
                    if not (isinstance(i, int) and n + 3 >= UNITS):
                        masked_max(n + 3, 2 * i + (j + 3) // 8, j + 3)
                        if copies:
                            page1 = page_number(dve, 2 * i + b, lo + 1)
                        exponent_bias(n + 3, j + 3)
                    if copies:
                        copy_page(b % 2, lo, page0)
                        copy_page(b % 2, lo + 1, page1)
                    if isinstance(i, int) and n < 3:
                        for m in range(2 * n, 2 * n + 2):
                            copy_page(1, m, page_number(dve, 1, m))

            dve_turn(0)
            with dve.Fori(1, 15) as i:
                dve_turn(i)
            dve_turn(15)

            for g in range(HK):
                par = g % 2
                dve.wait_ge(s_woh, g + 1)
                dve.scalar_tensor_tensor(out=wo16[:, par, 1], in0=wolands[par], scalar=WSCALE, in1=wo16[:, par, 0],
                                         op0=ALU.mult, op1=ALU.subtract).then_inc(s_wol, 1)
                for h in range(2):
                    dve.wait_ge(s_oh, 2 * g + h + 1)
                    dve.tensor_tensor(head_major(o16[:, par, 1], h), landed(par, h), head_major(o16[:, par, 0], h),
                                      ALU.subtract).then_inc(s_ol, 1)
            dve.wait_ge(s_ost[0], 16 * B // 2)
            dve.wait_ge(s_ost[1], 16 * B // 2)
            for n in range(TILES + 1):
                if n < TILES:
                    dve.wait_ge(s_ht, n + 1)
                    prep(dve.bn_stats(bn[:, n, :], htok[:, n, :]))
                    dve.bn_aggr(mv[:, n, :], bn[:, n, :]).then_inc(s_bn, 1)
                if n >= 1:
                    m = n - 1
                    dve.wait_ge(s_htt, m + 1)
                    dve.tensor_copy(hT[:, :, P * m:P * m + P],
                                    bank(m).rearrange("p (k c) -> p k c", k=KC)).then_inc(s_hT, 1)
            dve.wait_ge(s_wvh, 2)
            dve.scalar_tensor_tensor(out=wvu16[2 * VB:3 * VB, :], in0=C("fwvu", VB), scalar=WSCALE, in1=wvu16[0:VB, :],
                                     op0=ALU.mult, op1=ALU.subtract).then_inc(s_wvl, 1)
            for m in range(2):
                for n in range(4 * m, 4 * m + 4):
                    q = P * (n % 4)
                    dve.wait_ge(s_rsp, m + 1)
                    dve.scalar_tensor_tensor(out=rsc[:, n, :], in0=bank(4 + m)[:, q:q + P], scalar=float(1 / np.sqrt(RDIM)),
                                             in1=C("flog"), op0=ALU.mult, op1=ALU.add).then_inc(s_rse, 1)
                for n in range(4 * m, 4 * m + 4):
                    dve.wait_ge(s_rse, 8 * m + n % 4 + 1)
                    dve.max(top8[:, n, :], rsc[:, n, :]).then_inc(s_top, 1)
                for n in range(4 * m, 4 * m + 4):
                    dve.wait_ge(s_top, n + 1)
                    dve.match_replace(out=rep8[:, n, :], in_to_replace=top8[:, n, :], in_values=rsc[:, n, :],
                                      imm_value=-3e38).then_inc(s_rse, 1)
                for n in range(4 * m, 4 * m + 4):
                    q = P * (n % 4)
                    dve.wait_ge(s_asp, m + 1)
                    dve.scalar_tensor_tensor(out=asc[:, n, :], in0=bank(m)[:, q:q + P], scalar=float(1 / np.sqrt(BOT)),
                                             in1=C("flog"), op0=ALU.mult, op1=ALU.add).then_inc(s_ase, 1)
            dve.wait_ge(s_rse, 2 * TILES)
            dve.wait_ge(s_ase, TILES)
            prep(dve.tensor_tensor(rep8[:, :, :], rsc[:, :, :], rep8[:, :, :], ALU.not_equal))
            prep(dve.tensor_tensor(asc[:, :, :], asc[:, :, :], rep8[:, :, :], ALU.mult))
            prep(dve.tensor_scalar(rep8[:, :, :], rep8[:, :, :], -NEG, NEG, ALU.mult, ALU.add))
            prep(dve.tensor_tensor(asc[:, :, :], asc[:, :, :], rep8[:, :, :], ALU.add))
            prep(dve.tensor_reduce(amx[:, :], asc[:, :, :], AXX, ALU.max))
            dve.tensor_scalar(amx[:, :], amx[:, :], -1.0, None, ALU.mult).then_inc(s_am, 1)
            dve.wait_ge(s_mean, 1)
            prep(dve.tensor_scalar(lsum[:, 1:2], bank(7)[:, 0:1], 1.0 / TOK, 1e-6, ALU.mult, ALU.add))
            prep(dve.reciprocal(lsum[:, 1:2], lsum[:, 1:2]))
            prep(dve.tensor_scalar(sm[:, 2, :], sm[:, 0, :], lsum[:, 1:2], 0.5, ALU.mult, ALU.mult))
            dve.wait_ge(s_sg, 1)
            prep(dve.scalar_tensor_tensor(out=sm[:, 3, :], in0=sm[:, 1, :], scalar=2.5, in1=sm[:, 2, :],
                                          op0=ALU.mult, op1=ALU.add))
            prep(dve.tensor_scalar(sm[:, 3, :], sm[:, 3, :], 0.0, 5.0, ALU.max, ALU.min))
            prep(dve.tensor_scalar(sm[:, 3, :], sm[:, 3, :], 0.5, 1.0 / 1.5, ALU.subtract, ALU.mult))
            dve.tensor_scalar(sm[:, 3, :], sm[:, 3, :], 0.0, 1.0, ALU.max, ALU.min).then_inc(s_ga, 1)
            dve.wait_ge(s_gb, 1)
            prep(dve.scalar_tensor_tensor(out=sm[:, 5, :], in0=sm[:, 4, :], scalar=0.05, in1=sm[:, 4, :],
                                          op0=ALU.is_ge, op1=ALU.mult))
            dve.wait_ge(s_exw, TILES)
            prep(dve.reciprocal(sm[:, 6, :], wsum[:, :]))
            prep(dve.tensor_tensor(sm[:, 7, :], sm[:, 6, :], sm[:, 5, :], ALU.mult))
            for n in range(TILES):
                dve.tensor_scalar(asc[:, n, :], asc[:, n, :], sm[:, 7, n:n + 1], None, ALU.mult).then_inc(s_w8, 1)
            for h in range(2):
                sl = slice(HALF * h, HALF * h + HALF)
                dve.wait_ge(s_axe, 2 * h + 2)
                dve.tensor_tensor(aux16[VB:2 * VB, sl], bank(h)[0:VB], aux16[0:VB, sl], ALU.subtract).then_inc(s_axl, 1)
            dve.wait_ge(s_fa, 1)
            for n in range(2 * KC):
                m, h = n // 2, n % 2
                sl = slice(HALF * h, HALF * h + HALF)
                dve.wait_ge(s_fo, n + 1)
                dve.scalar_tensor_tensor(out=hT[:, m, sl], in0=bank(4 + n % 4), scalar=1 / WSCALE, in1=x2T[:, m, sl],
                                         op0=ALU.mult, op1=ALU.add).then_inc(s_fin, 1)

        @block.tensor
        def _(pe):
            pe.wait_ge(s_masks, 1)
            pe.matmul(bank(7)[:, 0:B], lhsT=A("bsess", SESS), rhs=onehot[:, :], start=True, stop=True).then_inc(s_bias, 1)

            def encoder_out(n, p):
                pe.wait_ge(s_g1, n + 1)
                for k in range(KC):
                    pe.matmul(bank(2 + k)[:, 2 * S * p:2 * S * p + 2 * S], lhsT=hbuf[:, p % 2, P * k:P * k + P],
                              rhs=A("w2"), start=True, stop=True).then_inc(s_co, 1)

            def encoder_half(h):
                for p in range(8):
                    n = 8 * h + p
                    pe.wait_ge(s_wst, 3 * n + 3)
                    pe.wait_ge(s_xsp, 2 * n + 2)
                    if p >= 2:
                        pe.wait_ge(s_g1, n - 1)
                    pe.matmul(bank(p % 2), lhsT=whi[:, p % 2, :], rhs=xs16[:, ds(n, 1), :].rearrange("p a n -> p (a n)"),
                              start=True, stop=False)
                    pe.matmul(bank(p % 2), lhsT=wlo[:, p % 2, :], rhs=xs16[0:2 * S, ds(n, 1), :].rearrange("p a n -> p (a n)"),
                              start=False, stop=True).then_inc(s_h1, 1)
                    if p >= 1:
                        encoder_out(n - 1, p - 1)
                encoder_out(8 * h + 7, 7)
                pe.wait_ge(s_cT, 2 * KC * h + 2 * KC)
                for k in range(KC):
                    mm = pe.matmul(bank(6), lhsT=A("wdown")[:, DM * k:DM * k + DM], rhs=condT[:, k, ds(HALF * h, HALF)],
                                   start=(k == 0), stop=(k == KC - 1))
                mm.then_inc(s_dn, 1)

            with pe.Fori(0, 2) as h:
                encoder_half(h)

            pe.wait_ge(s_pkb, 16)
            with pe.Fori(0, 2) as i:
                pe.wait_ge(s_u, i + 1)
                for n, w in enumerate([A("bcw"), A("xw")[:, 0:P], A("xw")[:, P:DIN]]):
                    rows = w.shape[1]
                    for h in range(2):
                        pe.matmul(bank(2 * n + h)[0:rows], lhsT=w, rhs=u[:, HALF * h:HALF * h + HALF],
                                  start=True, stop=True).then_inc(s_pr, 1)
                    if n == 0:
                        for m in range(TILES):
                            mm = pe.matmul(bank(6)[:, 8 * m:8 * m + 8], lhsT=u[:, P * m:P * m + P], rhs=A("dtw"),
                                           start=True, stop=True)
                        mm.then_inc(s_dtp, 1)
                for n in range(4):
                    pe.wait_ge(s_xp, 6 * i + n + 3)
                    c, h = n // 2, n % 2
                    pe.matmul(bank(2 + n), lhsT=A("zw")[:, P * c:P * c + P], rhs=u[:, HALF * h:HALF * h + HALF],
                              start=True, stop=True).then_inc(s_zp, 1)
                pe.wait_ge(s_R, 2 * i + 2)
                pe.wait_ge(s_xp, 6 * i + 2)
                for h in range(2):
                    for d, side in enumerate(("ufw", "ubw")):
                        mm = pe.matmul(bank(h), lhsT=A(side), rhs=Rm[:, d, 16 * h:16 * h + 16, :].rearrange("p a s -> p (a s)"),
                                       start=(d == 0), stop=(d == 1))
                    mm.then_inc(s_seg, 1)
                pe.wait_ge(s_xs, 4 * i + 2)
                pe.wait_ge(s_nv, i + 1)
                pe.wait_ge(s_zs, 4 * i + 4)
                for d in range(2):
                    for m in range(TILES):
                        mm = pe.matmul(bank((6, 4)[d] + m // 4)[:, P * (m % 4):P * (m % 4) + P], lhsT=Bt[:, P * m:P * m + P],
                                       rhs=Ct[:, P * m + 2 * d:P * m + 2 * d + P], start=True, stop=True)
                        if m % 4 == 3:
                            mm.then_inc(s_GG, 1)
                for n in range(4):
                    c, h = n // 2, n % 2
                    pe.wait_ge(s_xs, 4 * i + c + 3)
                    if n >= 2:
                        pe.wait_ge(s_xe, 4 * i + n - 1)
                    for m in range(4):
                        mm = pe.transpose(bank(2 + h)[:, P * m:P * m + P], xs[:, c, HALF * h + P * m:HALF * h + P * m + P],
                                          G("ident"))
                    mm.then_inc(s_xt, 1)
                pe.wait_ge(s_W, 16 * i + 16)
                for n in range(4):
                    c, h = n // 2, n % 2
                    for k in range(2):
                        mm = pe.matmul(bank(4 + n), lhsT=A("fcd")[:, DIN * k + P * c:DIN * k + P * c + P],
                                       rhs=xs[:, k, HALF * h:HALF * h + HALF], start=(k == 0), stop=(k == 1))
                    mm.then_inc(s_r, 1)
                pe.wait_ge(s_M, 4 * i + 4)
                pe.wait_ge(s_xe, 4 * i + 4)
                for n in range(4):
                    c, h = n // 2, n % 2
                    for m in range(4):
                        for q in range(2):
                            tile, head = 4 * h + m, 2 * c + q
                            mm = pe.matmul(bank(n)[64 * q:64 * q + 64, P * m:P * m + P],
                                           lhsT=xtok[:, tile, 64 * head:64 * head + 64], rhs=M[:, NH * tile + head, :],
                                           start=True, stop=True)
                    mm.then_inc(s_y, 1)
                pe.wait_ge(s_ysq, 2 * i + 2)
                pe.wait_ge(s_t, 4 * i + 4)
                for h in range(2):
                    for c in range(2):
                        mm = pe.matmul(bank(4 + h), lhsT=ones[:, :], rhs=cacc[:, c, HALF * h:HALF * h + HALF],
                                       start=(c == 0), stop=(c == 1))
                    mm.then_inc(s_ss0, 1)
                for h in range(2):
                    for c in range(2):
                        mm = pe.matmul(bank(6 + h), lhsT=outw[:, c, :], rhs=yb[:, c, HALF * h:HALF * h + HALF],
                                       start=(c == 0), stop=(c == 1))
                    mm.then_inc(s_hy, 1)
            pe.wait_ge(s_hf, 1)
            for n in range(2 * KC):
                h, k = n // KC, n % KC
                pe.matmul(bank(n), lhsT=A("wup")[:, P * k:P * k + P],
                          rhs=u[:, :].rearrange("p (s b) -> p b s", b=B)[:, 16 * h:16 * h + 16, :],
                          start=True, stop=True).then_inc(s_up, 1)

            def project(out, operands):
                for k in range(KC):
                    for a, b in ((0, 0), (0, 1), (1, 0)):
                        lhsT, rhs = operands(k, a, b)
                        mm = pe.matmul(out, lhsT=lhsT, rhs=rhs, start=(k == 0 and a + b == 0), stop=(k == KC - 1 and a == 1))
                mm.then_inc(s_pj, 1)

            def next_weights(n):
                pe.wait_ge(s_wh, n + 1)
                pe.wait_ge(s_wl, n + 1)

            def key_squares(n):
                pe.wait_ge(s_sq, n + 1)
                if n >= 2:
                    pe.wait_ge(s_kr1, n - 1)
                for c in range(4):
                    mm = pe.matmul(bank(6 + n % 2)[:, c:c + 1], lhsT=ksq[n % 2][:, P * c:P * c + P], rhs=mean_d[:, :],
                                   start=True, stop=True)
                mm.then_inc(s_ss, 1)

            def spread_key_scale(n):
                pe.wait_ge(s_kr2, n + 1)
                if n >= 2:
                    pe.wait_ge(s_po, n - 1)
                pe.matmul(bank(4 + n % 2), lhsT=ones[:, :], rhs=diag[n % 2].rearrange("p a c -> p (a c)"),
                          start=True, stop=True).then_inc(s_kb, 1)

            for n in range(KTILES):
                h, c = n // 4 % 2, P * (n % 4)
                if n % WTILES == 0:
                    next_weights(n // WTILES)
                if n in (0, 4):
                    pe.wait_ge(s_xl, n + KC)
                if n >= 4:
                    pe.wait_ge(s_sq, n - 3)
                    pe.wait_ge(s_ab, n - 3)
                project(bank(n % 4), lambda k, a, b: (w16[:, n // WTILES, a, k, c:c + P],
                                                      x16[:, b, k, HALF * h:HALF * h + HALF]))
                if n >= 1:
                    key_squares(n - 1)
                if n >= 2:
                    spread_key_scale(n - 2)
            key_squares(KTILES - 1)
            spread_key_scale(KTILES - 2)
            spread_key_scale(KTILES - 1)
            for n in range(VTILES):
                m = n % TILES
                if n % WTILES == 0:
                    next_weights(2 + n // WTILES)
                if n < 4:
                    pe.wait_ge(s_sq, KTILES - 3 + n)
                    pe.wait_ge(s_ab, KTILES - 3 + n)
                else:
                    pe.wait_ge(s_ve, n - 3)
                project(bank(n % 4), lambda k, a, b: (x16[:, a, k, P * m:P * m + P], w16[:, n // WTILES, b, k, :]))
            pe.wait_ge(s_ve, VTILES)
            pe.wait_ge(s_kr1, KTILES)

            def query_squares(i, m, part):
                h = m % 2
                if part == 0:
                    pe.wait_ge(s_sq, KTILES + QTILES * i + 4 * m + 4)
                for b in range(4 * part, 4 * part + 4):
                    c = 2 * i + (HK * (16 * h + b) + m // 2)
                    mm = pe.matmul(bank(7)[:, c:c + 1] if isinstance(i, int) else bank(7)[:, ds(c, 1)],
                                   lhsT=sqr[h][:, b].rearrange("p r s -> p (r s)"), rhs=mean_d[:, :], start=True, stop=True)
                if part == 3:
                    mm.then_inc(s_ss, 1)

            def pe_queries(i):
                for n in range(QTILES):
                    sl, m = n // WTILES, n // 4
                    h, c = m % 2, P * (n % 4)
                    if n % WTILES == 0:
                        next_weights(4 + 2 * i + sl)
                    pe.wait_ge(s_sq, KTILES + QTILES * i + n - 3)
                    pe.wait_ge(s_ab, KTILES + QTILES * i + n - 3)
                    project(bank(n % 4), lambda k, a, b: (w16[:, sl, a, k, c:c + P], x16[:, b, k, HALF * h:HALF * h + HALF]))
                    if m > 0:
                        query_squares(i, m - 1, n % 4)
                    elif not isinstance(i, int) or i > 0:
                        query_squares(i - 1, 3, n % 4)

            pe_queries(0)
            with pe.Fori(1, QTURNS - 1) as i:
                pe_queries(i)
            pe_queries(QTURNS - 1)
            for part in range(4):
                query_squares(QTURNS - 1, 3, part)

            def scores(n, b, j):
                par, g = j // 8 % 2, j % 8
                turn = b // 2 if isinstance(b, int) else None
                if isinstance(b, int) and b == 0 and g == HK - 2:
                    pe.wait_ge(s_ql, 3)
                if g == 0:
                    first = isinstance(b, int) and b == 0
                    pe.wait_ge(s_ql, 2 if first else 3 * b + 3)
                    pe.wait_ge(s_kc, NPP * b + NPP)
                after(pe, s_mx, n - 1)
                s = score(j)
                for m, (a, l) in enumerate(((0, 0), (0, 1), (1, 0))):
                    q = q16[:, par, a, P * g:P * g + P]
                    pe.matmul(s[:, 0:LC].rearrange("p (a c) -> p a c", c=S), lhsT=q,
                              rhs=kring16[:, par, 0:NPP, l, S * g:S * g + S], start=m == 0, stop=m == 2)
                    mm = pe.matmul(s[:, LC:LK], lhsT=q, rhs=kring16[:, par, NPP, l, S * g:S * g + S], start=m == 0, stop=m == 2)
                mm.then_inc(s_sc, 1)

            def transposes(n, j):
                slot = j % 4
                pe.wait_ge(s_pn, n + 1)
                after(pe, s_pt, n - 1)
                after(pe, s_ov, n - 2)
                pe.transpose(bank(6 + (j + 1) % 2)[0:S, P:2 * P], prob[:, slot, LC:LK], G("ident")).then_inc(s_t4, 1)
                for c in range(BPT):
                    mm = pe.transpose(bank(4 + j % 2)[:, P * c:P * c + P], prob[:, slot, P * c:P * c + P], G("ident"))
                mm.then_inc(s_tp, 1)

            def weighted(n, b, j, last=False):
                par, g = j // 8 % 2, j % 8
                if g == 0:
                    per = 16 * (NPP + 1)
                    pe.wait_ge(s_v[par], per * (b // 2) + per if isinstance(b, int) else (per // 2) * b + per - (per // 2) * par)
                pe.wait_ge(s_pt, n + 1)
                pe.wait_ge(s_p4, n + 2 if not last else n + 1)
                o = bank(6 + j % 2)[:, 0:P]
                for c in range(BPT):
                    pe.matmul(o, lhsT=vring[:, par, c, D * g:D * g + D], rhs=pT[:, j % 2, P * c:P * c + P],
                              start=(c == 0), stop=False)
                pe.matmul(o, lhsT=vring[0:S, par, BPT, D * g:D * g + D], rhs=pT4[:, j % 2, :],
                          start=False, stop=True).then_inc(s_pv, 1)

            for n in range(3):
                scores(n, 0, n)

            def pe_turn(i):
                for j in range(16):
                    n = 16 * i + j
                    first = isinstance(i, int) and n == 0
                    transposes(n, j)
                    if not (isinstance(i, int) and n + 3 >= UNITS):
                        scores(n + 3, 2 * i + (j + 3) // 8, j + 3)
                    if not first:
                        jj = (j - 1) % 16
                        weighted(n - 1, 2 * i + jj // 8 if j > 0 else 2 * i - 1, jj)

            pe_turn(0)
            with pe.Fori(1, 15) as i:
                pe_turn(i)
            pe_turn(15)
            weighted(UNITS - 1, B - 1, 15, last=True)

            pe.wait_ge(s_ov, UNITS)
            pe.wait_ge(s_pt, UNITS)

            def turn_tokens(n):
                pe.wait_ge(s_ht, n + 1)
                for k in range(KC):
                    mm = pe.transpose(bank(n)[:, P * k:P * k + P], htok[:, n, P * k:P * k + P], G("ident"))
                mm.then_inc(s_htt, 1)

            def output_heads(i):
                first, last = [isinstance(i, int) and i == n for n in (0, HK // 2 - 1)]
                for par in range(2):
                    g = 2 * i + par
                    pe.wait_ge(s_woh, g + 1)
                    pe.wait_ge(s_wol, g + 1)
                    for m in range(TILES):
                        if m % 4 == 0:
                            pe.wait_ge(s_oh, 2 * g + m // 4 + 1)
                            pe.wait_ge(s_ol, 2 * g + m // 4 + 1)
                        for r in range(REP):
                            for n, (a, b) in enumerate(((0, 0), (0, 1), (1, 0))):
                                mm = pe.matmul(bank(m), lhsT=o16[:, par, a, r, P * m:P * m + P], rhs=wo16[:, par, b, r, :],
                                               start=first and par + r + n == 0, stop=last and par == 1 and r == REP - 1 and n == 2)
                        if last and par == 1:
                            mm.then_inc(s_hp, 1)
                            if m >= 1:
                                turn_tokens(m - 1)
                    if not (last and par == 1):
                        mm.then_inc(s_hg, 1)

            output_heads(0)
            with pe.Fori(1, HK // 2 - 1) as i:
                output_heads(i)
            output_heads(HK // 2 - 1)
            turn_tokens(TILES - 1)
            pe.wait_ge(s_pkc, 16)
            pe.wait_ge(s_hT, TILES)
            pe.matmul(bank(4)[0:RDIM, 0:NSLOT], lhsT=C("fwr", BOT), rhs=C("fkeys", BOT), start=True, stop=True).then_inc(s_fp, 1)
            for k in range(KC):
                mm = pe.matmul(bank(5)[:, 0:VB], lhsT=C("fval")[:, NSLOT * k:NSLOT * k + NSLOT], rhs=C("fwvd")[:, VB * k:VB * k + VB],
                               start=(k == 0), stop=(k == KC - 1))
            mm.then_inc(s_fp, 1)
            for h in range(2):
                for k in range(KC):
                    mm = pe.matmul(bank(h)[0:BOT], lhsT=C("fwq")[:, BOT * k:BOT * k + BOT], rhs=hT[:, k, HALF * h:HALF * h + HALF],
                                   start=(k == 0), stop=(k == KC - 1))
                mm.then_inc(s_fp, 1)
            for m in range(2):
                pe.wait_ge(s_fe, 3 + m)
                pe.matmul(bank(2 + m)[0:RDIM], lhsT=C("fwr", BOT), rhs=queryT[:, HALF * m:HALF * m + HALF],
                          start=True, stop=True).then_inc(s_fp, 1)
            for m in range(2):
                pe.wait_ge(s_fe, 5 + m)
                for n in range(4):
                    tile = 4 * m + n
                    mm = pe.matmul(bank(4 + m)[:, P * n:P * n + P], lhsT=rqT[:, P * tile:P * tile + P], rhs=rkT[:, :],
                                   start=True, stop=True)
                mm.then_inc(s_rsp, 1)
                for n in range(4):
                    tile = 4 * m + n
                    mm = pe.matmul(bank(m)[:, P * n:P * n + P], lhsT=queryT[:, P * tile:P * tile + P], rhs=C("fkeys", BOT),
                                   start=True, stop=True)
                mm.then_inc(s_asp, 1)
            for h in range(2):
                for k in range(KC):
                    mm = pe.matmul(bank(6 + h), lhsT=C("fwu1")[:, P * k:P * k + P], rhs=hT[:, k, HALF * h:HALF * h + HALF],
                                   start=(k == 0), stop=(k == KC - 1))
                mm.then_inc(s_fp, 1)
            pe.wait_ge(s_fe, 8)
            for n in range(TILES):
                mm = pe.matmul(bank(6)[:, n:n + 1], lhsT=uT[:, P * n:P * n + P], rhs=C("fwu2"), start=True, stop=True)
            mm.then_inc(s_ler, 1)
            pe.wait_ge(s_lv, 1)
            pe.matmul(bank(7)[:, 0:1], lhsT=ones[:, :], rhs=lsum[:, 0:1], start=True, stop=True).then_inc(s_mean, 1)
            for m in range(2):
                for n in range(4):
                    tile = 4 * m + n
                    pe.wait_ge(s_w8, tile + 1)
                    mm = pe.transpose(bank(2 + m)[:, P * n:P * n + P], asc[:, tile, :], G("ident"))
                mm.then_inc(s_wt, 1)
            for h in range(2):
                pe.wait_ge(s_wte, h + 1)
                pe.matmul(bank(h)[0:VB], lhsT=AV[:, :], rhs=wTs[:, HALF * h:HALF * h + HALF], start=True, stop=True).then_inc(s_ax, 1)
            pe.wait_ge(s_wvl, 1)
            pe.wait_ge(s_axl, 2)
            pe.wait_ge(s_ga, 1)
            for n in range(2 * KC):
                m, h = n // 2, n % 2
                if n >= 4:
                    pe.wait_ge(s_fin, n - 3)
                pe.matmul(bank(4 + n % 4), lhsT=wvu16[:, P * m:P * m + P], rhs=aux16[:, HALF * h:HALF * h + HALF],
                          start=True, stop=True).then_inc(s_fo, 1)


def kernel(x, itok_B_0_7, itok_B_2182_4065, itok_Bx16_0_63, itok_B_207_1644, _lenS, L0_cond_W_sess, L0_cond_b_sess,
           L0_cond_W2, L0_cond_b2, L0_attn_w_down, L0_attn_b_down, L0_attn_w_up, L0_attn_b_up, L0_attn_gate1,
           L0_attn_hy_in_w, L0_attn_hy_conv_w, L0_attn_hy_conv_b, L0_attn_hy_dt_bias, L0_attn_hy_A_log, L0_attn_hy_D,
           L0_attn_hy_fcD_w, L0_attn_hy_norm_w, L0_attn_hy_out_w, L0_cond2_Wq, L0_cond2_Wk, L0_cond2_Wv, L0_cond2_Wo,
           L0_cond2_q_norm_w, L0_cond2_k_norm_w, L0_cond2_k_cache, L0_cond2_v_cache, L0_ffn_Wq, L0_ffn_Wr,
           L0_ffn_aux_keys, L0_ffn_aux_values, L0_ffn_Wvd, L0_ffn_Wvu, L0_ffn_Wu1, L0_ffn_bu1, L0_ffn_Wu2, L0_ffn_bu2,
           L0_ffn_gate_w1, L0_ffn_gate_bias, L0_ffn_log_rel):
    import concourse.bacc as bacc
    from concourse.bass_utils import run_bass_kernel_spmd

    f = np.float32

    def rows(a):
        a = np.asarray(a)
        return a.reshape(-1, P, a.shape[1]).transpose(1, 0, 2).reshape(P, -1)

    def every(a):
        a = np.asarray(a).reshape(1, -1)
        return np.broadcast_to(a, (P, a.shape[1]))

    def pack(cols, total, parts):
        out = np.zeros((P, total), f)
        for name, (at, n) in cols.items():
            a = np.asarray(parts[name])
            assert a.shape[1] == n, (name, a.shape, n)
            out[:a.shape[0], at:at + n] = a
        return out

    p = np.arange(P)
    conv = np.asarray(L0_attn_hy_conv_w)[:, 0, :]
    cb = np.asarray(L0_attn_hy_conv_b).reshape(-1, 1)
    inw = np.asarray(L0_attn_hy_in_w).T
    o = DIN

    def spread(a):
        out = np.zeros((3 * DST, a.shape[1]), f)
        out[0:DST], out[2 * DST:] = a[0:DST], a[DST:]
        return out

    same = p[:, None] // S == p[None, :] // S
    w2 = np.zeros((P, 2 * S), f)
    w2[0:CHID, 0:S] = w2[CHID:, S:] = np.asarray(L0_cond_W2)
    parts_a = {
        "sessidx": p[:, None], "chan": (p % S)[:, None], "tcol": p[:, None] + P * np.arange(KC)[None, :],
        "bsess": np.concatenate([np.asarray(L0_cond_b_sess)] * 2, 1), "w2": w2, "b2": every(L0_cond_b2),
        "wdown": rows(np.asarray(L0_attn_w_down).T), "bdown": np.asarray(L0_attn_b_down)[:, None],
        "srow": every(np.arange(S)),
        "invf": np.tile(1.0 / THETA ** (np.arange(0, D, 2, dtype=f) / D), 2)[:, None],
        "sign": np.where(p < 64, 1 / WSCALE, -1 / WSCALE)[:, None],
        "qnw": np.asarray(L0_cond2_q_norm_w)[:, None], "knw": np.asarray(L0_cond2_k_norm_w)[:, None],
        "zw": inw[:, 0:o], "xw": inw[:, o:2 * o], "bcw": spread(inw[:, 2 * o:2 * o + 2 * DST].T).T,
        "dtw": inw[:, 2 * o + 2 * DST:], "convx": rows(conv[0:o]), "convbc": spread(conv[o:]),
        "convbx": rows(cb[0:o]), "convbbc": spread(cb[o:]),
        "dtb": every(np.concatenate([np.asarray(L0_attn_hy_dt_bias)] * 2)), "alog": every(L0_attn_hy_A_log),
        "dskip": rows(np.repeat(np.asarray(L0_attn_hy_D), 64)[:, None]),
        "fcd": rows(np.repeat(np.asarray(L0_attn_hy_fcD_w), 64, axis=0).T),
        "normw": rows(np.asarray(L0_attn_hy_norm_w)[:, None]), "outw": rows(np.asarray(L0_attn_hy_out_w).T),
        "wup": np.asarray(L0_attn_w_up).T, "bup": rows(np.asarray(L0_attn_b_up)[:, None]),
        "gate1": every(L0_attn_gate1),
        "ufw": same & (p[:, None] > p[None, :]), "ubw": same & (p[:, None] < p[None, :]),
        "before": (p % S)[:, None] < np.arange(S)[None, :], "after": (p % S)[:, None] > np.arange(S)[None, :],
    }
    parts_b = {
        "ident": np.eye(P), "iota": every(np.arange(LC)),
    }
    parts_c = {
        "fwq": rows(np.asarray(L0_ffn_Wq).T), "fwr": np.asarray(L0_ffn_Wr).T, "fkeys": np.asarray(L0_ffn_aux_keys).T,
        "flog": every(L0_ffn_log_rel), "fval": rows(np.asarray(L0_ffn_aux_values).T), "fwvd": rows(np.asarray(L0_ffn_Wvd).T),
        "fwvu": np.asarray(L0_ffn_Wvu).T, "fwu1": rows(np.asarray(L0_ffn_Wu1).T), "fbu1": np.asarray(L0_ffn_bu1)[:, None],
        "fwu2": np.asarray(L0_ffn_Wu2).T, "fbu2": every(L0_ffn_bu2), "fgw": every(L0_ffn_gate_w1),
        "fgb": every(L0_ffn_gate_bias),
    }
    xf = np.asarray(x)
    ints = np.concatenate([np.asarray(a) for a in (itok_B_0_7, _lenS, itok_B_2182_4065, itok_B_207_1644)])
    ins = {
        "x": xf, "xT": xf.reshape(TOK, HID).T, "ints": np.broadcast_to(ints[None, :], (P, INTS)),
        "table": np.asarray(itok_Bx16_0_63).reshape(1, -1), "wsess": np.asarray(L0_cond_W_sess),
        "packa": pack(COL_A, COLS_A, parts_a), "packb": pack(COL_B, COLS_B, parts_b),
        "packc": pack(COL_C, COLS_C, parts_c),
        "wqT": np.asarray(L0_cond2_Wq).T, "wkT": np.asarray(L0_cond2_Wk).T, "wvT": np.asarray(L0_cond2_Wv).T,
        "woT": np.asarray(L0_cond2_Wo).T, "kcT": np.asarray(L0_cond2_k_cache).transpose(3, 0, 2, 1),
        "vc": np.asarray(L0_cond2_v_cache),
    }
    ins = {k: np.ascontiguousarray(v) for k, v in ins.items()}
    nc = bacc.Bacc("TRN2", target_bir_lowering=False, num_devices=1)
    t = {k: nc.dram_tensor(f"in_{k}", v.shape, mybir.dt.from_np(v.dtype), kind="ExternalInput").ap() for k, v in ins.items()}
    for k, shape in (("q_s", (B, D, HQ * S)), ("k_s", (B, D, HK * S)), ("v_s", (TOK, HK * D)), ("o_s", (B, D, HQ * S))):
        t[k] = nc.dram_tensor(k, shape, F32, kind="Internal").ap()
    t["out"] = nc.dram_tensor("out", (HID, TOK), F32, kind="ExternalOutput").ap()
    encoder_attention_memory(nc, t)
    r = run_bass_kernel_spmd(nc, [{f"in_{k}": v for k, v in ins.items()}], core_ids=[0])
    return np.ascontiguousarray(r.results[0]["out"].T).reshape(B, S, HID)
```
